# Optimizing a Trainium2 kernel written in Bass

```python
import numpy as np
import jax
import jax.numpy as jnp

def _softmax(x, axis=-1):
    return jax.nn.softmax(x, axis=axis)
def _gelu(x):
    return jax.nn.gelu(x, approximate=True)
def _silu(x):
    return jax.nn.silu(x)
def _sigmoid(x):
    return jax.nn.sigmoid(x)
def _layernorm(x, axis=-1, eps=1e-5):
    m = jnp.mean(x, axis=axis, keepdims=True)
    v = jnp.var(x, axis=axis, keepdims=True)
    return (x - m) / jnp.sqrt(v + eps)
def _scatter_add(tgt, idx, src, axis=0):
    return tgt.at[idx].add(src)
def _segment_sum(src, seg, n):
    return jax.ops.segment_sum(src, seg, n)

kernel_name = 'mk_adj_ffn_d2_adj_256_031f82'

def setup_inputs(seed: int = 0):
    np.random.seed(seed)
    _w = jnp.asarray
    def _rec_inputs():
        import jax
        import jax.numpy as jnp
        _gk = jax.random.key(seed)
        x = -0.0005207 + 1.001 * jax.random.normal(jax.random.fold_in(_gk, 1), (32, 512, 256), jnp.float32)
        _w = (1.0 + jnp.arange(512, dtype=jnp.float32)) ** -0.5
        _w = _w / _w.mean()
        _pij = jnp.clip(0.03125 * _w[:, None] * _w[None, :], 0.0, 1.0)
        _a = jax.random.uniform(jax.random.fold_in(_gk, 2), (32, 512, 512)) < _pij
        adj = _a.astype(jnp.int32)
        return x, adj
    x, adj = _rec_inputs()
    def _L0_gnn_setup():
        import jax, jax.numpy as jnp
        import numpy as np
        B, N, D = (8, 1024, 256)
        H, HO = (4, 64)
        T = 5
        NEG = -1000000000.0
        EPS = 1e-06
        key = jax.random.key(seed)
        ks = jax.random.split(key, 6)
        nodes_embed = jax.random.normal(ks[0], (B, N, D), dtype=jnp.float32)
        node_adj = jax.random.randint(ks[1], (B, N, N), 0, T + 1)
        W = jax.random.normal(ks[2], (H, D, HO), dtype=jnp.float32) * (1.0 / np.sqrt(D))
        a_src = jax.random.normal(ks[3], (H, T, HO), dtype=jnp.float32) * 0.1
        a_dst = jax.random.normal(ks[4], (H, T, HO), dtype=jnp.float32) * 0.1
        bias = jnp.zeros((H, HO), dtype=jnp.float32)
        ln_gamma = jnp.ones((H, HO), dtype=jnp.float32)
        ln_beta = jnp.zeros((H, HO), dtype=jnp.float32)
        return {'nodes_embed': nodes_embed, 'node_adj': node_adj, 'W': W, 'a_src': a_src, 'a_dst': a_dst, 'bias': bias, 'ln_gamma': ln_gamma, 'ln_beta': ln_beta}
    _L0_gnn_all = _L0_gnn_setup()
    _L0_gnn_in = {k: v for k, v in _L0_gnn_all.items() if k in ('W', 'a_src', 'a_dst', 'bias', 'ln_gamma', 'ln_beta', )}
    del _L0_gnn_all

    def _L0_ffn_setup():
        import jax, jax.numpy as jnp
        import numpy as np
        D_MODEL = 256
        D_STATE = 64
        D_CONV = 4
        EXPAND = 2
        HEADDIM = 64
        D_INNER = EXPAND * D_MODEL
        NHEADS = D_INNER // HEADDIM
        CONV_DIM = D_INNER + 2 * D_STATE
        D_IN_PROJ = 2 * D_INNER + 2 * D_STATE + NHEADS
        CHUNK = 256
        EPS = 1e-05

        def segsum(a):
            T = a.shape[-1]
            cs = jnp.cumsum(a, axis=-1)
            ss = cs[..., :, None] - cs[..., None, :]
            mask = jnp.tril(jnp.ones((T, T), dtype=bool))
            return jnp.where(mask, ss, -jnp.inf)

        def mamba2_block(x, W_in, conv_w, conv_b, dt_bias, A_log, D, norm_w, W_out, W_lin, b_lin):
            Bsz, L, _ = x.shape
            zxbcdt = x @ W_in
            z, xBC, dt = jnp.split(zxbcdt, [D_INNER, D_INNER + CONV_DIM], axis=-1)
            xp = jnp.pad(xBC, ((0, 0), (D_CONV - 1, 0), (0, 0)))
            conv = conv_b + sum((xp[:, k:k + L, :] * conv_w[:, k] for k in range(D_CONV)))
            xBC = jax.nn.silu(conv)
            xh, Bmat, Cmat = jnp.split(xBC, [D_INNER, D_INNER + D_STATE], axis=-1)
            dt = jax.nn.softplus(dt + dt_bias)
            A = -jnp.exp(A_log)
            nc = L // CHUNK
            xh = xh.reshape(Bsz, nc, CHUNK, NHEADS, HEADDIM)
            Bc = Bmat.reshape(Bsz, nc, CHUNK, D_STATE)
            Cc = Cmat.reshape(Bsz, nc, CHUNK, D_STATE)
            dtc = dt.reshape(Bsz, nc, CHUNK, NHEADS)
            dA = jnp.einsum('bclh,h->bhcl', dtc, A)
            A_cum = jnp.cumsum(dA, axis=-1)
            Lmat = jnp.exp(segsum(dA))
            xdt = xh * dtc[..., None]
            Y_diag = jnp.einsum('bcln,bcsn,bhcls,bcshp->bclhp', Cc, Bc, Lmat, xdt)
            decay_states = jnp.exp(A_cum[..., -1:] - A_cum)
            states = jnp.einsum('bcln,bhcl,bclhp->bchpn', Bc, decay_states, xdt)
            chunk_decay = jnp.exp(A_cum[..., -1])

            def step(h, inp):
                s, d = inp
                return (h * d[..., None, None] + s, h)
            _, prevs = jax.lax.scan(step, jnp.zeros_like(states[:, 0]), (jnp.moveaxis(states, 1, 0), jnp.moveaxis(chunk_decay, 2, 0)))
            prevs = jnp.moveaxis(prevs, 0, 1)
            Y_off = jnp.einsum('bcln,bchpn,bhcl->bclhp', Cc, prevs, jnp.exp(A_cum))
            Y = (Y_diag + Y_off + xh * D[:, None]).reshape(Bsz, L, D_INNER)
            Y = Y * jax.nn.silu(z)
            Y = Y * jax.lax.rsqrt(jnp.mean(Y * Y, axis=-1, keepdims=True) + EPS) * norm_w
            out = Y @ W_out
            return out @ W_lin + b_lin
        key = jax.random.key(seed)
        ks = jax.random.split(key, 12)
        B, L = (8, 4096)

        def gauss(k, shape, scale):
            return jax.random.normal(k, shape, dtype=jnp.float32) * scale
        return {'x': gauss(ks[0], (B, L, D_MODEL), 1.0), 'W_in': gauss(ks[1], (D_MODEL, D_IN_PROJ), D_MODEL ** (-0.5)), 'conv_w': gauss(ks[2], (CONV_DIM, D_CONV), 0.3), 'conv_b': gauss(ks[3], (CONV_DIM,), 0.1), 'dt_bias': jax.random.uniform(ks[4], (NHEADS,), minval=-4.0, maxval=-1.0), 'A_log': jnp.log(jax.random.uniform(ks[5], (NHEADS,), minval=1.0, maxval=16.0)), 'D': jnp.ones((NHEADS,), jnp.float32), 'norm_w': jnp.ones((D_INNER,), jnp.float32), 'W_out': gauss(ks[6], (D_INNER, D_MODEL), D_INNER ** (-0.5)), 'W_lin': gauss(ks[7], (D_MODEL, D_MODEL), D_MODEL ** (-0.5)), 'b_lin': jnp.zeros((D_MODEL,), jnp.float32)}
    _L0_ffn_all = _L0_ffn_setup()
    _L0_ffn_in = {k: v for k, v in _L0_ffn_all.items() if k in ('W_in', 'conv_w', 'conv_b', 'dt_bias', 'A_log', 'D', 'norm_w', 'W_out', 'W_lin', 'b_lin', )}
    del _L0_ffn_all

    def _L1_gnn_setup():
        import jax, jax.numpy as jnp
        import numpy as np
        NEG_INF = -1000000000.0
        LEAKY_ALPHA = 0.2
        key = jax.random.key(seed)
        k1, k2, k3, k4 = jax.random.split(key, 4)
        B, N, Din, Dout = (16, 2048, 256, 256)
        h = jax.random.normal(k1, (B, N, Din), dtype=jnp.float32)
        adj = jax.random.randint(k2, (B, N, N), 0, 2, dtype=jnp.int32)
        W = jax.random.normal(k3, (Din, Dout), dtype=jnp.float32) * (1.0 / np.sqrt(Din))
        a = jax.random.normal(k4, (2 * Dout,), dtype=jnp.float32) * (1.0 / np.sqrt(2 * Dout))
        return {'h': h, 'adj': adj, 'W': W, 'a': a}
    _L1_gnn_all = _L1_gnn_setup()
    _L1_gnn_in = {k: v for k, v in _L1_gnn_all.items() if k in ('W', 'a', )}
    del _L1_gnn_all

    def _L1_ffn_setup():
        import jax, jax.numpy as jnp
        import numpy as np
        B, T, D, H, L = (16, 4096, 256, 256, 2)

        def _lstm(x, W_ih, W_hh, b_ih, b_hh):
            x_proj = jnp.einsum('btd,gd->btg', x, W_ih) + b_ih + b_hh
            h0 = jnp.zeros((x.shape[0], W_hh.shape[1]), x.dtype)
            c0 = jnp.zeros_like(h0)

            def step(carry, xp):
                h, c = carry
                gates = xp + h @ W_hh.T
                i, f, g, o = jnp.split(gates, 4, axis=-1)
                c = jax.nn.sigmoid(f) * c + jax.nn.sigmoid(i) * jnp.tanh(g)
                h = jax.nn.sigmoid(o) * jnp.tanh(c)
                return ((h, c), h)
            _, hs = jax.lax.scan(step, (h0, c0), jnp.swapaxes(x_proj, 0, 1))
            return jnp.swapaxes(hs, 0, 1)
        key = jax.random.key(seed)
        ks = jax.random.split(key, 9)
        s = 1.0 / np.sqrt(H)
        u = lambda k, shape: jax.random.uniform(k, shape, jnp.float32, -s, s)
        return {'x': jax.random.normal(ks[0], (B, T, D), jnp.float32), 'W_ih': u(ks[1], (4 * H, D)), 'W_hh': u(ks[2], (4 * H, H)), 'b_ih': u(ks[3], (4 * H,)), 'b_hh': u(ks[4], (4 * H,)), 'W_lin': u(ks[5], (L, H)), 'b_lin': u(ks[6], (L,)), 'fw_att': jnp.full((1, H), 0.001, jnp.float32), 'bw_att': jnp.full((1, H), 0.001, jnp.float32)}
    _L1_ffn_all = _L1_ffn_setup()
    _L1_ffn_in = {k: v for k, v in _L1_ffn_all.items() if k in ('W_ih', 'W_hh', 'b_ih', 'b_hh', 'W_lin', 'b_lin', 'fw_att', 'bw_att', )}
    del _L1_ffn_all

    return {
        "x": x,
        "adj": adj,
        "L0_gnn_W": _L0_gnn_in["W"],
        "L0_gnn_a_src": _L0_gnn_in["a_src"],
        "L0_gnn_a_dst": _L0_gnn_in["a_dst"],
        "L0_gnn_bias": _L0_gnn_in["bias"],
        "L0_gnn_ln_gamma": _L0_gnn_in["ln_gamma"],
        "L0_gnn_ln_beta": _L0_gnn_in["ln_beta"],
        "L0_ffn_W_in": _L0_ffn_in["W_in"],
        "L0_ffn_conv_w": _L0_ffn_in["conv_w"],
        "L0_ffn_conv_b": _L0_ffn_in["conv_b"],
        "L0_ffn_dt_bias": _L0_ffn_in["dt_bias"],
        "L0_ffn_A_log": _L0_ffn_in["A_log"],
        "L0_ffn_D": _L0_ffn_in["D"],
        "L0_ffn_norm_w": _L0_ffn_in["norm_w"],
        "L0_ffn_W_out": _L0_ffn_in["W_out"],
        "L0_ffn_W_lin": _L0_ffn_in["W_lin"],
        "L0_ffn_b_lin": _L0_ffn_in["b_lin"],
        "L1_gnn_W": _L1_gnn_in["W"],
        "L1_gnn_a": _L1_gnn_in["a"],
        "L1_ffn_W_ih": _L1_ffn_in["W_ih"],
        "L1_ffn_W_hh": _L1_ffn_in["W_hh"],
        "L1_ffn_b_ih": _L1_ffn_in["b_ih"],
        "L1_ffn_b_hh": _L1_ffn_in["b_hh"],
        "L1_ffn_W_lin": _L1_ffn_in["W_lin"],
        "L1_ffn_b_lin": _L1_ffn_in["b_lin"],
        "L1_ffn_fw_att": _L1_ffn_in["fw_att"],
        "L1_ffn_bw_att": _L1_ffn_in["bw_att"],
    }

def reference(x, adj, L0_gnn_W, L0_gnn_a_src, L0_gnn_a_dst, L0_gnn_bias, L0_gnn_ln_gamma, L0_gnn_ln_beta, L0_ffn_W_in, L0_ffn_conv_w, L0_ffn_conv_b, L0_ffn_dt_bias, L0_ffn_A_log, L0_ffn_D, L0_ffn_norm_w, L0_ffn_W_out, L0_ffn_W_lin, L0_ffn_b_lin, L1_gnn_W, L1_gnn_a, L1_ffn_W_ih, L1_ffn_W_hh, L1_ffn_b_ih, L1_ffn_b_hh, L1_ffn_W_lin, L1_ffn_b_lin, L1_ffn_fw_att, L1_ffn_bw_att):
    import jax
    import jax.numpy as jnp
    def _L0_gnn_ref(nodes_embed, node_adj, W, a_src, a_dst, bias, ln_gamma, ln_beta):
        import jax, jax.numpy as jnp
        import numpy as np
        B, N, D = (8, 1024, 256)
        H, HO = (4, 64)
        T = 5
        NEG = -1000000000.0
        EPS = 1e-06
        h = jnp.einsum('bnd,hde->bhne', nodes_embed, W)
        e_src = jnp.einsum('bhne,hte->bhtn', h, a_src)
        e_dst = jnp.einsum('bhne,hte->bhtn', h, a_dst)
        n_types = a_src.shape[1]
        weight = jnp.zeros(h.shape[:2] + (h.shape[2], h.shape[2]), dtype=h.dtype)
        for t in range(n_types):
            mask = (node_adj == t + 1).astype(h.dtype)[:, None]
            weight = weight + mask * (e_src[:, :, t, :, None] + e_dst[:, :, t, None, :])
        weight = jax.nn.leaky_relu(weight, negative_slope=0.01)
        weight = jnp.where(node_adj[:, None] == 0, NEG, weight)
        attention = jax.nn.softmax(weight, axis=-1)
        dst = jnp.einsum('bhij,bhje->bhie', attention, h) + bias[None, :, None, :]
        out = jax.nn.relu(dst) + h
        mu = out.mean(axis=-1, keepdims=True)
        var = out.var(axis=-1, keepdims=True)
        out = (out - mu) / jnp.sqrt(var + EPS) * ln_gamma[None, :, None, :] + ln_beta[None, :, None, :]
        b, hh, n, e = out.shape
        return out.transpose(0, 2, 1, 3).reshape(b, n, hh * e)

    def _L0_ffn_ref(x, W_in, conv_w, conv_b, dt_bias, A_log, D, norm_w, W_out, W_lin, b_lin):
        import jax, jax.numpy as jnp
        import numpy as np
        D_MODEL = 256
        D_STATE = 64
        D_CONV = 4
        EXPAND = 2
        HEADDIM = 64
        D_INNER = EXPAND * D_MODEL
        NHEADS = D_INNER // HEADDIM
        CONV_DIM = D_INNER + 2 * D_STATE
        D_IN_PROJ = 2 * D_INNER + 2 * D_STATE + NHEADS
        CHUNK = 256
        EPS = 1e-05

        def segsum(a):
            T = a.shape[-1]
            cs = jnp.cumsum(a, axis=-1)
            ss = cs[..., :, None] - cs[..., None, :]
            mask = jnp.tril(jnp.ones((T, T), dtype=bool))
            return jnp.where(mask, ss, -jnp.inf)

        def mamba2_block(x, W_in, conv_w, conv_b, dt_bias, A_log, D, norm_w, W_out, W_lin, b_lin):
            Bsz, L, _ = x.shape
            zxbcdt = x @ W_in
            z, xBC, dt = jnp.split(zxbcdt, [D_INNER, D_INNER + CONV_DIM], axis=-1)
            xp = jnp.pad(xBC, ((0, 0), (D_CONV - 1, 0), (0, 0)))
            conv = conv_b + sum((xp[:, k:k + L, :] * conv_w[:, k] for k in range(D_CONV)))
            xBC = jax.nn.silu(conv)
            xh, Bmat, Cmat = jnp.split(xBC, [D_INNER, D_INNER + D_STATE], axis=-1)
            dt = jax.nn.softplus(dt + dt_bias)
            A = -jnp.exp(A_log)
            nc = L // CHUNK
            xh = xh.reshape(Bsz, nc, CHUNK, NHEADS, HEADDIM)
            Bc = Bmat.reshape(Bsz, nc, CHUNK, D_STATE)
            Cc = Cmat.reshape(Bsz, nc, CHUNK, D_STATE)
            dtc = dt.reshape(Bsz, nc, CHUNK, NHEADS)
            dA = jnp.einsum('bclh,h->bhcl', dtc, A)
            A_cum = jnp.cumsum(dA, axis=-1)
            Lmat = jnp.exp(segsum(dA))
            xdt = xh * dtc[..., None]
            Y_diag = jnp.einsum('bcln,bcsn,bhcls,bcshp->bclhp', Cc, Bc, Lmat, xdt)
            decay_states = jnp.exp(A_cum[..., -1:] - A_cum)
            states = jnp.einsum('bcln,bhcl,bclhp->bchpn', Bc, decay_states, xdt)
            chunk_decay = jnp.exp(A_cum[..., -1])

            def step(h, inp):
                s, d = inp
                return (h * d[..., None, None] + s, h)
            _, prevs = jax.lax.scan(step, jnp.zeros_like(states[:, 0]), (jnp.moveaxis(states, 1, 0), jnp.moveaxis(chunk_decay, 2, 0)))
            prevs = jnp.moveaxis(prevs, 0, 1)
            Y_off = jnp.einsum('bcln,bchpn,bhcl->bclhp', Cc, prevs, jnp.exp(A_cum))
            Y = (Y_diag + Y_off + xh * D[:, None]).reshape(Bsz, L, D_INNER)
            Y = Y * jax.nn.silu(z)
            Y = Y * jax.lax.rsqrt(jnp.mean(Y * Y, axis=-1, keepdims=True) + EPS) * norm_w
            out = Y @ W_out
            return out @ W_lin + b_lin
        return mamba2_block(x, W_in, conv_w, conv_b, dt_bias, A_log, D, norm_w, W_out, W_lin, b_lin)

    def _L1_gnn_ref(h, adj, W, a):
        import jax, jax.numpy as jnp
        import numpy as np
        NEG_INF = -1000000000.0
        LEAKY_ALPHA = 0.2
        Wh = jnp.einsum('bnd,de->bne', h, W)
        Dout = Wh.shape[-1]
        a1, a2 = (a[:Dout], a[Dout:])
        f_i = Wh @ a1
        f_j = Wh @ a2
        e = f_i[:, :, None] + f_j[:, None, :]
        e = jax.nn.leaky_relu(e, negative_slope=LEAKY_ALPHA)
        e = jnp.where(adj > 0, e, NEG_INF)
        alpha = jax.nn.softmax(e, axis=-1)
        out = jnp.einsum('bij,bjd->bid', alpha, Wh)
        return jax.nn.elu(out)

    def _L1_ffn_ref(x, W_ih, W_hh, b_ih, b_hh, W_lin, b_lin, fw_att, bw_att):
        import jax, jax.numpy as jnp
        import numpy as np
        B, T, D, H, L = (16, 4096, 256, 256, 2)

        def _lstm(x, W_ih, W_hh, b_ih, b_hh):
            x_proj = jnp.einsum('btd,gd->btg', x, W_ih) + b_ih + b_hh
            h0 = jnp.zeros((x.shape[0], W_hh.shape[1]), x.dtype)
            c0 = jnp.zeros_like(h0)

            def step(carry, xp):
                h, c = carry
                gates = xp + h @ W_hh.T
                i, f, g, o = jnp.split(gates, 4, axis=-1)
                c = jax.nn.sigmoid(f) * c + jax.nn.sigmoid(i) * jnp.tanh(g)
                h = jax.nn.sigmoid(o) * jnp.tanh(c)
                return ((h, c), h)
            _, hs = jax.lax.scan(step, (h0, c0), jnp.swapaxes(x_proj, 0, 1))
            return jnp.swapaxes(hs, 0, 1)
        lstm_out = _lstm(x, W_ih, W_hh, b_ih, b_hh)
        logits = jnp.einsum('bth,lh->btl', lstm_out, W_lin) + b_lin
        g = jax.lax.stop_gradient(jnp.argmax(logits, axis=-1).astype(lstm_out.dtype))[..., None]
        w = g * lstm_out
        inc = jnp.cumsum(w, axis=1)
        prefix = inc - w
        suffix = inc[:, -1:, :] - inc
        return 2.0 * lstm_out + prefix * fw_att + suffix * bw_att

    x = x + _L0_gnn_ref(_layernorm(x, axis=-1), adj, L0_gnn_W, L0_gnn_a_src, L0_gnn_a_dst, L0_gnn_bias, L0_gnn_ln_gamma, L0_gnn_ln_beta)
    x = x + _L0_ffn_ref(_layernorm(x, axis=-1), L0_ffn_W_in, L0_ffn_conv_w, L0_ffn_conv_b, L0_ffn_dt_bias, L0_ffn_A_log, L0_ffn_D, L0_ffn_norm_w, L0_ffn_W_out, L0_ffn_W_lin, L0_ffn_b_lin)
    x = x + _L1_gnn_ref(_layernorm(x, axis=-1), adj, L1_gnn_W, L1_gnn_a)
    x = x + _L1_ffn_ref(_layernorm(x, axis=-1), L1_ffn_W_ih, L1_ffn_W_hh, L1_ffn_b_ih, L1_ffn_b_hh, L1_ffn_W_lin, L1_ffn_b_lin, L1_ffn_fw_att, L1_ffn_bw_att)
    return x


_drawn_inputs = setup_inputs


def setup_inputs(seed=0):
    import zlib

    import numpy as np

    out = dict(_drawn_inputs(seed))
    spreads = {'L0_gnn_bias': (0.0, 0.1),
     'L0_gnn_ln_gamma': (1.0, 0.2),
     'L0_gnn_ln_beta': (0.0, 0.1),
     'L0_ffn_D': (1.0, 0.2),
     'L0_ffn_norm_w': (1.0, 0.2),
     'L0_ffn_b_lin': (0.0, 0.1),
     'L1_ffn_fw_att': (0.0010000000474974513, 0.6),
     'L1_ffn_bw_att': (0.0010000000474974513, 0.6)}
    factors = {'L1_ffn_b_ih': 3.386, 'L1_ffn_b_hh': 3.337, 'L1_ffn_W_lin': 8.0, 'L1_ffn_b_lin': 8.0}
    for name, (base, spread) in spreads.items():
        noise = np.random.default_rng([zlib.crc32(name.encode()), seed]).standard_normal(out[name].shape)
        drawn = base * np.exp(spread * noise) if base else spread * noise
        out[name] = jnp.asarray(drawn.astype(out[name].dtype))
    for name, factor in factors.items():
        out[name] = (out[name] * factor).astype(out[name].dtype)
    return out
```

```python
from contextlib import ExitStack

import numpy as np
import concourse.bass as bass
from concourse import mybir

F32 = mybir.dt.float32
BF16 = mybir.dt.bfloat16
I32 = mybir.dt.int32
ALU = mybir.AluOpType
ACT = mybir.ActivationFunctionType
AX = mybir.AxisListType.X

P = 128
D = 256
KC = D // P
NEG = -(2.0 ** 100)
EPS_LN = 1e-5
SLOTS = 3


PRE = (1, 3, 5)
POST_PE = (8, 10)
SQUARE = 14


class Batch:

    def __init__(self, reg, off, slots):
        self.reg, self.off, self.slots = reg, off, slots

    def __add__(self, n):
        return Batch(self.reg, self.off + n, self.slots)

    @property
    def slot(self):
        return self.off % self.slots

    def index(self):
        return self.off if self.reg is None else self.reg * self.slots + self.off

    def wait(self, eng, sem, per, more):
        least = self.off * per + more
        if self.reg is None:
            if least > 0:
                eng.wait_ge(sem, least)
        else:
            assert least >= 1, (sem, least)
            eng.wait_ge(sem, self.reg * (self.slots * per) + least)


    def wait_apart(self, eng, passed, sem, per, more):
        self.wait(eng, sem, per, more)
        if self.reg is not None:
            eng.sem_inc(passed, 1)

    def dma_wait(self, eng, sems, more=0):
        n = self.off // self.slots + 1 + more
        if self.reg is not None:
            assert n >= 1
            eng.wait_ge(sems[self.slot], self.reg * 16 + 16 * n)
        elif n > 0:
            eng.wait_ge(sems[self.slot], 16 * n)


    def dma_wait4(self, eng, sems):
        n = 64 * (self.off // self.slots + 1)
        eng.wait_ge(sems[self.slot], n if self.reg is None else self.reg * 64 + n)


def pipeline(eng, nb, before, body, after, slots=SLOTS):
    before(Batch(None, 0, slots))
    start = slots + 1
    rounds = (nb - 1 - start) // slots
    for b in range(min(start, nb)):
        body(Batch(None, b, slots))
    if rounds > 1:
        with eng.Fori(0, rounds) as i:
            for k in range(slots):
                body(Batch(i, start + k, slots))
        start += slots * rounds
    for b in range(start, nb):
        body(Batch(None, b, slots))
    after(Batch(None, nb - 1, slots))


class Memory:

    def __init__(self, nc, ctx, tag):
        self.nc, self.ctx, self.tag = nc, ctx, tag
        self.sems = []

    def sb(self, name, shape, dt=F32):
        return self.ctx.enter_context(self.nc.sbuf_tensor(f"{self.tag}_{name}", shape, dt))

    def ps(self, name, shape=(P, 512), dt=F32):
        return self.ctx.enter_context(self.nc.psum_tensor(f"{self.tag}_{name}_psum", list(shape), dt))

    def sem(self, name):
        self.sems.append(self.ctx.enter_context(self.nc.semaphore(f"{self.tag}_{name}")))
        return self.sems[-1]

    def clear(self):
        with self.nc.Block() as block:
            @block.gpsimd
            def _(g):
                for sem in self.sems:
                    g.sem_clear(sem)


def bcast(ap, n):
    return ap.unsqueeze(len(ap.shape)).to_broadcast(list(ap.shape) + [n])


def selectors():
    types = 4
    out = np.zeros((P, 2 + 2 * types * 4), np.float32)
    for q in (0, 64, 96):
        for t in range(types):
            for h in range(4):
                src, dst = q + 8 * t + h, q + 8 * t + 4 + h
                out[src, 0] = 1.0
                out[dst, 1] = 1.0
                c = 2 + 2 * (4 * t + h)
                out[dst, c] = 1.0
                out[src, c + 1] = 1.0
    return out


def decay_selectors():
    out = np.zeros((P, 2 + 2 * 8), np.float32)
    for q in (0, 64, 96):
        for h in range(8):
            pos, neg = q + h, q + 8 + h
            out[neg, 0] = 1.0
            out[pos, 1] = 1.0
            out[pos, 2 + 2 * h] = 1.0
            out[neg, 3 + 2 * h] = 1.0
    return out


def constants():
    tri = np.where(np.arange(P)[:, None] <= np.arange(P)[None, :], 0.0, NEG).astype(np.float32)
    repeat = np.zeros((P, P), np.float32)
    for b in range(32):
        repeat[b, b::32] = 1.0
    return {"repeat": repeat, "identity": np.eye(P, dtype=np.float32), "selectors": selectors(), "decay_selectors": decay_selectors(), "causal": tri}


def attention_phase(nc, layer, nb, x_in, adj, weights, consts, x_out):
    first = layer == 0
    H = 4 if first else 1
    E = D // H
    N = 512
    IT = N // P
    ALPHA = 0.01 if first else 0.2
    NP = 2 if first else 1
    ITEMS = NP * IT * (2 if first else 1)
    HH = ITEMS // (NP * IT)
    with ExitStack() as ctx:
        m = Memory(nc, ctx, f"g{layer}")
        ident = m.sb("ident", [P, P])
        ident_bf = m.sb("ident_bf", [P, P], BF16)
        sel = m.sb("sel", [P, 34])
        W = m.sb("W", [P, KC, D])
        WA = m.sb("WA", [P, KC, P])
        X = [m.sb(f"X{k}", [P, IT, D]) for k in range(SLOTS)]
        ADJ = m.sb("ADJ", [P, IT, N], I32)
        MASK = [m.sb(f"MASK{k}", [P, IT, N], BF16) for k in range(SLOTS)]
        stats = m.sb("stats", [P, IT, 6])
        mv = m.sb("mv", [P, IT, 2])
        rstd = m.sb("rstd", [P, IT])
        half = m.sb("half", [P, 16])
        XN = m.sb("XN", [P, IT, D])
        XT = m.sb("XT", [P, KC, N])
        HS = [m.sb(f"HS{k}", [P, IT, D]) for k in range(SLOTS)]
        parts = m.sb("parts", [P, N], BF16)
        rest = m.sb("rest", [P, N])
        L = [m.sb(f"L{k}", [P, N], BF16) for k in range(SLOTS)]
        R = [m.sb(f"R{k}", [P, H, N], BF16) for k in range(SLOTS)]
        relu = [m.sb(f"relu{k}", [P, N]) for k in range(2)]
        S = [m.sb(f"S{k}", [P, N]) for k in range(2)]
        nmax = m.sb("nmax", [P, 2])
        PR = [m.sb(f"PR{k}", [P, N]) for k in range(2)]
        PT = [m.sb(f"PT{k}", [P, N]) for k in range(4)]
        rsum = [m.sb(f"rsum{k}", [P, IT, H]) for k in range(SLOTS)]
        rinv = m.sb("rinv", [P, IT, H])
        OT = m.sb("OT", [P, 2, N])
        G = m.sb("G", [P, IT, D])
        XO = [m.sb(f"XO{k}", [P, IT, D]) for k in range(SLOTS)]
        Zb = [m.ps(f"Z{k}") for k in range(2)]
        PTb = [m.ps(f"PT{k}") for k in range(2)]
        Ob = [m.ps(f"O{k}") for k in range(2)]
        Ab = [m.ps(f"A{k}") for k in range(2)]

        names = ("const w setup_pe setup_v adj_loaded mask mv rstd xn xt_pe xt h_pe h hb e_pe parts lr "
                 "z relu s p t ev pv ot ob d1 d3 sum d4 sq ssq out rinv v zero").split()
        s = {n: m.sem(n) for n in names}
        x_loaded = [m.sem(f"x_loaded{k}") for k in range(SLOTS)]
        stored = [m.sem(f"stored{k}") for k in range(SLOTS)]
        if first:
            HB = [m.sb(f"HB{k}", [P, IT, D]) for k in range(SLOTS)]
            arow = m.sb("arow", [64, E])
            aT = m.sb("aT", [64, 64])
            WT = m.sb("WT", [64, H, D])
            bias, gamma, beta = (m.sb(n, [P, D]) for n in ("bias", "gamma", "beta"))
            sums = m.sb("sums", [P, 16])
            ssq = m.sb("ssq", [P, 16])
            SQ = m.sb("SQ", [P, IT, D])
            XB = m.sb("XB", [P, IT, D])
        else:
            HB = HS
            arow = m.sb("arow", [P, KC, 2])
            WT = m.sb("WT", [P, KC, D])
            mn = m.sb("mn", [P, IT, D])
            ex = m.sb("ex", [P, IT, D])

        xv = x_in.rearrange("b (t p) d -> b p t d", p=P)
        av = adj.rearrange("b (t p) j -> b p t j", p=P)
        ov = x_out.rearrange("b (t p) d -> b p t d", p=P)
        n_w = 6 * 16 if first else 3 * 16
        passed_v, passed_g, passed_pe = (m.sem(f"passed_{n}") for n in ("v", "g", "pe"))
        ctx.callback(m.clear)
        block = ctx.enter_context(nc.Block())

        @block.sync
        def _(sp):
            sp.dma_start(ident[:, :], consts["identity"]).then_inc(s["const"], 16)
            sp.dma_start(sel[:, :], consts["selectors"]).then_inc(s["const"], 16)
            if first:
                for kc in range(KC):
                    sp.dma_start(W[:, kc, :].rearrange("k (h e) -> k h e", h=H),
                                 weights["W"][:, kc * P:(kc + 1) * P, :].rearrange("h k e -> k h e")
                                 ).then_inc(s["w"], 16)
                sp.wait_ge(s["zero"], 1)
                sp.dma_start(arow[0:20, :], weights["a_src"].rearrange("h t e -> (h t) e")).then_inc(s["w"], 16)
                sp.dma_start(arow[32:52, :], weights["a_dst"].rearrange("h t e -> (h t) e")).then_inc(s["w"], 16)
                sp.dma_start(gamma[:, :], weights["gamma"].rearrange("(o h) e -> o (h e)", o=1).to_broadcast([P, D])
                             ).then_inc(s["w"], 16)
                sp.dma_start(beta[:, :], weights["beta"].rearrange("(o h) e -> o (h e)", o=1).to_broadcast([P, D])
                             ).then_inc(s["w"], 16)
                sp.dma_start(bias[:, :], weights["bias"].rearrange("(o h) e -> o (h e)", o=1).to_broadcast([P, D])
                             ).then_inc(s["const"], 16)
            else:
                sp.dma_start(W[:, :, :], weights["W"].rearrange("(c k) e -> k c e", k=P)).then_inc(s["w"], 16)
                for c in range(2):
                    sp.dma_start(arow[:, :, c], weights["a"][c * D:(c + 1) * D].rearrange("(k p) -> p k", p=P),
                                 allow_slow_non_contiguous=True
                                 ).then_inc(s["w"], 16)

            def load(b):
                b.wait(sp, s["out"], 1, 1 - SLOTS)
                sp.dma_start(X[b.slot][:, :, :], xv[b.index()]).then_inc(x_loaded[b.slot], 16)
                b.wait(sp, s["mask"], 1, 0)
                sp.dma_start(ADJ[:, :, :], av[b.index()]).then_inc(s["adj_loaded"], 16)

            def body(b):
                if b.reg is not None or b.off < nb - 1:
                    load(b + 1)
                if b.reg is not None or b.off > 0:
                    store(b + -1)

            def store(b):
                b.wait(sp, s["out"], 1, 1)
                sp.dma_start(ov[b.index()], XO[b.slot][:, :, :]).then_inc(stored[b.slot], 16)

            pipeline(sp, nb, load, body, store)
            for k in range(SLOTS):
                sp.wait_ge(stored[k], 16 * len(range(k, nb, SLOTS)))

        @block.tensor
        def _(pe):
            pe.wait_ge(s["const"], 48 if first else 32)
            pe.wait_ge(s["w"], n_w)
            if first:
                pe.transpose(Zb[0][0:64, 0:64], arow[:, :], ident[0:64, 0:64])
                for h in range(H):
                    for kc in range(KC):
                        ins = pe.transpose(Zb[1 + 0 * h][0:E, (h % 2) * D + kc * P:(h % 2) * D + (kc + 1) * P]
                                           if h < 2 else
                                           PTb[0][0:E, (h % 2) * D + kc * P:(h % 2) * D + (kc + 1) * P],
                                           W[:, kc, h * E:(h + 1) * E], ident[:, :])
                ins.then_inc(s["setup_pe"], 1)
                pe.wait_ge(s["setup_v"], 5)
                aTv = aT[:, :].rearrange("e (s x) -> e s x", s=2)
                for kc in range(KC):
                    for h in range(H):
                        ins = pe.matmul(Ab[kc][:, 10 * h:10 * h + 10].rearrange("p (s t) -> p s t", s=2),
                                        WT[:, h, kc * P:(kc + 1) * P],
                                        aTv[:, :, 5 * h:5 * h + 5], start=True, stop=True)
                ins.then_inc(s["setup_pe"], 1)
            else:
                for e in range(KC):
                    for kc in range(KC):
                        ins = pe.transpose(Zb[e][:, kc * P:(kc + 1) * P], W[:, kc, e * P:(e + 1) * P], ident[:, :])
                ins.then_inc(s["setup_pe"], 1)
                pe.wait_ge(s["setup_v"], 4)
                for kc in range(KC):
                    for e in range(KC):
                        ins = pe.matmul(Ab[kc][:, 0:2], WT[:, e, kc * P:(kc + 1) * P], arow[:, e, :],
                                        start=(e == 0), stop=(e == KC - 1))
                ins.then_inc(s["setup_pe"], 1)
            pe.wait_ge(s["setup_v"], 8)

            def xn_turned(b):
                b.wait(pe, s["xn"], IT, IT)
                for kc in range(KC):
                    if kc == 0:
                        b.wait(pe, s["parts"], 1, 0)
                    elif first:
                        b.wait(pe, s["d1"], NP, -2 * NP)
                    for t in range(IT):
                        ins = pe.transpose(Ab[kc][:, t * P:(t + 1) * P], XN[:, t, kc * P:(kc + 1) * P], ident[:, :])
                    ins.then_inc(s["xt_pe"], 1)

            def project(b):
                for g in range(2):
                    b.wait(pe, s["xt"], 2, 2)
                    for t in (2 * g, 2 * g + 1):
                        for kc in range(KC):
                            ins = pe.matmul(Ab[g][:, (t % 2) * D:(t % 2 + 1) * D], XT[:, kc, t * P:(t + 1) * P],
                                            W[:, kc, :], start=(kc == 0), stop=(kc == KC - 1))
                    ins.then_inc(s["h_pe"], 1)

            def logits(b):
                b.wait(pe, s["h"], 2, 1)
                for kc in range(KC):
                    ins = pe.matmul(Ab[0][:, :], WA[:, kc, :], XT[:, kc, :], start=(kc == 0), stop=(kc == KC - 1))
                ins.then_inc(s["e_pe"], 1)

            def scores(b, n):
                p, t, hh = n // (IT * HH), n // HH % IT, n % HH
                if n == 0:
                    b.wait(pe, s["lr"], H + 1, H + 1)
                    b.wait(pe, s["mask"], 1, 1)
                b.wait(pe, s["s"], ITEMS, n - 1)
                pe.matmul(Zb[n % 2][:, :], L[b.slot][:, t * P:(t + 1) * P], R[b.slot][:, HH * p + hh, :],
                          start=True, stop=False)
                pe.matmul(Zb[n % 2][:, :], ident_bf[:, :], MASK[b.slot][:, t, :],
                          start=False, stop=True).then_inc(s["z"], 1)

            def turn(b, n):
                b.wait(pe, s["p"], ITEMS, n + 1)
                b.wait(pe, s["ev"], ITEMS, n - 1)
                for k in range(IT):
                    ins = pe.transpose(PTb[n % 2][:, k * P:(k + 1) * P], PR[n % 2][:, k * P:(k + 1) * P], ident[:, :])
                ins.then_inc(s["t"], 1)

            def weigh(b, u):
                p, t = u // IT, u % IT
                b.wait(pe, s["ev"], ITEMS, HH * (u + 1))
                if u == 0:
                    b.wait(pe, s["hb"] if first else s["h"], 1 if first else 2, 1 if first else 2)
                if t == 0:
                    b.wait(pe, s["ot"], 2, p - 1 if first else 0)
                if first:
                    for k in range(IT):
                        for hh in range(HH):
                            ins = pe.matmul(Ob[p][hh * E:(hh + 1) * E, t * P:(t + 1) * P],
                                            HB[b.slot][:, k, (HH * p + hh) * E:(HH * p + hh + 1) * E],
                                            PT[(HH * u + hh) % 4][:, k * P:(k + 1) * P],
                                            start=(k == 0), stop=(k == IT - 1), skip_group_check=True)
                else:
                    for k in range(IT):
                        ins = pe.matmul(Ob[t // 2][:, (t % 2) * D:(t % 2 + 1) * D],
                                        PT[u % 4][:, k * P:(k + 1) * P], HB[b.slot][:, k, :],
                                        start=(k == 0), stop=(k == IT - 1))
                ins.then_inc(s["pv"], 1)

            def outputs_turned(b, p, newest):
                b.wait(pe, s["ot"], 2, p + 1)
                if p == 0:
                    newest.wait(pe, s["h"], 2, 2)
                else:
                    b.wait(pe, s["d1"], NP, p)
                for t in range(IT):
                    ins = pe.transpose(Ab[1][:, t * P:(t + 1) * P], OT[:, p, t * P:(t + 1) * P], ident[:, :])
                ins.then_inc(s["ob"], 1)

            def pre(b):
                xn_turned(b)
                project(b)
                logits(b)

            def body(b):
                some = b.reg is not None
                nxt, prev = some or b.off < nb - 1, some or b.off > 0
                for n in range(ITEMS + 3):
                    if n < ITEMS:
                        scores(b, n)
                    if 1 <= n <= ITEMS:
                        turn(b, n - 1)
                    if n >= 3 and (n - 3) % HH == HH - 1:
                        weigh(b, (n - 3) // HH)
                    if nxt and n == PRE[0]:
                        xn_turned(b + 1)
                    if nxt and n == PRE[1]:
                        project(b + 1)
                    if nxt and n == PRE[2]:
                        logits(b + 1)
                    if first and prev and n in POST_PE:
                        outputs_turned(b + -1, POST_PE.index(n), b + 1 if nxt else b)

            def after(b):
                if first:
                    for p in range(NP):
                        outputs_turned(b, p, b)

            pipeline(pe, nb, pre, body, after)

        @block.scalar
        def _(act):
            def xt_out(b):
                for kc in range(KC):
                    b.wait(act, s["xt_pe"], 2, kc + 1)
                    if kc == 0:
                        b.wait(act, s["e_pe"], 1, 0)
                    act.activation(XT[:, kc, :], Ab[kc][:, :], ACT.Copy).then_inc(s["xt"], 1)

            def h_out(b):
                b.wait(act, s["out" if first else "pv"], 1 if first else IT, (1 - SLOTS) * (1 if first else IT))
                for g in range(2):
                    b.wait(act, s["h_pe"], 2, g + 1)
                    act.activation(HS[b.slot][:, 2 * g:2 * g + 2, :].rearrange("p t d -> p (t d)"),
                                   Ab[g][:, :], ACT.Copy).then_inc(s["h"], 1)

            def relu_part(b, n):
                b.wait(act, s["z"], ITEMS, n + 1)
                b.wait(act, s["s"], ITEMS, n - 1)
                act.activation(relu[n % 2][:, :], Zb[n % 2][:, :], ACT.Relu,
                               scale=(1.0 - ALPHA) / ALPHA).then_inc(s["relu"], 1)

            def exp(b, n):
                p, t, hh = n // (IT * HH), n // HH % IT, n % HH
                b.wait(act, s["s"], ITEMS, n + 1)
                b.wait(act, s["t"], ITEMS, n - 1)
                if n == 0:
                    b.wait(act, s["rinv"], 1, 1 - SLOTS)
                act.activation(PR[n % 2][:, :], S[n % 2][:, :], ACT.Exp, scale=-1.0, bias=nmax[:, n % 2:n % 2 + 1],
                               accum_out=rsum[b.slot][:, t, HH * p + hh:HH * p + hh + 1]).then_inc(s["p"], 1)

            def o_out(b, p):
                b.wait(act, s["pv"], 2 * IT, IT * (p + 1))
                b.wait(act, s["ob"], NP, p - 1)
                act.activation(OT[:, p, :], Ob[p][:, :], ACT.Copy).then_inc(s["ot"], 1)

            def square(b):
                b.wait(act, s["d4"], 1, 1)
                act.activation(SQ[:, :, :].rearrange("p t d -> p (t d)"), G[:, :, :].rearrange("p t d -> p (t d)"),
                               ACT.Square).then_inc(s["sq"], 1)

            def pre(b):
                xt_out(b)
                h_out(b)

            def body(b):
                some = b.reg is not None
                nxt, prev = some or b.off < nb - 1, some or b.off > 0
                for n in range(ITEMS + 1):
                    if n < ITEMS:
                        relu_part(b, n)
                    if n >= 1:
                        exp(b, n - 1)
                    if nxt and n == PRE[0]:
                        xt_out(b + 1)
                    if nxt and n == PRE[1]:
                        h_out(b + 1)
                    if first and prev and n == 1:
                        o_out(b + -1, 1)
                    if first and n == 12:
                        o_out(b, 0)
                    if first and prev and n == SQUARE:
                        square(b + -1)

            def after(b):
                if first:
                    o_out(b, 1)
                    square(b)

            if first:
                pipeline(act, nb, pre, body, after)
            else:
                def gnn1_exp(b):
                    b.wait(act, s["d3"], 1, 1)
                    act.activation(ex[:, :, :].rearrange("p t d -> p (t d)"),
                                   mn[:, :, :].rearrange("p t d -> p (t d)"), ACT.Exp).then_inc(s["sq"], 1)

                def body1(b):
                    some = b.reg is not None
                    body(b)
                    gnn1_exp(b)

                pipeline(act, nb, pre, body1, lambda b: None)

        @block.vector
        def _(v):
            if first:
                v.memset(arow[:, :], 0.0).then_inc(s["zero"], 1)
            v.memset(half[:, :], -0.5).then_inc(s["v"], 1)
            v.memset(WA[:, :, :], 0.0).then_inc(s["v"], 1)
            v.wait_ge(s["const"], 48 if first else 32)
            v.wait_ge(s["v"], 2)
            v.tensor_copy(ident_bf[:, :], ident[:, :]).then_inc(s["setup_v"], 1)
            v.wait_ge(s["setup_pe"], 1)
            if first:
                v.tensor_copy(aT[:, :], Zb[0][0:64, 0:64]).then_inc(s["setup_v"], 1)
                v.tensor_copy(WT[:, 0:2, :].rearrange("e h d -> e (h d)"), Zb[1][0:64, :]).then_inc(s["setup_v"], 1)
                v.tensor_copy(WT[:, 2:4, :].rearrange("e h d -> e (h d)"), PTb[0][0:64, :]).then_inc(s["setup_v"], 1)
                v.nop().then_inc(s["setup_v"], 1)
                v.wait_ge(s["setup_pe"], 2)
                for q in (0, 64, 96):
                    for kc in range(KC):
                        for side in range(2):
                            ins = v.tensor_scalar(
                                WA[:, kc, q:q + 32].rearrange("p (t s h) -> p s h t", s=2, h=H)[:, side],
                                Ab[kc][:, 0:40].rearrange("p (h s t) -> p s h t", s=2, t=5)[:, side, :, 0:4],
                                ALPHA, None, ALU.mult)
                for _ in range(3):
                    ins = v.nop().then_inc(s["setup_v"], 1) if _ else ins.then_inc(s["setup_v"], 1)
            else:
                for e in range(KC):
                    v.tensor_copy(WT[:, e, :], Zb[e][:, 0:D]).then_inc(s["setup_v"], 1)
                v.nop().then_inc(s["setup_v"], 1)
                v.wait_ge(s["setup_pe"], 2)
                for q in (0, 64, 96):
                    for kc in range(KC):
                        for side in range(2):
                            ins = v.tensor_scalar(WA[:, kc, q + 4 * side:q + 4 * side + 1],
                                                  Ab[kc][:, side:side + 1], ALPHA, None, ALU.mult)
                for _ in range(4):
                    ins = v.nop().then_inc(s["setup_v"], 1) if _ else ins.then_inc(s["setup_v"], 1)

            def norm_stats(b):
                b.dma_wait(v, x_loaded)
                b.wait(v, s["xn"], IT, 0)
                for t in range(IT):
                    ins = v.bn_stats(stats[:, t, :], X[b.slot][:, t, :])
                ins.then_inc(s["v"], 1)
                b.wait_apart(v, passed_v, s["v"], NV, 2 + 1)
                for t in range(IT):
                    ins = v.bn_aggr(mv[:, t, :], stats[:, t, :])
                ins.then_inc(s["mv"], 1)

            def make_mask(b):
                b.wait(v, s["adj_loaded"], 16, 16)
                b.wait(v, s["z"], ITEMS, (1 - SLOTS) * ITEMS)
                v.tensor_scalar(MASK[b.slot][:, :, :].rearrange("p t j -> p (t j)"),
                                ADJ[:, :, :].rearrange("p t j -> p (t j)"), 0.0 if first else 0.5, NEG,
                                ALU.is_equal if first else ALU.is_lt, ALU.mult).then_inc(s["mask"], 1)

            def split(b):
                b.wait(v, s["e_pe"], 1, 1)
                b.wait(v, s["lr"], H + 1, 0)
                v.tensor_copy(parts[:, :], Ab[0][:, :]).then_inc(s["v"], 1)
                b.wait(v, s["v"], NV, 2 + 2)
                v.tensor_tensor(rest[64:P, :], Ab[0][64:P, :], parts[64:P, :], ALU.subtract).then_inc(s["v"], 1)
                b.wait(v, s["v"], NV, 2 + 3)
                v.tensor_copy(parts[64:P, :], rest[64:P, :]).then_inc(s["v"], 1)
                b.wait(v, s["v"], NV, 2 + 4)
                v.tensor_tensor(rest[96:P, :], rest[96:P, :], parts[96:P, :], ALU.subtract).then_inc(s["v"], 1)
                b.wait(v, s["v"], NV, 2 + 5)
                v.tensor_copy(parts[96:P, :], rest[96:P, :]).then_inc(s["parts"], 1)

            def leaky(b, n):
                b.wait(v, s["relu"], ITEMS, n + 1)
                b.wait_apart(v, passed_v, s["p"], ITEMS, n - 1)
                v.tensor_tensor_reduce(S[n % 2][:, :], Zb[n % 2][:, :], relu[n % 2][:, :], -1.0, 3e38,
                                       ALU.add, ALU.min, nmax[:, n % 2:n % 2 + 1]).then_inc(s["s"], 1)

            def evacuate(b, n):
                b.wait(v, s["t"], ITEMS, n + 1)
                b.wait(v, s["pv"], ITEMS // HH, (n - 4) // HH + 1)
                v.tensor_copy(PT[n % 4][:, :], PTb[n % 2][:, :]).then_inc(s["ev"], 1)

            def recip(b):
                b.wait(v, s["p"], ITEMS, ITEMS)
                b.wait(v, s["d1"], NP, 0)
                v.reciprocal(rinv[:, :, :].rearrange("p t h -> p (t h)"),
                             rsum[b.slot][:, :, :].rearrange("p t h -> p (t h)")).then_inc(s["rinv"], 1)

            def normalise(b, p):
                b.wait(v, s["ob"], NP, p + 1)
                if p == 0:
                    b.wait(v, s["rinv"], 1, 1)
                    b.wait(v, s["out"], 1, 0)
                v.tensor_tensor(G[:, :, 2 * p * E:2 * (p + 1) * E].rearrange("p t (h e) -> p t h e", h=2),
                                Ab[1][:, :].rearrange("p (t h e) -> p t h e", t=IT, h=2),
                                bcast(rinv[:, :, 2 * p:2 * p + 2], E), ALU.mult).then_inc(s["d1"], 1)

            flat = "p t d -> p (t d)"
            heads = "p t (h e) -> p (t h) e"

            def residual_sum(b):
                b.wait(v, s["d1"], NP, NP)
                v.scalar_tensor_tensor(out=G[:, :, :].rearrange(flat), in0=G[:, :, :].rearrange(flat), scalar=0.0,
                                       in1=HS[b.slot][:, :, :].rearrange(flat), op0=ALU.max,
                                       op1=ALU.add).then_inc(s["d3"], 1)
                b.wait(v, s["d3"], 1, 1)
                v.tensor_reduce(sums[:, :], G[:, :, :].rearrange(heads, h=H), AX, ALU.add).then_inc(s["sum"], 1)

            def squares_sum(b):
                b.wait(v, s["sq"], 1, 1)
                v.tensor_reduce(ssq[:, :], SQ[:, :, :].rearrange(heads, h=H), AX, ALU.add).then_inc(s["ssq"], 1)

            NV = 5

            def pre(b):
                norm_stats(b)
                make_mask(b)
                split(b)

            def body(b):
                some = b.reg is not None
                nxt, prev = some or b.off < nb - 1, some or b.off > 0
                for n in range(ITEMS + 2):
                    if n < ITEMS:
                        leaky(b, n)
                    if n >= 2:
                        evacuate(b, n - 2)
                    if nxt and n == 0:
                        norm_stats(b + 1)
                    if nxt and n == PRE[2]:
                        split(b + 1)
                    if nxt and n == 1 and not first or nxt and n == 7 and first:
                        make_mask(b + 1)
                    if first and prev:
                        if n == 1:
                            recip(b + -1)
                        if n in POST_PE:
                            normalise(b + -1, POST_PE.index(n))
                        if n == POST_PE[1] + 1:
                            residual_sum(b + -1)
                        if n == SQUARE + 1:
                            squares_sum(b + -1)

            def after(b):
                if first:
                    recip(b)
                    for p in range(NP):
                        normalise(b, p)
                    residual_sum(b)
                    squares_sum(b)

            def elu_sum(b):
                b.wait(v, s["p"], ITEMS, ITEMS)
                v.reciprocal(rinv[:, :, 0], rsum[b.slot][:, :, 0]).then_inc(s["rinv"], 1)
                b.wait(v, s["rinv"], 1, 1)
                b.wait(v, s["pv"], IT, IT)
                for g in range(2):
                    v.tensor_tensor(G[:, 2 * g:2 * g + 2, :], Ob[g][:, :].rearrange("p (t d) -> p t d", t=2),
                                    bcast(rinv[:, 2 * g:2 * g + 2, 0], D), ALU.mult).then_inc(s["ot"], 1)
                b.wait(v, s["ot"], 2, 2)
                v.tensor_scalar(mn[:, :, :].rearrange(flat), G[:, :, :].rearrange(flat), 0.0, None,
                                ALU.min).then_inc(s["d3"], 1)
                v.tensor_scalar(G[:, :, :].rearrange(flat), G[:, :, :].rearrange(flat), 0.0, -1.0,
                                ALU.max, ALU.add).then_inc(s["sum"], 1)
                b.wait(v, s["sum"], 1, 1)
                v.tensor_tensor(G[:, :, :].rearrange(flat), G[:, :, :].rearrange(flat),
                                X[b.slot][:, :, :].rearrange(flat), ALU.add).then_inc(s["d4"], 1)
                b.wait(v, s["d4"], 1, 1)
                b.wait(v, s["sq"], 1, 1)
                b.dma_wait(v, stored, -1)
                v.tensor_tensor(XO[b.slot][:, :, :].rearrange(flat), G[:, :, :].rearrange(flat),
                                ex[:, :, :].rearrange(flat), ALU.add).then_inc(s["out"], 1)

            if first:
                pipeline(v, nb, pre, body, after)
            else:
                def body1(b):
                    body(b)
                    elu_sum(b)

                pipeline(v, nb, pre, body1, lambda b: None)

        @block.gpsimd
        def _(g):
            pool = m.sem("pool")
            g.wait_ge(s["setup_v"], 8)

            def normalised(b):
                b.wait_apart(g, passed_g, s["mv"], 1, 1)
                b.wait_apart(g, passed_g, s["xt_pe"], 2, 0)
                g.tensor_scalar(rstd[:, :], mv[:, :, 1], EPS_LN, None, ALU.add).then_inc(pool, 1)
                b.wait_apart(g, passed_g, pool, 2, 1)
                g.tensor_tensor(rstd[:, :], rstd[:, :], half[:, 0:IT], ALU.pow).then_inc(pool, 1)
                b.wait_apart(g, passed_g, pool, 2, 2)
                for t in range(IT):
                    g.tensor_scalar(XN[:, t, :], X[b.slot][:, t, :], mv[:, t, 0:1], rstd[:, t:t + 1],
                                    ALU.subtract, ALU.mult).then_inc(s["xn"], 1)

            def rows(b):
                b.wait_apart(g, passed_g, s["parts"], 1, 1)
                b.wait_apart(g, passed_g, s["z"], ITEMS, (1 - SLOTS) * ITEMS)
                g.tensor_scalar(L[b.slot][:, :], parts[:, :], sel[:, 0:1], sel[:, 1:2], ALU.mult, ALU.add
                                ).then_inc(s["lr"], 1)
                for h in range(H):
                    g.tensor_scalar(R[b.slot][:, h, :], parts[:, :], sel[:, 2 + 2 * h:3 + 2 * h],
                                    sel[:, 3 + 2 * h:4 + 2 * h], ALU.mult, ALU.add).then_inc(s["lr"], 1)

            def bias_added(b):
                b.wait_apart(g, passed_g, s["h"], 2, 2)
                b.wait_apart(g, passed_g, s["pv"], ITEMS // HH, (1 - SLOTS) * (ITEMS // HH))
                g.tensor_tensor(HB[b.slot][:, :, :], HS[b.slot][:, :, :],
                                bias[:, :].unsqueeze(1).to_broadcast([P, IT, D]), ALU.add).then_inc(s["hb"], 1)

            heads = "p t (h e) -> p (t h) e"

            def layernorm(b):
                b.wait_apart(g, passed_g, s["out"], 1, 0)
                g.tensor_tensor(XB[:, :, :], X[b.slot][:, :, :],
                                beta[:, :].unsqueeze(1).to_broadcast([P, IT, D]), ALU.add).then_inc(pool2, 1)
                b.wait_apart(g, passed_g, s["sum"], 1, 1)
                g.tensor_scalar(sums[:, :], sums[:, :], 1.0 / E, None, ALU.mult).then_inc(pool2, 1)
                b.wait_apart(g, passed_g, pool2, 7, 2)
                Gv = G[:, :, :].rearrange(heads, h=H)
                g.tensor_tensor(Gv, Gv, bcast(sums[:, :], E), ALU.subtract).then_inc(s["d4"], 1)
                b.wait_apart(g, passed_g, s["ssq"], 1, 1)
                g.tensor_scalar(ssq[:, :], ssq[:, :], 1.0 / E, 1e-6, ALU.mult, ALU.add).then_inc(pool2, 1)
                b.wait_apart(g, passed_g, pool2, 7, 3)
                g.tensor_tensor(ssq[:, :], ssq[:, :], half[:, :], ALU.pow).then_inc(pool2, 1)
                b.wait_apart(g, passed_g, pool2, 7, 4)
                g.tensor_tensor(Gv, Gv, bcast(ssq[:, :], E), ALU.mult).then_inc(pool2, 1)
                b.wait_apart(g, passed_g, pool2, 7, 5)
                g.tensor_tensor(G[:, :, :], G[:, :, :], gamma[:, :].unsqueeze(1).to_broadcast([P, IT, D]),
                                ALU.mult).then_inc(pool2, 2)
                b.wait_apart(g, passed_g, pool2, 7, 7)
                b.dma_wait(g, stored, -1)
                g.tensor_tensor(XO[b.slot][:, :, :], G[:, :, :], XB[:, :, :], ALU.add).then_inc(s["out"], 1)

            pool2 = m.sem("pool2")

            def pre(b):
                normalised(b)
                if first:
                    bias_added(b)
                rows(b)

            def body(b):
                some = b.reg is not None
                if some or b.off < nb - 1:
                    pre(b + 1)
                if first and (some or b.off > 0):
                    layernorm(b + -1)

            pipeline(g, nb, pre, body, layernorm if first else lambda b: None)




def state_space_phase(nc, nb, x_in, w, consts, x_out):
    N, T = 512, 4
    DI, DS, NH, HD = 512, 64, 8, 64
    CT = DI // P
    EPS = 1e-5
    PAIRS = NH // 2
    PACK = [[(0, 0, 0, 512)], [(0, 1, 0, 384), (0, 3, 384, 128)], [(1, 0, 0, 512)],
            [(1, 1, 0, 384), (1, 3, 384, 128)], [(0, 2, 0, 256), (1, 2, 256, 256)]]
    GKIND = [0, 1, 0, 1, 2]
    NZ = len(PACK)
    ITEMS = PAIRS * NZ
    NM = 2 * NZ
    PROJ = ["dt", "bc"] + [("x", c) for c in range(CT)] + [("z", c) for c in range(CT)]
    NP = len(PROJ)
    with ExitStack() as ctx:
        m = Memory(nc, ctx, "ssm")
        ident = m.sb("ident", [P, P])
        ident_bf = m.sb("ident_bf", [P, P], BF16)
        causal = m.sb("causal", [P, P])
        causal_bf = m.sb("causal_bf", [P, P], BF16)
        sel = m.sb("sel", [P, 2 + 2 * NH])
        ones = m.sb("ones", [P, N])
        half = m.sb("half", [P, 16])
        W_in = m.sb("W_in", [P, KC, 2 * DI + 2 * DS])
        Wdt = m.sb("Wdt", [P, KC, P])
        W_out = m.sb("W_out", [P, CT, D])
        W_lin = m.sb("W_lin", [P, KC, D])
        WoT = m.sb("WoT", [P, KC, DI])
        Wc = m.sb("Wc", [P, CT, D])
        cw = m.sb("cw", [P, CT + 1, 4])
        cb = m.sb("cb", [P, CT + 1])
        skip = m.sb("skip", [P, CT])
        normw = m.sb("normw", [P, CT])
        dtb = m.sb("dtb", [P, 1])
        alog = m.sb("alog", [P, 1])
        aexp = m.sb("aexp", [P, 1])
        sign = m.sb("sign", [P, 1])
        blin = m.sb("blin", [P, D])
        X = [m.sb(f"X{k}", [P, T, D]) for k in range(2)]
        stats = m.sb("stats", [P, T, 6])
        mv = m.sb("mv", [P, T, 2])
        rstd = m.sb("rstd", [P, T])
        XN = m.sb("XN", [P, T, D])
        XT = m.sb("XT", [P, KC, N])
        sp_abs = m.sb("sp_abs", [P, N])
        sp_pos = m.sb("sp_pos", [P, N])
        DT = m.sb("DT", [P, N])
        dA = m.sb("dA", [P, N])
        AC = m.sb("AC", [P, N])
        parts = m.sb("parts", [P, N], BF16)
        rest = m.sb("rest", [P, N])
        dtt = m.sb("dtt", [P, T, NH])
        L = [m.sb(f"L{k}", [P, N], BF16) for k in range(2)]
        R = [m.sb(f"R{k}", [P, NH, N], BF16) for k in range(2)]
        CV = [m.sb(f"CV{k}", [P, N]) for k in range(2)]
        TH = [m.sb(f"TH{k}", [P, N]) for k in range(2)]
        BP = m.sb("BP", [P, N])
        CP = m.sb("CP", [P, N])
        XC = [m.sb(f"XC{k}", [P, CT, N]) for k in range(2)]
        ZS = [m.sb(f"ZS{k}", [P, CT, N]) for k in range(2)]
        XD = [m.sb(f"XD{k}", [P, T, DI]) for k in range(2)]
        G = [m.sb(f"G{k}", [P, 3, N]) for k in range(2)]
        EX = [m.sb(f"EX{k}", [P, N]) for k in range(2)]
        M = [m.sb(f"M{k}", [P, N]) for k in range(NM)]
        Y = m.sb("Y", [P, CT, N])
        SQ = [m.sb(f"SQ{k}", [P, N]) for k in range(2)]
        SS = m.sb("SS", [P, N])
        rms = m.sb("rms", [P, T])
        OUT = m.sb("OUT", [P, T, D])
        Zb = [m.ps(f"Z{k}") for k in range(2)]
        Yb = [m.ps(f"Y{k}") for k in range(2)]
        Jb = [m.ps(f"J{k}") for k in range(2)]
        Ab = [m.ps(f"A{k}") for k in range(2)]
        names = ("zero w setup_pe setup_v setup_a st mv rstd xn xt_pe xt pj conv tap th silu zs sp_a sp_b sp_c "
                 "spr dt dA ac s1 s2 s3 s4 parts dtt_pe dtt lr g_pe gr xd_pe xd z ex m y y1 y2 sq ss ss_pe ssr "
                 "rms1 rms o_pe o xb out stored").split()
        s = {n: m.sem(n) for n in names}
        x_loaded = [m.sem(f"x_loaded{k}") for k in range(2)]
        xv = x_in.rearrange("b (t p) d -> b p t d", p=P)
        ov = x_out.rearrange("b (t p) d -> b p t d", p=P)
        flat = "p t d -> p (t d)"
        TAPS = 3 * (CT + 1)

        def bank_read(b, eng, k):
            if k < 0:
                b.wait(eng, s["zs"], CT, k + 1)
            elif k == 0:
                b.wait(eng, s["spr"], 1, 1)
            elif k <= CT + 1:
                b.wait(eng, s["tap"], TAPS, 3 * k)
            else:
                b.wait(eng, s["zs"], CT, k - CT - 1)

        def tanh_read(b, eng, k):
            if k <= 0:
                b.wait(eng, s["zs"], CT, -1 if k == 0 else 0)
            elif k <= CT + 1:
                b.wait(eng, s["silu"], CT + 2, k + 1)
            else:
                b.wait(eng, s["zs"], CT, k - CT - 1)

        passed_v, passed_g, passed_pe = (m.sem(f"passed_{n}") for n in ("v", "g", "pe"))
        ctx.callback(m.clear)
        block = ctx.enter_context(nc.Block())

        @block.sync
        def _(sp):
            n = 0

            def put(dst, src, **kw):
                nonlocal n
                n += 1
                sp.dma_start(dst, src, **kw).then_inc(s["w"], 16)

            put(ident[:, :], consts["identity"])
            put(causal[:, :], consts["causal"])
            put(sel[:, :], consts["decay_selectors"])
            put(W_in[:, :, :], w["W_in"].rearrange("(c k) e -> k c e", k=P)[:, :, 0:2 * DI + 2 * DS])
            put(W_out[:, :, :], w["W_out"].rearrange("(c k) e -> k c e", k=P))
            put(W_lin[:, :, :], w["W_lin"].rearrange("(c k) e -> k c e", k=P))
            put(cw[:, :, :], w["conv_w"].rearrange("(c k) e -> k c e", k=P))
            put(cb[:, :], w["conv_b"].rearrange("(c k) -> k c", k=P), allow_slow_non_contiguous=True)
            put(normw[:, :], w["norm_w"].rearrange("(c k) -> k c", k=P), allow_slow_non_contiguous=True)
            put(blin[:, :], w["b_lin"].rearrange("(o d) -> o d", o=1).to_broadcast([P, D]))
            for h in range(2):
                put(skip[HD * h:HD * (h + 1), :],
                    w["D"].rearrange("(o c h) -> o c h", o=1, h=2)[:, :, h].to_broadcast([HD, CT]),
                    allow_slow_non_contiguous=True)
            sp.wait_ge(s["zero"], 4)
            wdt = w["W_in"].rearrange("(c k) e -> k c e", k=P)[:, :, 2 * DI + 2 * DS:]
            for q in (0, 64, 96):
                for r in (q, q + NH):
                    put(Wdt[:, :, r:r + NH], wdt)
                    put(dtb[r:r + NH, :], w["dt_bias"].rearrange("(h o) -> h o", o=1))
                    put(alog[r:r + NH, :], w["A_log"].rearrange("(h o) -> h o", o=1))
            assert n == N_W

            def load(b):
                b.wait(sp, s["out"], 1, -1)
                sp.dma_start(X[b.slot][:, :, :], xv[b.index()]).then_inc(x_loaded[b.slot], 16)

            def body(b):
                if b.reg is not None or b.off > 0:
                    store(b + -1)
                if b.reg is not None or b.off < nb - 1:
                    load(b + 1)

            def store(b):
                b.wait(sp, s["out"], 1, 1)
                sp.dma_start(ov[b.index()], OUT[:, :, :]).then_inc(s["stored"], 16)

            pipeline(sp, nb, load, body, store, 2)
            sp.wait_ge(s["stored"], 16 * nb)

        @block.tensor
        def _(pe):
            pe.wait_ge(s["w"], 16 * N_W)
            for kc in range(KC):
                for c in range(CT):
                    ins = pe.transpose(Zb[kc][:, c * P:(c + 1) * P], W_out[:, c, kc * P:(kc + 1) * P], ident[:, :])
            ins.then_inc(s["setup_pe"], 1)
            pe.wait_ge(s["setup_v"], 2)
            for c in range(CT):
                for kc in range(KC):
                    ins = pe.matmul(Jb[c // 2][:, (c % 2) * D:(c % 2 + 1) * D], WoT[:, kc, c * P:(c + 1) * P],
                                    W_lin[:, kc, :], start=(kc == 0), stop=(kc == KC - 1))
            ins.then_inc(s["setup_pe"], 1)
            pe.wait_ge(s["setup_v"], 8)

            def xn_turned(b):
                b.wait(pe, s["xn"], T, T)
                for kc in range(KC):
                    b.wait(pe, s["o"], 2, kc - 1 - 2)
                    for t in range(T):
                        ins = pe.transpose(Ab[1 - kc][:, t * P:(t + 1) * P], XN[:, t, kc * P:(kc + 1) * P],
                                           ident[:, :])
                    ins.then_inc(s["xt_pe"], 1)

            def project(b, k):
                if k == 0:
                    b.wait(pe, s["xt"], 2, 2)
                bank_read(b, pe, k - 2)
                what = PROJ[k]
                for kc in range(KC):
                    if what == "dt":
                        lhs = Wdt[:, kc, :]
                    else:
                        c = 2 * DI if what == "bc" else (DI if what[0] == "x" else 0) + what[1] * P
                        lhs = W_in[:, kc, c:c + P]
                    ins = pe.matmul(Jb[k % 2][:, :], lhs, XT[:, kc, :], start=(kc == 0), stop=(kc == KC - 1))
                ins.then_inc(s["pj"], 1)

            def dt_turned(b):
                b.wait(pe, s["dt"], 1, 1)
                b.wait_apart(pe, passed_pe, s["xt"], 2, 2)
                for t in range(T):
                    ins = pe.transpose(Ab[1][:, NH * t:NH * (t + 1)], DT[0:NH, t * P:(t + 1) * P],
                                       ident[0:NH, 0:NH])
                ins.then_inc(s["dtt_pe"], 1)

            def products(b):
                b.wait(pe, s["silu"], 6, 2)
                for g in range(3):
                    if g == 1:
                        b.wait(pe, s["dtt"], 1, 1)
                    if g == 2:
                        b.wait(pe, s["gr"], 4, 1)
                    for (_, t, c, n) in (PACK[0], PACK[1], PACK[4][0:1])[g]:
                        ins = pe.matmul(Ab[g % 2][:, c:c + n], BP[:, t * P:(t + 1) * P], CP[:, t * P:],
                                        start=True, stop=True, skip_group_check=True)
                    ins.then_inc(s["g_pe"], 1)

            def x_turned(b, t):
                b.wait(pe, s["silu"], 6, 6)
                if t < 2:
                    b.wait(pe, s["gr"], 4, 2 if t == 0 else 4)
                else:
                    b.wait(pe, s["xd"], T, t - 1)
                for c in range(CT):
                    ins = pe.transpose(Ab[1 - t % 2][:, c * P:(c + 1) * P], XC[b.slot][:, c, t * P:(t + 1) * P],
                                       ident[:, :])
                ins.then_inc(s["xd_pe"], 1)

            def exponents(b, n):
                q, i = n // NZ, n % NZ
                if n == 0:
                    b.wait(pe, s["lr"], NH + 1, NH + 1)
                b.wait(pe, s["ex"], ITEMS, n - 1)
                for (hh, t, c, cols) in PACK[i]:
                    pe.matmul(Zb[n % 2][:, c:c + cols], L[b.slot][:, t * P:(t + 1) * P],
                              R[b.slot][:, 2 * q + hh, t * P:], start=True, stop=False, skip_group_check=True)
                    ins = pe.matmul(Zb[n % 2][:, c:c + P], ident_bf[:, :], causal_bf[:, :],
                                    start=False, stop=True, skip_group_check=True)
                ins.then_inc(s["z"], 1)

            def outputs(b, q):
                b.wait(pe, s["m"], ITEMS, NZ * (q + 1))
                b.wait(pe, s["y1"], PAIRS, q - 1)
                if q == 0:
                    b.wait(pe, s["xd"], T, T)
                where = {(hh, t): (i, c, cols) for i, p in enumerate(PACK) for (hh, t, c, cols) in p}
                for t in range(T):
                    for hh in range(2):
                        i, c, cols = where[hh, t]
                        h = 2 * q + hh
                        ins = pe.matmul(Yb[q % 2][HD * hh:HD * (hh + 1), t * P:], XD[b.slot][:, t, HD * h:HD * (h + 1)],
                                        M[(NZ * q + i) % NM][:, c:c + cols], start=(t == 0), stop=(t == T - 1),
                                        skip_group_check=True)
                ins.then_inc(s["y"], 1)

            def sums(b, newest):
                b.wait(pe, s["ss"], PAIRS - 1, PAIRS - 1)
                newest.wait(pe, s["xd"], T, T)
                for t in range(T):
                    ins = pe.matmul(Ab[0][:, t:t + 1], SS[:, t * P:(t + 1) * P], ones[:, 0:1], start=True, stop=True)
                ins.then_inc(s["ss_pe"], 1)

            def result(b):
                for g in range(2):
                    if g == 1:
                        b.wait(pe, s["ssr"], 1, 1)
                    for t in (2 * g, 2 * g + 1):
                        for c in range(CT):
                            ins = pe.matmul(Ab[1 - g][:, (t % 2) * D:(t % 2 + 1) * D], Y[:, c, t * P:(t + 1) * P],
                                            Wc[:, c, :], start=(c == 0), stop=(c == CT - 1))
                    ins.then_inc(s["o_pe"], 1)

            def pre(b):
                xn_turned(b)
                for k in range(NP):
                    project(b, k)
                    if k == 1:
                        dt_turned(b)
                products(b)
                for t in range(T):
                    x_turned(b, t)

            def body(b):
                some = b.reg is not None
                nxt, prev = some or b.off < nb - 1, some or b.off > 0
                for n in range(ITEMS + LAG_Y + 1):
                    if n < ITEMS:
                        exponents(b, n)
                    if n == 0 and prev:
                        sums(b + -1, b)
                        result(b + -1)
                    if nxt:
                        if n == 3:
                            xn_turned(b + 1)
                        if 4 <= n < 4 + NP:
                            project(b + 1, n - 4)
                        if n == 6:
                            dt_turned(b + 1)
                        if n == 9:
                            products(b + 1)
                        if 15 <= n < 19:
                            x_turned(b + 1, n - 15)
                    if n >= LAG_Y and (n - LAG_Y) % NZ == NZ - 1:
                        outputs(b, (n - LAG_Y) // NZ)

            def after(b):
                sums(b, b)
                result(b)

            pipeline(pe, nb, pre, body, after, 2)

        @block.scalar
        def _(act):
            act.wait_ge(s["w"], 16 * N_W)
            act.activation(aexp[:, :], alog[:, :], ACT.Exp).then_inc(s["setup_a"], 1)
            act.wait_ge(s["setup_v"], 8)

            def xt_out(b):
                b.wait(act, s["pj"], NP, 0)
                for kc in range(KC):
                    b.wait(act, s["xt_pe"], 2, kc + 1)
                    act.activation(XT[:, kc, :], Ab[1 - kc][:, :], ACT.Copy).then_inc(s["xt"], 1)

            def softplus(b):
                b.wait(act, s["pj"], NP, 1)
                b.wait(act, s["dt"], 1, 0)
                act.activation(sp_abs[:, :], Jb[0][:, :], ACT.Abs, bias=dtb[:, :]).then_inc(s["sp_a"], 1)
                b.wait(act, s["sp_a"], 1, 1)
                act.activation(sp_abs[:, :], sp_abs[:, :], ACT.Exp, scale=-1.0).then_inc(s["sp_b"], 1)
                b.wait(act, s["sp_b"], 1, 1)
                act.activation(sp_abs[:, :], sp_abs[:, :], ACT.Ln, bias=1.0).then_inc(s["sp_c"], 1)

            def conv_first(b, k):
                c = CT if k == 1 else k - 2
                b.wait(act, s["pj"], NP, k + 1)
                b.wait(act, s["silu"], CT + 2, 0 if k == 1 else k - 1 if k > 2 else -1)
                act.activation(CV[k % 2][:, :], Jb[k % 2][:, :], ACT.Identity, scale=cw[:, c, 3:4],
                               bias=cb[:, c:c + 1]).then_inc(s["conv"], 1)

            def tanh_conv(b, k):
                b.wait(act, s["tap"], TAPS, 3 * k)
                tanh_read(b, act, k - 2 if k != 1 else -1)
                act.activation(TH[k % 2][:, :], CV[k % 2][:, :], ACT.Tanh, scale=0.5).then_inc(s["th"], 1)

            def tanh_z(b, k):
                b.wait(act, s["pj"], NP, k + 1)
                tanh_read(b, act, k - 2)
                act.activation(TH[k % 2][:, :], Jb[k % 2][:, :], ACT.Tanh, scale=0.5).then_inc(s["th"], 1)

            def products_out(b):
                for g in range(3):
                    b.wait(act, s["g_pe"], 3, g + 1)
                    for c in ((0, N),) if g < 2 else ((0, N // 2), (N // 2, N)):
                        n = c[1] - c[0]
                        act.activation(G[b.slot][:, g, c[0]:c[1]], Ab[g % 2][:, 0:n], ACT.Copy,
                                       scale=0.125).then_inc(s["gr"], 1)

            def decay(b, n):
                b.wait(act, s["z"], ITEMS, n + 1)
                b.wait(act, s["m"], ITEMS, n - 1)
                act.activation(EX[n % 2][:, :], Zb[n % 2][:, :], ACT.Exp).then_inc(s["ex"], 1)

            def square(b, q):
                b.wait(act, s["y2"], PAIRS, q + 1)
                b.wait(act, s["ss"], PAIRS - 1, max(q - 2, 0) if q else -1)
                act.activation((SS if q == 0 else SQ[q % 2])[:, :], Y[:, q, :], ACT.Square).then_inc(s["sq"], 1)

            def result_out(b):
                b.wait(act, s["rms"], 1, 1)
                b.wait(act, s["stored"], 16, 0)
                for t in range(T):
                    g = t // 2
                    b.wait(act, s["o_pe"], 2, g + 1)
                    ins = act.activation(OUT[:, t, :], Ab[1 - g][:, (t % 2) * D:(t % 2 + 1) * D], ACT.Copy,
                                         scale=rms[:, t:t + 1])
                    if t % 2:
                        ins.then_inc(s["o"], 1)

            def pre(b):
                xt_out(b)
                softplus(b)
                for k in range(1, NP):
                    if k <= CT + 1:
                        conv_first(b, k)
                        tanh_conv(b, k)
                    else:
                        tanh_z(b, k)
                products_out(b)

            def body(b):
                some = b.reg is not None
                nxt, prev = some or b.off < nb - 1, some or b.off > 0
                for n in range(ITEMS + LAG_Q + 1):
                    if n < ITEMS:
                        decay(b, n)
                    if n == 1 and prev:
                        result_out(b + -1)
                    if nxt:
                        if n == 3:
                            xt_out(b + 1)
                        if n == 4:
                            softplus(b + 1)
                        k = n - 4
                        if 1 <= k <= CT + 1:
                            conv_first(b + 1, k)
                        if 1 <= k - 1 <= CT + 1:
                            tanh_conv(b + 1, k - 1)
                        if CT + 1 < k < NP:
                            tanh_z(b + 1, k)
                        if n == 9:
                            products_out(b + 1)
                    if n >= LAG_Q and (n - LAG_Q) % NZ == NZ - 1:
                        square(b, (n - LAG_Q) // NZ)

            pipeline(act, nb, pre, body, result_out, 2)

        @block.vector
        def _(v):
            v.memset(Wdt[:, :, :], 0.0).then_inc(s["zero"], 1)
            v.memset(dtb[:, :], 0.0).then_inc(s["zero"], 1)
            v.memset(alog[:, :], 0.0).then_inc(s["zero"], 1)
            v.memset(BP[:, :], 0.0).then_inc(s["zero"], 1)
            v.memset(CP[:, :], 0.0)
            v.memset(ones[:, :], 1.0)
            v.memset(half[:, :], -0.5)
            v.wait_ge(s["setup_pe"], 1)
            for kc in range(KC):
                v.tensor_copy(WoT[:, kc, :], Zb[kc][:, :]).then_inc(s["setup_v"], 1)
            v.wait_ge(s["w"], 16 * N_W)
            v.tensor_copy(ident_bf[:, :], ident[:, :]).then_inc(s["setup_v"], 1)
            v.tensor_copy(causal_bf[:, :], causal[:, :]).then_inc(s["setup_v"], 1)
            v.tensor_scalar(skip[:, :], skip[:, :], 0.5, None, ALU.mult).then_inc(s["setup_v"], 1)
            v.wait_ge(s["setup_a"], 1)
            v.tensor_scalar(sign[:, :], sel[:, 0:1], 1.0, sel[:, 1:2], ALU.mult, ALU.subtract
                            ).then_inc(s["setup_v"], 1)
            v.wait_ge(s["setup_v"], 6)
            v.tensor_tensor(aexp[:, :], aexp[:, :], sign[:, :], ALU.mult).then_inc(s["setup_v"], 1)
            v.wait_ge(s["setup_pe"], 2)
            for c in range(CT):
                ins = v.tensor_scalar(Wc[:, c, :], Jb[c // 2][:, (c % 2) * D:(c % 2 + 1) * D], normw[:, c:c + 1],
                                      None, ALU.mult)
            ins.then_inc(s["setup_v"], 1)
            v.wait_ge(s["setup_v"], 8)

            def norm_stats(b):
                b.dma_wait(v, x_loaded)
                b.wait(v, s["xn"], T, 0)
                for t in range(T):
                    ins = v.bn_stats(stats[:, t, :], X[b.slot][:, t, :])
                ins.then_inc(s["st"], 1)
                b.wait_apart(v, passed_v, s["st"], 1, 1)
                for t in range(T):
                    ins = v.bn_aggr(mv[:, t, :], stats[:, t, :])
                ins.then_inc(s["mv"], 1)

            def steps(b):
                b.wait(v, s["sp_c"], 1, 1)
                b.wait(v, s["dtt_pe"], 1, 0)
                v.tensor_scalar(sp_pos[:, :], Jb[0][:, :], dtb[:, 0:1], 0.0, ALU.add, ALU.max).then_inc(s["spr"], 1)
                b.wait(v, s["spr"], 1, 1)
                v.tensor_tensor(DT[:, :], sp_pos[:, :], sp_abs[:, :], ALU.add).then_inc(s["dt"], 1)
                b.wait(v, s["dt"], 1, 1)
                v.tensor_scalar(dA[:, :], DT[:, :], aexp[:, 0:1], None, ALU.mult).then_inc(s["dA"], 1)
                b.wait(v, s["dA"], 1, 1)
                v.tensor_tensor_scan(AC[:, :], ones[:, :], dA[:, :], 0.0, ALU.mult, ALU.add).then_inc(s["ac"], 1)
                b.wait(v, s["ac"], 1, 1)
                b.wait(v, s["lr"], NH + 1, 0)
                v.tensor_copy(parts[:, :], AC[:, :]).then_inc(s["s1"], 1)
                b.wait(v, s["s1"], 1, 1)
                v.tensor_tensor(rest[64:P, :], AC[64:P, :], parts[64:P, :], ALU.subtract).then_inc(s["s2"], 1)
                b.wait(v, s["s2"], 1, 1)
                v.tensor_copy(parts[64:P, :], rest[64:P, :]).then_inc(s["s3"], 1)
                b.wait(v, s["s3"], 1, 1)
                v.tensor_tensor(rest[96:P, :], rest[96:P, :], parts[96:P, :], ALU.subtract).then_inc(s["s4"], 1)
                b.wait(v, s["s4"], 1, 1)
                v.tensor_copy(parts[96:P, :], rest[96:P, :]).then_inc(s["parts"], 1)

            def dt_out(b):
                b.wait(v, s["dtt_pe"], 1, 1)
                b.wait(v, s["xd"], T, 0)
                v.tensor_copy(dtt[:, :, :].rearrange("p t h -> p (t h)"), Ab[1][:, 0:T * NH]).then_inc(s["dtt"], 1)

            def taps(b, k):
                c = CT if k == 1 else k - 2
                b.wait(v, s["conv"], CT + 1, k)
                for j in range(1, 4):
                    b.wait(v, s["tap"], TAPS, 3 * (k - 1) + j - 1)
                    v.scalar_tensor_tensor(out=CV[k % 2][:, j:], in0=Jb[k % 2][:, 0:N - j], scalar=cw[:, c, 3 - j:4 - j],
                                           in1=CV[k % 2][:, j:], op0=ALU.mult, op1=ALU.add).then_inc(s["tap"], 1)

            def silu_conv(b, k):
                b.wait(v, s["th"], NP - 1, k)
                if k == 1:
                    b.wait(v, s["g_pe"], 3, 0)
                    for r, dst in ((0, BP), (64, CP)):
                        ins = v.scalar_tensor_tensor(out=dst[0:64, :], in0=TH[1][r:r + 64, :], scalar=1.0,
                                                     in1=CV[1][r:r + 64, :], op0=ALU.add, op1=ALU.mult)
                        ins.then_inc(s["silu"], 1)
                    v.wait_ge(s["zero"], 4)
                else:
                    b.wait(v, s["y1"], PAIRS, -PAIRS)
                    ins = v.scalar_tensor_tensor(out=XC[b.slot][:, k - 2, :], in0=TH[k % 2][:, :], scalar=1.0,
                                                 in1=CV[k % 2][:, :], op0=ALU.add, op1=ALU.mult)
                    ins.then_inc(s["silu"], 1)

            def silu_z(b, k):
                b.wait(v, s["th"], NP - 1, k)
                b.wait(v, s["y2"], PAIRS, -PAIRS)
                v.scalar_tensor_tensor(out=ZS[b.slot][:, k - CT - 2, :], in0=TH[k % 2][:, :], scalar=1.0,
                                       in1=Jb[k % 2][:, :], op0=ALU.add, op1=ALU.mult).then_inc(s["zs"], 1)

            def x_dt(b, t):
                b.wait(v, s["xd_pe"], T, t + 1)
                b.wait(v, s["dtt"], 1, 1)
                b.wait(v, s["y"], PAIRS, -PAIRS)
                v.tensor_tensor(XD[b.slot][:, t, :].rearrange("p (h e) -> p h e", h=NH),
                                Ab[1 - t % 2][:, :].rearrange("p (h e) -> p h e", h=NH), bcast(dtt[:, t, :], HD),
                                ALU.mult).then_inc(s["xd"], 1)

            def decayed(b, n):
                q, i = n // NZ, n % NZ
                b.wait(v, s["ex"], ITEMS, n + 1)
                if n == 0:
                    b.wait(v, s["gr"], 4, 4)
                b.wait(v, s["y"], PAIRS, q - 1)
                v.tensor_tensor(M[n % NM][:, :], EX[n % 2][:, :], G[b.slot][:, GKIND[i], :], ALU.mult
                                ).then_inc(s["m"], 1)

            def gated(b, q):
                b.wait(v, s["y"], PAIRS, q + 1)
                if q == 0:
                    b.wait(v, s["o_pe"], 2, 0)
                v.scalar_tensor_tensor(out=Y[:, q, :], in0=XC[b.slot][:, q, :], scalar=skip[:, q:q + 1],
                                       in1=Yb[q % 2][:, :], op0=ALU.mult, op1=ALU.add).then_inc(s["y1"], 1)
                b.wait(v, s["y1"], PAIRS, q + 1)
                v.tensor_tensor(Y[:, q, :], Y[:, q, :], ZS[b.slot][:, q, :], ALU.mult).then_inc(s["y2"], 1)

            def mean_square(b):
                b.wait(v, s["ss_pe"], 1, 1)
                b.wait(v, s["o"], 2, 0)
                v.tensor_scalar(rms[:, :], Ab[0][:, 0:T], 0.25 / DI, EPS, ALU.mult, ALU.add).then_inc(s["ssr"], 1)

            def pre(b):
                norm_stats(b)
                for k in range(NP):
                    if k == 0:
                        steps(b)
                    elif k <= CT + 1:
                        taps(b, k)
                        silu_conv(b, k)
                    else:
                        silu_z(b, k)
                    if k == 1:
                        dt_out(b)
                for t in range(T):
                    x_dt(b, t)

            def body(b):
                some = b.reg is not None
                nxt, prev = some or b.off < nb - 1, some or b.off > 0
                for n in range(ITEMS + LAG_V + 1):
                    if n < ITEMS:
                        decayed(b, n)
                    if n == 0 and prev:
                        mean_square(b + -1)
                    if nxt:
                        if n == 1:
                            norm_stats(b + 1)
                        k = n - 5
                        if k == 0:
                            steps(b + 1)
                        if 1 <= k <= CT + 1:
                            taps(b + 1, k)
                        if k == 1:
                            dt_out(b + 1)
                        if 1 <= k - 1 <= CT + 1:
                            silu_conv(b + 1, k - 1)
                        if CT + 1 < k - 1 < NP:
                            silu_z(b + 1, k - 1)
                        if 16 <= n < 20:
                            x_dt(b + 1, n - 16)
                    if n >= LAG_V and (n - LAG_V) % NZ == NZ - 1:
                        gated(b, (n - LAG_V) // NZ)

            pipeline(v, nb, pre, body, mean_square, 2)

        @block.gpsimd
        def _(g):
            g.wait_ge(s["setup_v"], 8)

            def normalised(b):
                b.wait_apart(g, passed_g, s["mv"], 1, 1)
                b.wait_apart(g, passed_g, s["xt_pe"], 2, 0)
                g.tensor_scalar(rstd[:, :], mv[:, :, 1], EPS_LN, None, ALU.add).then_inc(s["rstd"], 1)
                b.wait_apart(g, passed_g, s["rstd"], 2, 1)
                g.tensor_tensor(rstd[:, :], rstd[:, :], half[:, 0:T], ALU.pow).then_inc(s["rstd"], 1)
                b.wait_apart(g, passed_g, s["rstd"], 2, 2)
                for t in range(T):
                    g.tensor_scalar(XN[:, t, :], X[b.slot][:, t, :], mv[:, t, 0:1], rstd[:, t:t + 1],
                                    ALU.subtract, ALU.mult).then_inc(s["xn"], 1)

            def rows(b):
                b.wait_apart(g, passed_g, s["parts"], 1, 1)
                b.wait_apart(g, passed_g, s["z"], ITEMS, -ITEMS)
                g.tensor_scalar(L[b.slot][:, :], parts[:, :], sel[:, 0:1], sel[:, 1:2], ALU.mult, ALU.add
                                ).then_inc(s["lr"], 1)
                for h in range(NH):
                    g.tensor_scalar(R[b.slot][:, h, :], parts[:, :], sel[:, 2 + 2 * h:3 + 2 * h],
                                    sel[:, 3 + 2 * h:4 + 2 * h], ALU.mult, ALU.add).then_inc(s["lr"], 1)

            def squares(b, q):
                b.wait_apart(g, passed_g, s["sq"], PAIRS, q + 1)
                b.wait_apart(g, passed_g, s["ss"], PAIRS - 1, q - 1)
                g.tensor_tensor(SS[:, :], SS[:, :], SQ[q % 2][:, :], ALU.add).then_inc(s["ss"], 1)

            def finish(b):
                b.wait_apart(g, passed_g, s["ssr"], 1, 1)
                g.tensor_tensor(rms[:, :], rms[:, :], half[:, 0:T], ALU.pow).then_inc(s["rms1"], 1)
                b.wait_apart(g, passed_g, s["rms1"], 1, 1)
                g.tensor_scalar(rms[:, :], rms[:, :], 0.5, None, ALU.mult).then_inc(s["rms"], 1)
                g.tensor_tensor(X[b.slot][:, :, :], X[b.slot][:, :, :], blin[:, :].unsqueeze(1).to_broadcast([P, T, D]),
                                ALU.add).then_inc(s["xb"], 1)
                b.wait_apart(g, passed_g, s["xb"], 1, 1)
                b.wait_apart(g, passed_g, s["o"], 2, 2)
                g.tensor_tensor(OUT[:, :, :], OUT[:, :, :], X[b.slot][:, :, :], ALU.add).then_inc(s["out"], 1)

            def pre(b):
                normalised(b)
                rows(b)

            def body(b):
                some = b.reg is not None
                nxt, prev = some or b.off < nb - 1, some or b.off > 0
                if prev:
                    finish(b + -1)
                if nxt:
                    normalised(b + 1)
                squares(b, 1)
                if nxt:
                    rows(b + 1)
                squares(b, 2)
                squares(b, 3)

            pipeline(g, nb, pre, body, finish, 2)


N_W = 12 + 3 * 2 * 3
LAG_Y, LAG_Q, LAG_V = 1, 3, 2


def lstm_phase(nc, x_in, w, consts, x_out):
    B, NT, S, J, HB = 32, 512, 16, 4, 64
    CH = NT // S
    TILES = B * S // P
    BT = P // S
    GATES = (0, 1, 3, 2)
    with ExitStack() as ctx:
        m = Memory(nc, ctx, "lstm")
        ident = m.sb("ident", [P, P])
        rep = m.sb("rep", [P, P])
        rep_bf = m.sb("rep_bf", [P, P], BF16)
        ones_bf = m.sb("ones_bf", [P, B], BF16)
        half = m.sb("half", [P, 16])
        Wih = m.sb("Wih", [P, KC, J, 4 * HB])
        Whh = m.sb("Whh", [P, KC, J, 4 * HB])
        bias = m.sb("bias", [P, J * 4 * HB], BF16)
        wl = m.sb("wl", [P, KC, 2])
        bl = m.sb("bl", [B, 2])
        fw = m.sb("fw", [P, HB])
        bw = m.sb("bw", [P, HB])
        cinc = m.sb("cinc", [P, HB])
        cown = m.sb("cown", [P, HB])
        U = m.sb("U", [P, NT, HB])
        raw = m.sb("raw", [P, TILES, D])
        XN = m.sb("XN", [P, TILES, D])
        stats = m.sb("stats", [P, TILES, 6])
        mv = m.sb("mv", [P, TILES, 2])
        rstd = m.sb("rstd", [P, TILES])
        XT = [m.sb(f"XT{k}", [P, KC, B, S]) for k in range(2)]
        H = [m.sb(f"H{k}", [P, S, HB]) for k in range(2)]
        TC = [m.sb(f"TC{k}", [P, 5, HB]) for k in range(2)]
        AB = m.sb("AB", [P, 2, HB])
        tc = m.sb("tc", [P, HB])
        HT = [m.sb(f"HT{k}", [P, HB]) for k in range(2)]
        lg = m.sb("lg", [B, S, 2])
        gate = m.sb("gate", [P, S], BF16)
        gS = m.sb("gS", [P, S])
        own = m.sb("own", [P, S, HB])
        inc = m.sb("inc", [P, S + 1, HB])
        Gb = [m.ps(f"G{k}") for k in range(2)]
        XTb = [m.ps(f"XT{k}") for k in range(2)]
        LGb = [m.ps(f"LG{k}") for k in range(2)]
        REPb = m.ps("REP")
        names = ("w setup_v setup_pe wready zero raw_in st mv rstd xn xt_pe xt g tg ab c2 tc h ht lgp lg gate repp gs "
                 "own inc a u done tot bias1 bias2 fin outs").split()
        s = {n: m.sem(n) for n in names}
        resid = [m.sem(f"resid{k}") for k in range(2)]
        xv = x_in.rearrange("b (c t) d -> c b t d", t=S)
        passed_v, passed_g, passed_pe = (m.sem(f"passed_{n}") for n in ("v", "g", "pe"))
        ctx.callback(m.clear)
        block = ctx.enter_context(nc.Block())

        flatU = U[:, :, :].rearrange("p t e -> p (t e)")
        nat_ih = flatU[:, 0:8 * D].rearrange("p (r k) -> p r k", k=D)
        nat_hh = flatU[:, 8 * D:16 * D].rearrange("p (r k) -> p r k", k=D)
        b1 = flatU[:, 16 * D:20 * D]
        b2 = flatU[:, 20 * D:24 * D]
        b3 = flatU[:, 24 * D:28 * D]
        b4 = flatU[:, 28 * D:30 * D].bitcast(BF16)

        @block.sync
        def _(sp):
            n = 0

            def put(dst, src, **kw):
                nonlocal n
                n += 1
                sp.dma_start(dst, src, **kw).then_inc(s["w"], 16)

            put(ident[:, :], consts["identity"])
            put(rep[:, :], consts["repeat"])
            put(nat_ih, w["W_ih"].rearrange("(r p) k -> p r k", p=P))
            for c in range(KC):
                for j in range(J):
                    k = HB * j + 32 * c
                    put(nat_hh[:, :, P * c + 32 * j:P * c + 32 * (j + 1)],
                        w["W_hh"].rearrange("(r p) k -> p r k", p=P)[:, :, k:k + 32])
            put(b1, w["b_ih"].rearrange("(o g) -> o g", o=1).to_broadcast([P, 4 * D]))
            put(b2, w["b_hh"].rearrange("(o g) -> o g", o=1).to_broadcast([P, 4 * D]))
            put(bl[:, :], w["b_lin"].rearrange("(o l) -> o l", o=1).to_broadcast([B, 2]))
            for c in range(KC):
                for l in range(2):
                    src = w["W_lin"][l, :].rearrange("(j c p o) -> c j p o", j=J, c=KC, o=1)[c]
                    for j in range(J):
                        sp.dma_start(wl[32 * j:32 * (j + 1), c, l:l + 1], src[j]).then_inc(s["zero"], 16)
            for j in range(J):
                put(fw[32 * j:32 * (j + 1), :], w["fw_att"][:, HB * j:HB * (j + 1)].to_broadcast([B, HB]))
                put(bw[32 * j:32 * (j + 1), :], w["bw_att"][:, HB * j:HB * (j + 1)].to_broadcast([B, HB]))
            assert n == N_PUT
            sp.wait_ge(s["setup_v"], 1)

            def load(c):
                c.wait(sp, s["xn"], TILES, 0)
                for k in range(TILES):
                    for b in range(BT):
                        sp.dma_start(raw[S * b:S * (b + 1), k, :], xv[c.index()][BT * k + b]
                                     ).then_inc(s["raw_in"], 16)

            def residual(c):
                c.wait(sp, s["done"], 1, -1)
                for j in range(J):
                    sp.dma_start(U[32 * j:32 * (j + 1), bass.ds(c.index() * S, S), :],
                                 xv[c.index()][:, :, HB * j:HB * (j + 1)]).then_inc(resid[c.slot], 16)

            def body(c):
                if c.reg is not None or c.off < CH - 1:
                    load(c + 1)
                residual(c)

            pipeline(sp, CH, load, body, lambda c: None, 2)

            def store(c):
                (c + 1).wait(sp, s["fin"], 1, 0)
                for j in range(J):
                    sp.dma_start(x_out.rearrange("b (c t) d -> c b t d", t=S)[c.index()][:, :, HB * j:HB * (j + 1)],
                                 U[32 * j:32 * (j + 1), bass.ds(c.index() * S, S), :]).then_inc(s["outs"], 16)

            with sp.Fori(0, CH) as i:
                store(Batch(i, 0, 1))
            sp.wait_ge(s["outs"], 16 * J * CH)

        @block.tensor
        def _(pe):
            pe.wait_ge(s["w"], 16 * N_PUT)
            n = 0
            for nat in (nat_ih, nat_hh):
                for c in range(KC):
                    for r0 in range(0, 8, 4):
                        pe.wait_ge(s["wready"], 4 * max(n - 1, 0))
                        for r in range(r0, r0 + 4):
                            ins = pe.transpose(XTb[n % 2][:, (r % 4) * P:(r % 4 + 1) * P],
                                               nat[:, r, c * P:(c + 1) * P], ident[:, :])
                        ins.then_inc(s["setup_pe"], 1)
                        n += 1
            pe.wait_ge(s["setup_v"], 1)
            pe.wait_ge(s["wready"], 4 * n)

            def turned(c):
                c.wait(pe, s["xn"], TILES, TILES)
                for kc in range(KC):
                    c.wait(pe, s["xt"], KC, kc - 1)
                    for k in range(TILES):
                        ins = pe.transpose(XTb[kc][:, k * P:(k + 1) * P], XN[:, k, kc * P:(kc + 1) * P], ident[:, :])
                    ins.then_inc(s["xt_pe"], 1)

            def inputs(c, t):
                if t == 0:
                    c.wait(pe, s["xt"], KC, KC)
                c.wait(pe, s["tg"], S, t - 1)
                bank = Gb[t % 2]
                for j in range(J):
                    pe.matmul(bank[32 * j:32 * (j + 1), 0:4 * HB], ones_bf[:, :], bias[:, 4 * HB * j:4 * HB * (j + 1)],
                              start=True, stop=False, skip_group_check=True)
                for kc in range(KC):
                    for j in range(J):
                        pe.matmul(bank[32 * j:32 * (j + 1), 0:4 * HB], XT[c.slot][:, kc, :, t], Wih[:, kc, j, :],
                                  start=False, stop=False, skip_group_check=True)

            def hidden(c, t):
                c.wait(pe, s["ht"], S, t + 1)
                for kc in range(KC):
                    for j in range(J):
                        ins = pe.matmul(Gb[t % 2][32 * j:32 * (j + 1), 0:4 * HB], HT[t % 2][:, 32 * kc:32 * (kc + 1)],
                                        Whh[:, kc, j, :], start=False, stop=(kc == KC - 1), skip_group_check=True)
                ins.then_inc(s["g"], 1)

            def logit(c, t, turned_h):
                for kc in range(KC):
                    ins = pe.matmul(LGb[c.slot][0:B, 2 * t:2 * t + 2], turned_h[:, 32 * kc:32 * (kc + 1)], wl[:, kc, :],
                                    start=(kc == 0), stop=(kc == KC - 1), skip_group_check=True)
                ins.then_inc(s["lgp"], 1)

            def repeat_gate(c):
                c.wait(pe, s["gate"], 1, 1)
                c.wait(pe, s["gs"], 1, 0)
                pe.matmul(REPb[:, 0:S], rep_bf[:, :], gate[:, :], start=True, stop=True).then_inc(s["repp"], 1)

            def before(c):
                turned(c)
                inputs(c, 0)

            def body(c):
                some = c.reg is not None
                nxt, prev = some or c.off < CH - 1, some or c.off > 0
                for t in range(S):
                    hidden(c, t)
                    if t < S - 1:
                        inputs(c, t + 1)
                    elif nxt:
                        inputs(c + 1, 0)
                    if t > 0:
                        logit(c, t - 1, HT[t % 2])
                    elif prev:
                        logit(c + -1, S - 1, HT[0])
                    if prev and t == 2:
                        repeat_gate(c + -1)
                    if nxt and t == 11:
                        turned(c + 1)

            def after(c):
                c.wait(pe, s["ht"], S, S + 1)
                logit(c, S - 1, HT[0])
                repeat_gate(c)

            pipeline(pe, CH, before, body, after, 2)

        @block.scalar
        def _(act):
            def evacuate(c, kc):
                c.wait(act, s["xt_pe"], KC, kc + 1)
                c.wait(act, s["g"], S, -S)
                act.activation(XT[c.slot][:, kc, :, :].rearrange("p b t -> p (b t)"), XTb[kc][:, :], ACT.Copy
                               ).then_inc(s["xt"], 1)

            def gates(c, t):
                c.wait(act, s["g"], S, t + 1)
                c.wait(act, s["h"], S, t - 1)
                act.activation(TC[t % 2][:, 0:4, :].rearrange("p g e -> p (g e)"), Gb[t % 2][:, 0:4 * HB], ACT.Tanh
                               ).then_inc(s["tg"], 1)

            def cell(c, t):
                c.wait(act, s["c2"], S, t + 1)
                act.activation(tc[:, :], TC[(t + 1) % 2][:, 4, :], ACT.Tanh, scale=0.5).then_inc(s["tc"], 1)

            def before(c):
                act.wait_ge(s["wready"], 32)
                evacuate(c, 0)
                evacuate(c, 1)

            def body(c):
                nxt = c.reg is not None or c.off < CH - 1
                for t in range(S):
                    gates(c, t)
                    cell(c, t)
                    if nxt and t in (12, 13):
                        evacuate(c + 1, t - 12)

            pipeline(act, CH, before, body, lambda c: None, 2)

        @block.vector
        def _(v):
            v.memset(ones_bf[:, :], 1.0)
            v.memset(half[:, :], -0.5)
            v.memset(bias[:, :], 0.0)
            v.memset(gate[:, :], 0.0)
            v.memset(TC[0][:, 4, :], 0.0)
            v.memset(inc[:, S, :], 0.0).then_inc(s["tot"], 1)
            n = 0
            for which in range(2):
                W = (Wih, Whh)[which]
                for c in range(KC):
                    for r0 in range(0, 8, 4):
                        v.wait_ge(s["setup_pe"], n + 1)
                        for r in range(r0, r0 + 4):
                            g = GATES[r // 2]
                            scale = (1.0 if g == 3 else 0.5) * (0.5 if which else 1.0)
                            v.tensor_scalar(W[:, c, 2 * (r % 2):2 * (r % 2) + 2, g * HB:(g + 1) * HB],
                                            XTb[n % 2][:, (r % 4) * P:(r % 4 + 1) * P].rearrange("p (j e) -> p j e", j=2),
                                            scale, None, ALU.mult).then_inc(s["wready"], 1)
                        n += 1
            v.wait_ge(s["w"], 16 * N_PUT)
            v.tensor_copy(rep_bf[:, :], rep[:, :])
            v.tensor_tensor(b3, b1, b2, ALU.add).then_inc(s["bias1"], 1)
            v.wait_ge(s["bias1"], 1)
            for r in range(4):
                g = GATES[r]
                v.tensor_scalar(b1.rearrange("p (j g e) -> p j g e", j=J, g=4)[:, :, g],
                                b3[:, r * D:(r + 1) * D].rearrange("p (j e) -> p j e", j=J),
                                1.0 if g == 3 else 0.5, None, ALU.mult).then_inc(s["bias1"], 1)
            v.wait_ge(s["bias1"], 5)
            for k, q in enumerate((0, 64, 96)):
                v.tensor_copy(b4, b1).then_inc(s["bias2"], 1)
                v.wait_ge(s["bias2"], 3 * k + 1)
                v.tensor_copy(bias[q:q + 1, :], b4[q:q + 1, :]).then_inc(s["bias2"], 1)
                v.tensor_tensor(b1, b1, b4, ALU.subtract).then_inc(s["bias2"], 1)
                v.wait_ge(s["bias2"], 3 * k + 3)
            v.tensor_tensor(cinc[:, :], fw[:, :], bw[:, :], ALU.subtract).then_inc(s["bias1"], 1)
            v.tensor_scalar(cown[:, :], fw[:, :], -0.5, None, ALU.mult)
            v.tensor_scalar(bw[:, :], bw[:, :], 0.5, None, ALU.mult)
            v.wait_ge(s["zero"], 16 * 2 * KC * J)
            v.tensor_scalar(wl[:, :, :], wl[:, :, :], 0.5, None, ALU.mult)
            v.wait_ge(s["bias1"], 6)
            v.tensor_scalar(cinc[:, :], cinc[:, :], 0.5, None, ALU.mult).then_inc(s["setup_v"], 1)
            v.memset(HT[0][:, :], 0.0).then_inc(s["ht"], 1)
            v.wait_ge(s["tot"], 1)

            def norm(c, k):
                if k == 0:
                    c.wait(v, s["raw_in"], 16 * P // S * TILES, 16 * P // S * TILES)
                    c.wait(v, s["xn"], TILES, 0)
                if k < TILES:
                    v.bn_stats(stats[:, k, :], raw[:, k, :]).then_inc(s["st"], 1)
                else:
                    c.wait_apart(v, passed_v, s["st"], TILES, TILES)
                    for i in range(TILES):
                        ins = v.bn_aggr(mv[:, i, :], stats[:, i, :])
                    ins.then_inc(s["mv"], 1)

            def step(c, t):
                c.wait(v, s["tg"], S, t + 1)
                c.wait(v, s["c2"], S, t)
                v.scalar_tensor_tensor(out=AB[:, :, :], in0=TC[t % 2][:, 0:2, :], scalar=1.0, in1=TC[t % 2][:, 3:5, :],
                                       op0=ALU.add, op1=ALU.mult).then_inc(s["ab"], 1)
                c.wait(v, s["ab"], S, t + 1)
                v.scalar_tensor_tensor(out=TC[(t + 1) % 2][:, 4, :], in0=AB[:, 1, :], scalar=0.5, in1=AB[:, 0, :],
                                       op0=ALU.mult, op1=ALU.add).then_inc(s["c2"], 1)
                if t == 0:
                    c.wait(v, s["done"], 1, -1)
                c.wait(v, s["tc"], S, t + 1)
                v.scalar_tensor_tensor(out=H[c.slot][:, t, :], in0=TC[t % 2][:, 2, :], scalar=1.0, in1=tc[:, :],
                                       op0=ALU.add, op1=ALU.mult).then_inc(s["h"], 1)
                c.wait(v, s["h"], S, t + 1)
                c.wait(v, s["lgp"], S, t - 1)
                v.transpose(HT[(t + 1) % 2][:, :], H[c.slot][:, t, :]).then_inc(s["ht"], 1)

            def choose(c):
                c.wait(v, s["lgp"], S, S)
                v.tensor_tensor(lg[:, :, :], LGb[c.slot][0:B, 0:2 * S].rearrange("b (t l) -> b t l", l=2),
                                bl[:, :].unsqueeze(1).to_broadcast([B, S, 2]), ALU.add).then_inc(s["lg"], 1)
                c.wait(v, s["lg"], 1, 1)
                c.wait(v, s["repp"], 1, 0)
                v.tensor_tensor(gate[0:B, :], lg[:, :, 1], lg[:, :, 0], ALU.is_gt).then_inc(s["gate"], 1)

            def gate_out(c):
                c.wait(v, s["repp"], 1, 1)
                c.wait(v, s["own"], 1, 0)
                v.tensor_copy(gS[:, :], REPb[:, 0:S]).then_inc(s["gs"], 1)

            def before(c):
                for k in range(TILES + 1):
                    norm(c, k)

            def body(c):
                some = c.reg is not None
                nxt, prev = some or c.off < CH - 1, some or c.off > 0
                for t in range(S):
                    step(c, t)
                    if prev and t == 1:
                        choose(c + -1)
                    if prev and t == 2:
                        gate_out(c + -1)
                    if nxt and 3 <= t < 3 + TILES + 1:
                        norm(c + 1, t - 3)

            def after(c):
                choose(c)
                gate_out(c)

            pipeline(v, CH, before, body, after, 2)
            v.wait_ge(s["done"], CH)
            v.wait_ge(s["tot"], 2)
            with v.Fori(0, CH) as i:
                Uc = U[:, bass.ds(i * S, S), :]
                v.tensor_tensor(Uc, Uc, bw[:, :].unsqueeze(1).to_broadcast([P, S, HB]), ALU.add).then_inc(s["fin"], 1)

        @block.gpsimd
        def _(g):
            g.wait_ge(s["setup_v"], 1)

            def normalised(c):
                c.wait_apart(g, passed_g, s["mv"], 1, 1)
                c.wait_apart(g, passed_g, s["xt_pe"], KC, 0)
                g.tensor_scalar(rstd[:, :], mv[:, :, 1], EPS_LN, None, ALU.add).then_inc(s["rstd"], 1)
                c.wait_apart(g, passed_g, s["rstd"], 2, 1)
                g.tensor_tensor(rstd[:, :], rstd[:, :], half[:, 0:TILES], ALU.pow).then_inc(s["rstd"], 1)
                c.wait_apart(g, passed_g, s["rstd"], 2, 2)
                for k in range(TILES):
                    g.tensor_scalar(XN[:, k, :], raw[:, k, :], mv[:, k, 0:1], rstd[:, k:k + 1],
                                    ALU.subtract, ALU.mult).then_inc(s["xn"], 1)

            def sums(c):
                c.wait_apart(g, passed_g, s["gs"], 1, 1)
                Hc = H[c.slot][:, :, :]
                g.tensor_tensor(own[:, :, :], Hc, bcast(gS[:, :], HB), ALU.mult).then_inc(s["own"], 1)
                g.tensor_copy(inc[:, 0, :], inc[:, S, :]).then_inc(s["inc"], 1)
                c.wait_apart(g, passed_g, s["own"], 1, 1)
                for t in range(S):
                    c.wait_apart(g, passed_g, s["inc"], S + 1, t + 1)
                    g.tensor_tensor(inc[:, t + 1, :], inc[:, t, :], own[:, t, :], ALU.add).then_inc(s["inc"], 1)
                c.wait_apart(g, passed_g, s["inc"], S + 1, S + 1)
                g.tensor_tensor(own[:, :, :], own[:, :, :], cown[:, :].unsqueeze(1).to_broadcast([P, S, HB]),
                                ALU.mult).then_inc(s["a"], 1)
                c.dma_wait4(g, resid)
                Uc = U[:, bass.ds(c.index() * S, S), :]
                g.tensor_tensor(Uc, Uc, Hc, ALU.add).then_inc(s["u"], 1)
                c.wait_apart(g, passed_g, s["u"], 3, 1)
                c.wait_apart(g, passed_g, s["a"], 2, 1)
                g.tensor_tensor(Uc, Uc, own[:, :, :], ALU.add).then_inc(s["u"], 1)
                c.wait_apart(g, passed_g, s["u"], 3, 2)
                g.tensor_tensor(own[:, :, :], inc[:, 1:, :], cinc[:, :].unsqueeze(1).to_broadcast([P, S, HB]),
                                ALU.mult).then_inc(s["a"], 1)
                c.wait_apart(g, passed_g, s["a"], 2, 2)
                g.tensor_tensor(Uc, Uc, own[:, :, :], ALU.add).then_inc(s["u"], 1)
                c.wait_apart(g, passed_g, s["u"], 3, 3)
                g.nop().then_inc(s["done"], 1)

            def body(c):
                some = c.reg is not None
                if some or c.off > 0:
                    sums(c + -1)
                if some or c.off < CH - 1:
                    normalised(c + 1)

            def after(c):
                sums(c)
                g.tensor_tensor(bw[:, :], bw[:, :], inc[:, S, :], ALU.mult).then_inc(s["tot"], 1)

            pipeline(g, CH, normalised, body, after, 2)


N_PUT = 6 + 2 * 4 + 2 * 4


GNN0 = {"W": "L0_gnn_W", "a_src": "L0_gnn_a_src", "a_dst": "L0_gnn_a_dst", "bias": "L0_gnn_bias",
        "gamma": "L0_gnn_ln_gamma", "beta": "L0_gnn_ln_beta"}
SSM = {n: f"L0_ffn_{n}" for n in "W_in conv_w conv_b dt_bias A_log D norm_w W_out W_lin b_lin".split()}
GNN1 = {"W": "L1_gnn_W", "a": "L1_gnn_a"}
LSTM = {n: f"L1_ffn_{n}" for n in "W_ih W_hh b_ih b_hh W_lin b_lin fw_att bw_att".split()}


def build(nc, a, consts, out):
    nb = a["x"].shape[0]
    x1, x2, x3 = (nc.dram_tensor(f"x{k}", list(a["x"].shape), F32).ap() for k in (1, 2, 3))
    pick = lambda names: {n: a[full] for n, full in names.items()}
    attention_phase(nc, 0, nb, a["x"], a["adj"], pick(GNN0), consts, x1)
    state_space_phase(nc, nb, x1, pick(SSM), consts, x2)
    attention_phase(nc, 1, nb, x2, a["adj"], pick(GNN1), consts, x3)
    lstm_phase(nc, x3, pick(LSTM), consts, out)


def kernel(**inputs):
    import concourse.bacc as bacc
    from concourse.bass_utils import run_bass_kernel_spmd

    nc = bacc.Bacc("TRN2", target_bir_lowering=False, num_devices=1)
    arrays, aps = {}, {}
    for name, value in {**inputs, **constants()}.items():
        value = np.ascontiguousarray(value)
        arrays[f"in_{name}"] = value
        aps[name] = nc.dram_tensor(f"in_{name}", value.shape, mybir.dt.from_np(value.dtype), kind="ExternalInput").ap()
    out = nc.dram_tensor("out", inputs["x"].shape, F32, kind="ExternalOutput").ap()
    build(nc, aps, aps, out)
    result = run_bass_kernel_spmd(nc, [arrays], core_ids=[0])
    return result.results[0]["out"]
```

```python
from contextlib import ExitStack

import numpy as np
import concourse.bass as bass
from concourse import mybir

F32 = mybir.dt.float32
BF16 = mybir.dt.bfloat16
I32 = mybir.dt.int32
ALU = mybir.AluOpType
ACT = mybir.ActivationFunctionType
AX = mybir.AxisListType.X

P = 128
D = 256
KC = D // P
NEG = -(2.0 ** 100)
EPS_LN = 1e-5


class Batch:

    def __init__(self, reg, off, slots):
        self.reg, self.off, self.slots = reg, off, slots

    def __add__(self, n):
        return Batch(self.reg, self.off + n, self.slots)

    @property
    def slot(self):
        return self.off % self.slots

    def index(self):
        return self.off if self.reg is None else self.reg * self.slots + self.off

    def wait(self, eng, sem, per, more):
        least = self.off * per + more
        if self.reg is None:
            if least > 0:
                eng.wait_ge(sem, least)
        else:
            assert least >= 1, (sem, least)
            eng.wait_ge(sem, self.reg * (self.slots * per) + least)


    def wait_apart(self, eng, passed, sem, per, more):
        self.wait(eng, sem, per, more)
        if self.reg is not None:
            eng.sem_inc(passed, 1)

    def dma_wait(self, eng, sems, more=0):
        n = self.off // self.slots + 1 + more
        if self.reg is not None:
            assert n >= 1
            eng.wait_ge(sems[self.slot], self.reg * 16 + 16 * n)
        elif n > 0:
            eng.wait_ge(sems[self.slot], 16 * n)


    def dma_wait4(self, eng, sems):
        n = 64 * (self.off // self.slots + 1)
        eng.wait_ge(sems[self.slot], n if self.reg is None else self.reg * 64 + n)


def pipeline(eng, nb, before, body, after, slots, ahead=1, behind=1):
    before(Batch(None, 0, slots))
    start = slots + behind
    rounds = (nb - ahead - start) // slots
    for b in range(min(start, nb)):
        body(Batch(None, b, slots))
    if rounds > 1:
        with eng.Fori(0, rounds) as i:
            for k in range(slots):
                body(Batch(i, start + k, slots))
        start += slots * rounds
    for b in range(start, nb):
        body(Batch(None, b, slots))
    after(Batch(None, nb - 1, slots))


class Memory:

    def __init__(self, nc, ctx, tag):
        self.nc, self.ctx, self.tag = nc, ctx, tag
        self.sems = []

    def sb(self, name, shape, dt=F32):
        return self.ctx.enter_context(self.nc.sbuf_tensor(f"{self.tag}_{name}", shape, dt))

    def ps(self, name, shape=(P, 512), dt=F32):
        return self.ctx.enter_context(self.nc.psum_tensor(f"{self.tag}_{name}_psum", list(shape), dt))

    def sem(self, name):
        self.sems.append(self.ctx.enter_context(self.nc.semaphore(f"{self.tag}_{name}")))
        return self.sems[-1]

    def clear(self, failed=None, *_):
        if failed:
            return
        with self.nc.Block() as block:
            @block.gpsimd
            def _(g):
                for sem in self.sems:
                    g.sem_clear(sem)


def bcast(ap, n):
    return ap.unsqueeze(len(ap.shape)).to_broadcast(list(ap.shape) + [n])


def selectors(types=4, quadrants=(0, 64, 96)):
    out = np.zeros((P, 2 + 2 * types * 4), np.float32)
    for q in quadrants:
        for t in range(types):
            for h in range(4):
                src, dst = q + 8 * t + h, q + 8 * t + 4 + h
                out[src, 0] = 1.0
                out[dst, 1] = 1.0
                c = 2 + 2 * (4 * t + h)
                out[dst, c] = 1.0
                out[src, c + 1] = 1.0
    return out


def decay_selectors():
    out = np.zeros((P, 2 + 2 * 8), np.float32)
    for q in (0, 64, 96):
        for h in range(8):
            pos, neg = q + h, q + 8 + h
            out[neg, 0] = 1.0
            out[pos, 1] = 1.0
            out[pos, 2 + 2 * h] = 1.0
            out[neg, 3 + 2 * h] = 1.0
    return out


def constants():
    tri = np.where(np.arange(P)[:, None] <= np.arange(P)[None, :], 0.0, NEG).astype(np.float32)
    repeat = np.zeros((P, P), np.float32)
    for b in range(32):
        repeat[b, b::32] = 1.0
    return {"repeat": repeat, "identity": np.eye(P, dtype=np.float32), "selectors": selectors(),
            "typed_selectors": selectors(5, (0,)), "decay_selectors": decay_selectors(), "causal": tri}


def attention_phase(nc, layer, nb, x_in, adj, weights, consts, x_out, kept=None):
    first = layer == 0
    H = 4 if first else 1
    E = D // H
    N = 512
    IT = N // P
    ALPHA = 0.01 if first else 0.2
    SLOTS = 3 if first else 4
    NP = 2 if first else 1
    ITEMS = NP * IT * (2 if first else 1)
    HH = ITEMS // (NP * IT)
    with ExitStack() as ctx:
        m = Memory(nc, ctx, f"g{layer}")
        ident = m.sb("ident", [P, P])
        ident_bf = m.sb("ident_bf", [P, P], BF16)
        sel = m.sb("sel", [P, 34])
        W = m.sb("W", [P, KC, D])
        WA = m.sb("WA", [P, KC, P])
        X = [m.sb(f"X{k}", [P, IT, D]) for k in range(SLOTS)]
        ADJ = m.sb("ADJ", [P, IT, N], I32)
        MASK = [m.sb(f"MASK{k}", [P, IT, N], BF16) for k in range(SLOTS)]
        stats = m.sb("stats", [P, IT, 6])
        mv = m.sb("mv", [P, IT, 2])
        rstd = m.sb("rstd", [P, IT])
        half = m.sb("half", [P, 16])
        XN = m.sb("XN", [P, IT, D])
        XT = m.sb("XT", [P, KC, N])
        HS = [m.sb(f"HS{k}", [P, IT, D]) for k in range(SLOTS)]
        parts = m.sb("parts", [P, N], BF16)
        rest = m.sb("rest", [P, N])
        L = [m.sb(f"L{k}", [P, N], BF16) for k in range(SLOTS)]
        R = [m.sb(f"R{k}", [P, H, N], BF16) for k in range(SLOTS)]
        relu = [m.sb(f"relu{k}", [P, N]) for k in range(4)]
        S = [m.sb(f"S{k}", [P, N]) for k in range(4)]
        nmax = m.sb("nmax", [P, 4])
        PR = [m.sb(f"PR{k}", [P, N]) for k in range(4)]
        rsum = [m.sb(f"rsum{k}", [P, IT, H]) for k in range(SLOTS)]
        rinv = m.sb("rinv", [P, IT, H])
        G = m.sb("G", [P, IT, D])
        XO = [m.sb(f"XO{k}", [P, IT, D]) for k in range(SLOTS)]
        Zb = [m.ps(f"Z{k}") for k in range(2)]
        PTb = [m.ps(f"PT{k}") for k in range(2)]
        Ob = [m.ps(f"O{k}") for k in range(2)]
        Ab = [m.ps(f"A{k}") for k in range(2)]

        names = ("const w setup_pe setup_v adj_loaded mask st mv rstd xn xt_pe xt h_pe h hb e_pe parts lr "
                 "z relu s p t ev pv ot ob d1 d3 sum d4 sq ssq out rinv v zero check xb").split()
        s = {n: m.sem(n) for n in names}
        x_loaded = [m.sem(f"x_loaded{k}") for k in range(SLOTS)]
        stored = [m.sem(f"stored{k}") for k in range(SLOTS)]
        if first:
            HB = [m.sb(f"HB{k}", [P, IT, D]) for k in range(SLOTS)]
            PT = [m.sb(f"PT{k}", [P, IT, N]) for k in range(H)]
            OT = m.sb("OT", [P, 2, N])
            arow = m.sb("arow", [64, E])
            aT = m.sb("aT", [64, 64])
            WT = m.sb("WT", [64, H, D])
            checked = m.sb("checked", [P, IT * N], BF16)
            bias, gamma, beta = (m.sb(n, [P, D]) for n in ("bias", "gamma", "beta"))
            sums = m.sb("sums", [P, 16])
            ssq = m.sb("ssq", [P, 16])
            SQ = m.sb("SQ", [P, IT, D])
            XB = m.sb("XB", [P, IT, D])
        else:
            HB = HS
            PT = [m.sb(f"PT{k}", [P, N]) for k in range(4)]
            arow = m.sb("arow", [P, KC, 2])
            WT = m.sb("WT", [P, KC, D])
            mn = m.sb("mn", [P, IT, D])
            ex = m.sb("ex", [P, IT, D])

        xv = x_in.rearrange("b (t p) d -> b p t d", p=P)
        av = adj.rearrange("b (t p) j -> b p t j", p=P)
        ov = x_out.rearrange("b (t p) d -> b p t d", p=P)

        TURN, EVACUATE, WEIGH = 2, 3, 4

        def lagged(b, n, lag):
            if n >= lag:
                return b, n - lag
            return (b + -1, n - lag + ITEMS) if b.reg is not None or b.off > 0 else None

        def around(b):
            return [b.reg is not None or 0 <= b.off + k < nb for k in (-2, -1, 1, 2)]

        n_w = 6 * 16 if first else 3 * 16
        passed_v, passed_g, passed_pe, passed_a = (m.sem(f"passed_{n}") for n in ("v", "g", "pe", "act"))
        ctx.push(m.clear)
        block = ctx.enter_context(nc.Block())

        @block.sync
        def _(sp):
            sp.dma_start(X[0][:, :, :], xv[0]).then_inc(x_loaded[0], 16)
            sp.dma_start(ident[:, :], consts["identity"]).then_inc(s["const"], 16)
            sp.dma_start(sel[:, :], consts["selectors"]).then_inc(s["const"], 16)
            if first:
                for kc in range(KC):
                    sp.dma_start(W[:, kc, :].rearrange("k (h e) -> k h e", h=H),
                                 weights["W"][:, kc * P:(kc + 1) * P, :].rearrange("h k e -> k h e")
                                 ).then_inc(s["w"], 16)
                sp.wait_ge(s["zero"], 1)
                sp.dma_start(arow[0:20, :], weights["a_src"].rearrange("h t e -> (h t) e")).then_inc(s["w"], 16)
                sp.dma_start(arow[32:52, :], weights["a_dst"].rearrange("h t e -> (h t) e")).then_inc(s["w"], 16)
                sp.dma_start(gamma[:, :], weights["gamma"].rearrange("(o h) e -> o (h e)", o=1).to_broadcast([P, D])
                             ).then_inc(s["w"], 16)
                sp.dma_start(beta[:, :], weights["beta"].rearrange("(o h) e -> o (h e)", o=1).to_broadcast([P, D])
                             ).then_inc(s["w"], 16)
                sp.dma_start(bias[:, :], weights["bias"].rearrange("(o h) e -> o (h e)", o=1).to_broadcast([P, D])
                             ).then_inc(s["const"], 16)
            else:
                sp.dma_start(W[:, :, :], weights["W"].rearrange("(c k) e -> k c e", k=P)).then_inc(s["w"], 16)
                for c in range(2):
                    sp.dma_start(arow[:, :, c], weights["a"][c * D:(c + 1) * D].rearrange("(k p) -> p k", p=P),
                                 allow_slow_non_contiguous=True
                                 ).then_inc(s["w"], 16)

            def load_x(b):
                b.wait(sp, s["xb"] if first else s["d4"], 1, 1 - SLOTS)
                sp.dma_start(X[b.slot][:, :, :], xv[b.index()]).then_inc(x_loaded[b.slot], 16)

            def load_adj(b):
                b.wait(sp, s["mask"], 1, 0)
                if first:
                    b.wait(sp, s["check"], 1, 0)
                sp.dma_start(ADJ[:, :, :], av[b.index()]).then_inc(s["adj_loaded"], 16)

            def before(b):
                load_adj(b)
                load_x(b + 1)

            def body(b):
                prev2, prev, nxt, nxt2 = around(b)
                if nxt:
                    load_adj(b + 1)
                if nxt2:
                    load_x(b + 2)
                if first and prev:
                    store(b + -1)
                if not first and prev2:
                    store(b + -2)

            def after(b):
                if not first:
                    store(b + -1)
                store(b)

            def store(b):
                b.wait(sp, s["out"], 1, 1)
                sp.dma_start(ov[b.index()], XO[b.slot][:, :, :]).then_inc(stored[b.slot], 16)

            pipeline(sp, nb, before, body, after, SLOTS, 2, 1 if first else 2)
            for k in range(SLOTS):
                sp.wait_ge(stored[k], 16 * len(range(k, nb, SLOTS)))

        @block.tensor
        def _(pe):
            pe.wait_ge(s["const"], 48 if first else 32)
            pe.wait_ge(s["w"], n_w)
            if first:
                pe.transpose(Zb[0][0:64, 0:64], arow[:, :], ident[0:64, 0:64])
                for h in range(H):
                    for kc in range(KC):
                        ins = pe.transpose(Zb[1 + 0 * h][0:E, (h % 2) * D + kc * P:(h % 2) * D + (kc + 1) * P]
                                           if h < 2 else
                                           PTb[0][0:E, (h % 2) * D + kc * P:(h % 2) * D + (kc + 1) * P],
                                           W[:, kc, h * E:(h + 1) * E], ident[:, :])
                ins.then_inc(s["setup_pe"], 1)
                pe.wait_ge(s["setup_v"], 5)
                aTv = aT[:, :].rearrange("e (s x) -> e s x", s=2)
                for kc in range(KC):
                    for h in range(H):
                        ins = pe.matmul(Ab[kc][:, 10 * h:10 * h + 10].rearrange("p (s t) -> p s t", s=2),
                                        WT[:, h, kc * P:(kc + 1) * P],
                                        aTv[:, :, 5 * h:5 * h + 5], start=True, stop=True)
                ins.then_inc(s["setup_pe"], 1)
            else:
                for e in range(KC):
                    for kc in range(KC):
                        ins = pe.transpose(Zb[e][:, kc * P:(kc + 1) * P], W[:, kc, e * P:(e + 1) * P], ident[:, :])
                ins.then_inc(s["setup_pe"], 1)
                pe.wait_ge(s["setup_v"], 4)
                for kc in range(KC):
                    for e in range(KC):
                        ins = pe.matmul(Ab[kc][:, 0:2], WT[:, e, kc * P:(kc + 1) * P], arow[:, e, :],
                                        start=(e == 0), stop=(e == KC - 1))
                ins.then_inc(s["setup_pe"], 1)
            pe.wait_ge(s["setup_v"], 8)

            def xn_turned(b):
                b.wait(pe, s["xn"], IT, IT)
                for kc in range(KC):
                    if kc == 0:
                        b.wait(pe, s["parts"], 1, 0)
                    elif first:
                        b.wait(pe, s["d1"], NP, -2 * NP)
                    else:
                        b.wait(pe, s["h"], 2, 0)
                    for t in range(IT):
                        ins = pe.transpose(Ab[kc][:, t * P:(t + 1) * P], XN[:, t, kc * P:(kc + 1) * P], ident[:, :])
                    ins.then_inc(s["xt_pe"], 1)

            def project(b):
                for g in range(2):
                    b.wait(pe, s["xt"], 2, 2)
                    for t in (2 * g, 2 * g + 1):
                        for kc in range(KC):
                            ins = pe.matmul(Ab[g][:, (t % 2) * D:(t % 2 + 1) * D], XT[:, kc, t * P:(t + 1) * P],
                                            W[:, kc, :], start=(kc == 0), stop=(kc == KC - 1))
                    ins.then_inc(s["h_pe"], 1)

            def logits(b):
                b.wait(pe, s["h"], 2, 1)
                for kc in range(KC):
                    ins = pe.matmul(Ab[0][:, :], WA[:, kc, :], XT[:, kc, :], start=(kc == 0), stop=(kc == KC - 1))
                ins.then_inc(s["e_pe"], 1)

            def scores(b, n):
                p, t, hh = n // (IT * HH), n // HH % IT, n % HH
                if n == 0:
                    b.wait(pe, s["lr"], H + 1, H + 1)
                    b.wait(pe, s["mask"], 1, 1)
                b.wait(pe, s["s"], ITEMS, n - 1)
                pe.matmul(Zb[n % 2][:, :], L[b.slot][:, t * P:(t + 1) * P], R[b.slot][:, HH * p + hh, :],
                          start=True, stop=False)
                pe.matmul(Zb[n % 2][:, :], ident_bf[:, :], MASK[b.slot][:, t, :],
                          start=False, stop=True).then_inc(s["z"], 1)

            def turn(b, n):
                b.wait(pe, s["p"], ITEMS, n + 1)
                b.wait(pe, s["ev"], ITEMS, n - 1)
                for k in range(IT):
                    ins = pe.transpose(PTb[n % 2][:, k * P:(k + 1) * P], PR[n % 4][:, k * P:(k + 1) * P], ident[:, :])
                ins.then_inc(s["t"], 1)

            def weigh_pass(b, p, ks):
                if ks[0] == 0:
                    b.wait(pe, s["ev"], ITEMS, ITEMS // NP * (p + 1))
                    b.wait(pe, s["hb"], 1, 1)
                    b.wait(pe, s["ot"], NP, p + 1 - NP)
                for k in ks:
                    for hh in range(HH):
                        h = HH * p + hh
                        ins = pe.matmul(Ob[p][hh * E:(hh + 1) * E, :], HB[b.slot][:, k, h * E:(h + 1) * E],
                                        PT[h][:, k, :], start=(k == 0), stop=(k == IT - 1), skip_group_check=True)
                if ks[-1] == IT - 1:
                    ins.then_inc(s["pv"], 1)

            def weigh(b, t):
                b.wait(pe, s["ev"], ITEMS, t + 1)
                if t == 0:
                    b.wait(pe, s["h"], 2, 2)
                    b.wait(pe, s["ot"], 2, 0)
                for k in range(IT):
                    ins = pe.matmul(Ob[t // 2][:, (t % 2) * D:(t % 2 + 1) * D], PT[t % 4][:, k * P:(k + 1) * P],
                                    HB[b.slot][:, k, :], start=(k == 0), stop=(k == IT - 1))
                ins.then_inc(s["pv"], 1)

            def outputs_turned(b, p, newest):
                b.wait(pe, s["ot"], 2, p + 1)
                if p == 0:
                    newest.wait(pe, s["h"], 2, 2)
                else:
                    b.wait(pe, s["d1"], NP, p)
                for t in range(IT):
                    ins = pe.transpose(Ab[1][:, t * P:(t + 1) * P], OT[:, p, t * P:(t + 1) * P], ident[:, :])
                ins.then_inc(s["ob"], 1)

            def pre(b):
                xn_turned(b)
                project(b)
                logits(b)

            XN_AT, PROJECT_AT, LOGITS_AT = (1, 2, 4) if first else (0, 1, 2)

            def attend(at, f):
                if at is not None:
                    f(*at)

            SECOND_AT = 3
            FIRST_AT = SECOND_AT + ITEMS // NP
            TILES_AT_ONCE = 1

            def weigh_part(b, p, n):
                if 0 <= n < IT // TILES_AT_ONCE:
                    weigh_pass(b, p, range(TILES_AT_ONCE * n, TILES_AT_ONCE * (n + 1)))

            def body(b):
                prev2, prev, nxt, nxt2 = around(b)
                for n in range(ITEMS):
                    scores(b, n)
                    attend(lagged(b, n, TURN), turn)
                    if nxt and n == XN_AT:
                        xn_turned(b + 1)
                    if nxt and n == PROJECT_AT:
                        project(b + 1)
                    if nxt and n == LOGITS_AT:
                        logits(b + 1)
                    if first:
                        if prev:
                            weigh_part(b + -1, 1, n - SECOND_AT)
                        weigh_part(b, 0, n - FIRST_AT)
                    else:
                        attend(lagged(b, n, WEIGH), weigh)
                    if first and prev and n in (6, 8):
                        outputs_turned(b + -1, (n - 6) // 2, b + 1 if nxt else b)

            def after(b):
                for n in range(ITEMS, ITEMS + WEIGH):
                    if n - TURN < ITEMS:
                        turn(b, n - TURN)
                    if not first:
                        weigh(b, n - WEIGH)
                if first:
                    weigh_pass(b, 1, range(IT))
                    for p in range(NP):
                        outputs_turned(b, p, b)

            pipeline(pe, nb, pre, body, after, SLOTS, 2, 1 if first else 2)

        @block.scalar
        def _(act):
            def xt_out(b):
                for kc in range(KC):
                    b.wait(act, s["xt_pe"], 2, kc + 1)
                    if kc == 0:
                        b.wait(act, s["e_pe"], 1, 0)
                    act.activation(XT[:, kc, :], Ab[kc][:, :], ACT.Copy).then_inc(s["xt"], 1)

            def h_out(b):
                b.wait(act, s["d3" if first else "pv"], 1 if first else IT, (1 - SLOTS) * (1 if first else IT))
                for g in range(2):
                    b.wait(act, s["h_pe"], 2, g + 1)
                    act.activation(HS[b.slot][:, 2 * g:2 * g + 2, :].rearrange("p t d -> p (t d)"),
                                   Ab[g][:, :], ACT.Copy).then_inc(s["h"], 1)

            def relu_part(b, n):
                b.wait(act, s["z"], ITEMS, n + 1)
                b.wait(act, s["s"], ITEMS, n - 3)
                act.activation(relu[n % 4][:, :], Zb[n % 2][:, :], ACT.Relu,
                               scale=(1.0 - ALPHA) / ALPHA).then_inc(s["relu"], 1)

            def exp(b, n):
                p, t, hh = n // (IT * HH), n // HH % IT, n % HH
                b.wait(act, s["s"], ITEMS, n + 1)
                b.wait(act, s["t"], ITEMS, n - 3)
                if n == 0:
                    b.wait(act, s["rinv"], 1, 1 - SLOTS)
                act.activation(PR[n % 4][:, :], S[n % 4][:, :], ACT.Exp, scale=-1.0, bias=nmax[:, n % 4:n % 4 + 1],
                               accum_out=rsum[b.slot][:, t, HH * p + hh:HH * p + hh + 1]).then_inc(s["p"], 1)

            def o_out(b, p):
                b.wait(act, s["pv"], NP, p + 1)
                b.wait(act, s["ob"], NP, p - 1)
                act.activation(OT[:, p, :], Ob[p][:, :], ACT.Copy).then_inc(s["ot"], 1)

            def check(b):
                b.wait(act, s["check"], 1, 0)
                b.wait_apart(act, passed_a, s["adj_loaded"], 16, 16)
                act.activation(checked[:, :], ADJ[:, :, :].rearrange("p t j -> p (t j)"), ACT.Square,
                               bias=half[:, 0:1], accum_out=kept["odd"][:, bass.ds(b.index(), 1)]
                               ).then_inc(s["check"], 1)

            def square(b):
                b.wait(act, s["d4"], 1, 1)
                act.activation(SQ[:, :, :].rearrange("p t d -> p (t d)"), G[:, :, :].rearrange("p t d -> p (t d)"),
                               ACT.Square).then_inc(s["sq"], 1)

            def pre(b):
                xt_out(b)
                h_out(b)
                if first:
                    check(b)

            act.wait_ge(s["v"], 2)

            def exp_min(b):
                b.wait(act, s["d3"], 1, 1)
                act.activation(ex[:, :, :].rearrange("p t d -> p (t d)"),
                               mn[:, :, :].rearrange("p t d -> p (t d)"), ACT.Exp).then_inc(s["sq"], 1)

            XT_AT, H_AT = (1, 3) if first else (0, 1)

            def body(b):
                prev2, prev, nxt, nxt2 = around(b)
                for n in range(ITEMS):
                    relu_part(b, n)
                    at = lagged(b, n, 1)
                    if at is not None:
                        exp(*at)
                    if nxt and n == XT_AT:
                        xt_out(b + 1)
                    if nxt and n == H_AT:
                        h_out(b + 1)
                    if first:
                        if prev and n == 7:
                            o_out(b + -1, 1)
                        if nxt and n == 10:
                            check(b + 1)
                        if n == 15:
                            o_out(b, 0)
                        if prev and n == 12:
                            square(b + -1)
                    elif prev2 and n == 1:
                        exp_min(b + -2)

            def after(b):
                exp(b, ITEMS - 1)
                if first:
                    o_out(b, 1)
                    square(b)
                else:
                    exp_min(b + -1)
                    exp_min(b)

            pipeline(act, nb, pre, body, after, SLOTS, 2, 1 if first else 2)

        @block.vector
        def _(v):
            def norm_stats(b):
                b.dma_wait(v, x_loaded)
                b.wait(v, s["xn"], IT, 0)
                for t in range(IT):
                    ins = v.bn_stats(stats[:, t, :], X[b.slot][:, t, :])
                ins.then_inc(s["st"], 1)
                b.wait_apart(v, passed_v, s["st"], 1, 1)
                for t in range(IT):
                    ins = v.bn_aggr(mv[:, t, :], stats[:, t, :])
                ins.then_inc(s["mv"], 1)

            if first:
                v.memset(arow[:, :], 0.0).then_inc(s["zero"], 1)
            v.memset(half[:, :], -0.5).then_inc(s["v"], 1)
            v.memset(WA[:, :, :], 0.0).then_inc(s["v"], 1)
            norm_stats(Batch(None, 0, SLOTS))
            v.wait_ge(s["const"], 48 if first else 32)
            v.wait_ge(s["v"], 2)
            v.tensor_copy(ident_bf[:, :], ident[:, :]).then_inc(s["setup_v"], 1)
            v.wait_ge(s["setup_pe"], 1)
            if first:
                v.tensor_copy(aT[:, :], Zb[0][0:64, 0:64]).then_inc(s["setup_v"], 1)
                v.tensor_copy(WT[:, 0:2, :].rearrange("e h d -> e (h d)"), Zb[1][0:64, :]).then_inc(s["setup_v"], 1)
                v.tensor_copy(WT[:, 2:4, :].rearrange("e h d -> e (h d)"), PTb[0][0:64, :]).then_inc(s["setup_v"], 1)
                v.nop().then_inc(s["setup_v"], 1)
                v.wait_ge(s["setup_pe"], 2)
                for q in (0, 64, 96):
                    for kc in range(KC):
                        for side in range(2):
                            ins = v.tensor_scalar(
                                WA[:, kc, q:q + 32].rearrange("p (t s h) -> p s h t", s=2, h=H)[:, side],
                                Ab[kc][:, 0:40].rearrange("p (h s t) -> p s h t", s=2, t=5)[:, side, :, 0:4],
                                ALPHA, None, ALU.mult)
                for kc in range(KC):
                    for side in range(2):
                        ins = v.tensor_copy(kept["WG"][:, kc, :].rearrange("p (t s h) -> p s h t", s=2, h=H)[:, side],
                                            Ab[kc][:, 0:40].rearrange("p (h s t) -> p s h t", s=2, t=5)[:, side])
                for _ in range(3):
                    ins = v.nop().then_inc(s["setup_v"], 1) if _ else ins.then_inc(s["setup_v"], 1)
            else:
                for e in range(KC):
                    v.tensor_copy(WT[:, e, :], Zb[e][:, 0:D]).then_inc(s["setup_v"], 1)
                v.nop().then_inc(s["setup_v"], 1)
                v.wait_ge(s["setup_pe"], 2)
                for q in (0, 64, 96):
                    for kc in range(KC):
                        for side in range(2):
                            ins = v.tensor_scalar(WA[:, kc, q + 4 * side:q + 4 * side + 1],
                                                  Ab[kc][:, side:side + 1], ALPHA, None, ALU.mult)
                for _ in range(4):
                    ins = v.nop().then_inc(s["setup_v"], 1) if _ else ins.then_inc(s["setup_v"], 1)

            def normalised_x(b):
                b.wait(v, s["rstd"], 1, 1)
                b.wait(v, s["xt_pe"], KC, 0)
                for t in range(IT):
                    v.tensor_scalar(XN[:, t, :], X[b.slot][:, t, :], mv[:, t, 0:1], rstd[:, t:t + 1],
                                    ALU.subtract, ALU.mult).then_inc(s["xn"], 1)

            def make_mask(b):
                b.wait(v, s["adj_loaded"], 16, 16)
                b.wait(v, s["z"], ITEMS, (1 - SLOTS) * ITEMS)
                v.tensor_scalar(MASK[b.slot][:, :, :].rearrange("p t j -> p (t j)"),
                                ADJ[:, :, :].rearrange("p t j -> p (t j)"), 0.0 if first else 0.5, NEG,
                                ALU.is_equal if first else ALU.is_lt, ALU.mult).then_inc(s["mask"], 1)

            def split(b, stages=(0, 1, 2)):
                if 0 in stages:
                    b.wait(v, s["e_pe"], 1, 1)
                    b.wait(v, s["lr"], H + 1, 0)
                    v.tensor_copy(parts[:, :], Ab[0][:, :]).then_inc(s["v"], 1)
                    b.wait(v, s["v"], NV, 2 + 1)
                    v.tensor_tensor(rest[64:P, :], Ab[0][64:P, :], parts[64:P, :], ALU.subtract).then_inc(s["v"], 1)
                if 1 in stages:
                    b.wait(v, s["v"], NV, 2 + 2)
                    v.tensor_copy(parts[64:P, :], rest[64:P, :]).then_inc(s["v"], 1)
                    b.wait(v, s["v"], NV, 2 + 3)
                    v.tensor_tensor(rest[96:P, :], rest[96:P, :], parts[96:P, :], ALU.subtract).then_inc(s["v"], 1)
                if 2 in stages:
                    b.wait(v, s["v"], NV, 2 + 4)
                    v.tensor_copy(parts[96:P, :], rest[96:P, :]).then_inc(s["parts"], 1)

            def leaky(b, n):
                b.wait(v, s["relu"], ITEMS, n + 1)
                b.wait_apart(v, passed_v, s["p"], ITEMS, n - 3)
                v.tensor_tensor_reduce(S[n % 4][:, :], Zb[n % 2][:, :], relu[n % 4][:, :], -1.0, 3e38,
                                       ALU.add, ALU.min, nmax[:, n % 4:n % 4 + 1]).then_inc(s["s"], 1)

            def evacuate(b, n):
                b.wait(v, s["t"], ITEMS, n + 1)
                if first:
                    p, t, hh = n // (IT * HH), n // HH % IT, n % HH
                    b.wait(v, s["pv"], NP, p + 1 - NP)
                    v.tensor_copy(PT[HH * p + hh][:, :, t * P:(t + 1) * P],
                                  PTb[n % 2][:, :].rearrange("p (k i) -> p k i", k=IT)).then_inc(s["ev"], 1)
                else:
                    b.wait(v, s["pv"], IT, n - 3)
                    v.tensor_copy(PT[n % 4][:, :], PTb[n % 2][:, :]).then_inc(s["ev"], 1)

            def recip(b):
                b.wait(v, s["p"], ITEMS, ITEMS)
                b.wait(v, s["d1"], NP, 0)
                v.reciprocal(rinv[:, :, :].rearrange("p t h -> p (t h)"),
                             rsum[b.slot][:, :, :].rearrange("p t h -> p (t h)")).then_inc(s["rinv"], 1)

            def normalise(b, p):
                b.wait(v, s["ob"], NP, p + 1)
                if p == 0:
                    b.wait(v, s["rinv"], 1, 1)
                    b.wait(v, s["out"], 1, 0)
                v.tensor_tensor(G[:, :, 2 * p * E:2 * (p + 1) * E].rearrange("p t (h e) -> p t h e", h=2),
                                Ab[1][:, :].rearrange("p (t h e) -> p t h e", t=IT, h=2),
                                bcast(rinv[:, :, 2 * p:2 * p + 2], E), ALU.mult).then_inc(s["d1"], 1)

            flat = "p t d -> p (t d)"
            heads = "p t (h e) -> p (t h) e"

            def residual_sum(b):
                b.wait(v, s["d1"], NP, NP)
                v.scalar_tensor_tensor(out=G[:, :, :].rearrange(flat), in0=G[:, :, :].rearrange(flat), scalar=0.0,
                                       in1=HS[b.slot][:, :, :].rearrange(flat), op0=ALU.max,
                                       op1=ALU.add).then_inc(s["d3"], 1)
                b.wait(v, s["d3"], 1, 1)
                v.tensor_reduce(sums[:, :], G[:, :, :].rearrange(heads, h=H), AX, ALU.add).then_inc(s["sum"], 1)

            def squares_sum(b):
                b.wait(v, s["sq"], 1, 1)
                v.tensor_reduce(ssq[:, :], SQ[:, :, :].rearrange(heads, h=H), AX, ALU.add).then_inc(s["ssq"], 1)

            NV = 4

            def pre(b):
                if not first:
                    normalised_x(b)
                make_mask(b)
                split(b)
                norm_stats(b + 1)
                if not first:
                    normalised_x(b + 1)

            def elu_parts(b):
                b.wait(v, s["p"], ITEMS, ITEMS)
                v.reciprocal(rinv[:, :, 0], rsum[b.slot][:, :, 0]).then_inc(s["rinv"], 1)
                b.wait(v, s["rinv"], 1, 1)
                b.wait(v, s["pv"], IT, IT)
                b.wait(v, s["out"], 1, 0)
                for g in range(2):
                    v.tensor_tensor(G[:, 2 * g:2 * g + 2, :], Ob[g][:, :].rearrange("p (t d) -> p t d", t=2),
                                    bcast(rinv[:, 2 * g:2 * g + 2, 0], D), ALU.mult).then_inc(s["ot"], 1)
                b.wait(v, s["ot"], 2, 2)
                v.tensor_scalar(mn[:, :, :].rearrange(flat), G[:, :, :].rearrange(flat), 0.0, None,
                                ALU.min).then_inc(s["d3"], 1)
                v.tensor_scalar(G[:, :, :].rearrange(flat), G[:, :, :].rearrange(flat), 0.0, -1.0,
                                ALU.max, ALU.add).then_inc(s["sum"], 1)
                b.wait(v, s["sum"], 1, 1)
                v.tensor_tensor(G[:, :, :].rearrange(flat), G[:, :, :].rearrange(flat),
                                X[b.slot][:, :, :].rearrange(flat), ALU.add).then_inc(s["d4"], 1)

            def elu_sum(b):
                b.wait(v, s["d4"], 1, 1)
                b.wait(v, s["sq"], 1, 1)
                b.dma_wait(v, stored, -1)
                v.tensor_tensor(XO[b.slot][:, :, :].rearrange(flat), G[:, :, :].rearrange(flat),
                                ex[:, :, :].rearrange(flat), ALU.add).then_inc(s["out"], 1)

            def body(b):
                prev2, prev, nxt, nxt2 = around(b)
                for n in range(ITEMS):
                    if not first and prev2 and n == 0:
                        elu_parts(b + -2)
                    at = lagged(b, n, EVACUATE)
                    if at is not None:
                        evacuate(*at)
                    leaky(b, n)
                    if first:
                        if nxt and n in (4, 5, 6):
                            split(b + 1, (n - 4,))
                        if nxt2 and n == 8:
                            norm_stats(b + 2)
                        if nxt and n == 11:
                            make_mask(b + 1)
                        if prev:
                            if n == 2:
                                recip(b + -1)
                            if n in (7, 9):
                                normalise(b + -1, (n - 7) // 2)
                            if n == 10:
                                residual_sum(b + -1)
                            if n == 13:
                                squares_sum(b + -1)
                    else:
                        if nxt and n == 1:
                            make_mask(b + 1)
                        if nxt and n == 2:
                            split(b + 1)
                        if prev2 and n == 2:
                            elu_sum(b + -2)
                        if nxt2 and n == 1:
                            norm_stats(b + 2)
                        if nxt2 and n == 3:
                            normalised_x(b + 2)

            def after(b):
                if not first:
                    elu_parts(b + -1)
                for n in range(ITEMS - EVACUATE, ITEMS):
                    evacuate(b, n)
                if first:
                    recip(b)
                    for p in range(NP):
                        normalise(b, p)
                    residual_sum(b)
                    squares_sum(b)
                else:
                    elu_sum(b + -1)
                    elu_parts(b)
                    elu_sum(b)

            pipeline(v, nb, pre, body, after, SLOTS, 2, 1 if first else 2)

        @block.gpsimd
        def _(g):
            pool = m.sem("pool")
            g.wait_ge(s["v"], 2)

            def normalised(b):
                b.wait_apart(g, passed_g, s["mv"], 1, 1)
                b.wait_apart(g, passed_g, s["xt_pe"], 2, 0)
                g.tensor_scalar(rstd[:, :], mv[:, :, 1], EPS_LN, None, ALU.add).then_inc(pool, 1)
                b.wait_apart(g, passed_g, pool, 2 if first else 1, 1)
                g.tensor_tensor(rstd[:, :], rstd[:, :], half[:, 0:IT], ALU.pow).then_inc(pool if first else s["rstd"], 1)
                if first:
                    b.wait_apart(g, passed_g, pool, 2, 2)
                    for t in range(IT):
                        g.tensor_scalar(XN[:, t, :], X[b.slot][:, t, :], mv[:, t, 0:1], rstd[:, t:t + 1],
                                        ALU.subtract, ALU.mult).then_inc(s["xn"], 1)

            def rows(b):
                b.wait_apart(g, passed_g, s["parts"], 1, 1)
                b.wait_apart(g, passed_g, s["z"], ITEMS, (1 - SLOTS) * ITEMS)
                g.tensor_scalar(L[b.slot][:, :], parts[:, :], sel[:, 0:1], sel[:, 1:2], ALU.mult, ALU.add
                                ).then_inc(s["lr"], 1)
                for h in range(H):
                    g.tensor_scalar(R[b.slot][:, h, :], parts[:, :], sel[:, 2 + 2 * h:3 + 2 * h],
                                    sel[:, 3 + 2 * h:4 + 2 * h], ALU.mult, ALU.add).then_inc(s["lr"], 1)

            def bias_added(b):
                b.wait_apart(g, passed_g, s["h"], 2, 2)
                b.wait_apart(g, passed_g, s["pv"], NP, (1 - SLOTS) * NP)
                g.tensor_tensor(HB[b.slot][:, :, :], HS[b.slot][:, :, :],
                                bias[:, :].unsqueeze(1).to_broadcast([P, IT, D]), ALU.add).then_inc(s["hb"], 1)

            heads = "p t (h e) -> p (t h) e"

            def residual(b):
                b.wait_apart(g, passed_g, s["out"], 1, 0)
                g.tensor_tensor(XB[:, :, :], X[b.slot][:, :, :],
                                beta[:, :].unsqueeze(1).to_broadcast([P, IT, D]), ALU.add).then_inc(s["xb"], 1)

            def centred(b):
                b.wait_apart(g, passed_g, s["sum"], 1, 1)
                g.tensor_scalar(sums[:, :], sums[:, :], 1.0 / E, None, ALU.mult).then_inc(pool2, 1)
                b.wait_apart(g, passed_g, pool2, 6, 1)
                Gv = G[:, :, :].rearrange(heads, h=H)
                g.tensor_tensor(Gv, Gv, bcast(sums[:, :], E), ALU.subtract).then_inc(s["d4"], 1)

            def layernorm(b):
                Gv = G[:, :, :].rearrange(heads, h=H)
                b.wait_apart(g, passed_g, s["ssq"], 1, 1)
                g.tensor_scalar(ssq[:, :], ssq[:, :], 1.0 / E, 1e-6, ALU.mult, ALU.add).then_inc(pool2, 1)
                b.wait_apart(g, passed_g, pool2, 6, 2)
                g.tensor_tensor(ssq[:, :], ssq[:, :], half[:, :], ALU.pow).then_inc(pool2, 1)
                b.wait_apart(g, passed_g, pool2, 6, 3)
                g.tensor_tensor(Gv, Gv, bcast(ssq[:, :], E), ALU.mult).then_inc(pool2, 1)
                b.wait_apart(g, passed_g, pool2, 6, 4)
                g.tensor_tensor(G[:, :, :], G[:, :, :], gamma[:, :].unsqueeze(1).to_broadcast([P, IT, D]),
                                ALU.mult).then_inc(pool2, 2)
                b.wait_apart(g, passed_g, pool2, 6, 6)
                b.wait_apart(g, passed_g, s["xb"], 1, 1)
                b.dma_wait(g, stored, -1)
                g.tensor_tensor(XO[b.slot][:, :, :], G[:, :, :], XB[:, :, :], ALU.add).then_inc(s["out"], 1)

            pool2 = m.sem("pool2")

            def pre(b):
                normalised(b)
                g.wait_ge(s["setup_v"], 8)
                if first:
                    bias_added(b)
                rows(b)
                normalised(b + 1)

            def body(b):
                prev2, prev, nxt, nxt2 = around(b)
                if first and prev:
                    residual(b + -1)
                if nxt2 and not first:
                    normalised(b + 2)
                if nxt:
                    if first:
                        bias_added(b + 1)
                    rows(b + 1)
                if first and prev:
                    centred(b + -1)
                if nxt2 and first:
                    normalised(b + 2)
                if first and prev:
                    layernorm(b + -1)

            def after(b):
                if first:
                    residual(b)
                    centred(b)
                    layernorm(b)

            pipeline(g, nb, pre, body, after, SLOTS, 2, 1 if first else 2)


def typed_attention_phase(nc, nb, x_in, adj, weights, consts, kept, x_out):
    H, T = 4, 5
    E, N = D // H, 512
    IT = N // P
    ROWS = 2 * H * T
    with ExitStack() as ctx:
        m = Memory(nc, ctx, "ty")
        ident = m.sb("ident", [P, P])
        sel = m.sb("sel", [P, 2 + 2 * T * H])
        W = m.sb("W", [P, KC, D])
        bias, gamma, beta = (m.sb(n, [P, D]) for n in ("bias", "gamma", "beta"))
        odd = m.sb("odd", [P, 2])
        ones = m.sb("ones", [P, P])
        any_odd = m.sb("any_odd", [P, 1], I32)
        half = m.sb("half", [P, IT * H])
        X, XN, HS, G, SQ = (m.sb(n, [P, IT, D]) for n in ("X", "XN", "HS", "G", "SQ"))
        ADJ = m.sb("ADJ", [P, IT, N], I32)
        stats = m.sb("stats", [P, IT, 6])
        mv = m.sb("mv", [P, IT, 2])
        rstd = m.sb("rstd", [P, IT])
        XT = m.sb("XT", [P, KC, N])
        rows, left, right = (m.sb(n, [P, N]) for n in ("rows", "left", "right"))
        Z, TM, PR, PT = (m.sb(n, [P, IT, N]) for n in ("Z", "TM", "PR", "PT"))
        nmax, rsum, rinv = (m.sb(n, [P, IT]) for n in ("nmax", "rsum", "rinv"))
        sums = m.sb("sums", [P, IT * H])
        Zb = [m.ps(f"Z{k}") for k in range(IT)]
        Ab = [m.ps(f"A{k}") for k in range(2)]
        Eb = m.ps("E")
        s = {n: m.sem(n) for n in "const odd odd_pe var root loaded v xn xt_pe xt h_pe h right typed z p t ev pv g out stored passed".split()}
        ctx.push(m.clear)
        block = ctx.enter_context(nc.Block())
        flat = "p t d -> p (t d)"
        xv = x_in.rearrange("b (t p) d -> b p t d", p=P)
        av = adj.rearrange("b (t p) j -> b p t j", p=P)
        ov = x_out.rearrange("b (t p) d -> b p t d", p=P)

        def asked(eng):
            eng.wait_ge(s["odd"], 2)
            return eng.value_load(any_odd[0:1, 0:1], min_val=0, max_val=P) > 0

        def wait(eng, i, sem, per, nth):
            assert 1 <= nth <= per
            eng.wait_ge(s[sem], i * per + nth)
            eng.sem_inc(s["passed"], 1)

        @block.sync
        def _(sp):
            with sp.If(asked(sp)):
                sp.dma_start(ident[:, :], consts["identity"]).then_inc(s["const"], 16)
                sp.dma_start(sel[:, :], consts["typed_selectors"]).then_inc(s["const"], 16)
                for kc in range(KC):
                    sp.dma_start(W[:, kc, :].rearrange("k (h e) -> k h e", h=H),
                                 weights["W"][:, kc * P:(kc + 1) * P, :].rearrange("h k e -> k h e")
                                 ).then_inc(s["const"], 16)
                for tile, name in ((bias, "bias"), (gamma, "gamma"), (beta, "beta")):
                    sp.dma_start(tile[:, :], weights[name].rearrange("(o h) e -> o (h e)", o=1).to_broadcast([P, D])
                                 ).then_inc(s["const"], 16)
                with sp.Fori(0, nb) as i:
                    sp.dma_start(X[:, :, :], xv[i]).then_inc(s["loaded"], 16)
                    sp.dma_start(ADJ[:, :, :], av[i]).then_inc(s["loaded"], 16)
                    wait(sp, i, "out", 1, 1)
                    sp.dma_start(ov[i], G[:, :, :]).then_inc(s["stored"], 16)
                    wait(sp, i, "stored", 16, 16)

        @block.tensor
        def _(pe):
            pe.wait_ge(s["odd"], 1)
            pe.matmul(Eb[:, 0:1], ones[:, :], odd[:, 1:2], start=True, stop=True).then_inc(s["odd_pe"], 1)
            with pe.If(asked(pe)):
                pe.wait_ge(s["const"], 7 * 16)
                with pe.Fori(0, nb) as i:
                    wait(pe, i, "xn", 1, 1)
                    for kc in range(KC):
                        for t in range(IT):
                            ins = pe.transpose(Ab[kc][:, t * P:(t + 1) * P], XN[:, t, kc * P:(kc + 1) * P], ident[:, :])
                    ins.then_inc(s["xt_pe"], 1)
                    wait(pe, i, "xt", 1, 1)
                    for t in range(IT):
                        for kc in range(KC):
                            pe.matmul(Ab[t // 2][:, (t % 2) * D:(t % 2 + 1) * D], XT[:, kc, t * P:(t + 1) * P],
                                      W[:, kc, :], start=(kc == 0), stop=(kc == KC - 1))
                    for kc in range(KC):
                        ins = pe.matmul(Eb[0:ROWS, :], kept["WG"][:, kc, :], XT[:, kc, :],
                                        start=(kc == 0), stop=(kc == KC - 1))
                    ins.then_inc(s["h_pe"], 1)
                    for h in range(H):
                        for ty in range(T):
                            k = T * h + ty + 1
                            wait(pe, i, "right", H * T, k)
                            for t in range(IT):
                                ins = pe.matmul(Zb[t][:, :], left[0:ROWS, t * P:(t + 1) * P], right[0:ROWS, :],
                                                start=True, stop=True)
                            ins.then_inc(s["typed"], 1)
                        wait(pe, i, "p", H, h + 1)
                        for k in range(IT):
                            for t in range(IT):
                                ins = pe.transpose(Zb[k][:, t * P:(t + 1) * P], PR[:, t, k * P:(k + 1) * P], ident[:, :])
                        ins.then_inc(s["t"], 1)
                        wait(pe, i, "ev", H, h + 1)
                        for t in range(IT):
                            for k in range(IT):
                                ins = pe.matmul(Ab[0][:, t * E:(t + 1) * E], PT[:, k, t * P:(t + 1) * P],
                                                HS[:, k, h * E:(h + 1) * E], start=(k == 0), stop=(k == IT - 1))
                        ins.then_inc(s["pv"], 1)

        @block.gpsimd
        def _(g):
            with g.If(asked(g)):
                with g.Fori(0, nb) as i:
                    for k, tile in enumerate((rstd, sums)):
                        wait(g, i, "var", 2, k + 1)
                        g.tensor_tensor(tile[:, :], tile[:, :], half[:, 0:tile.shape[1]], ALU.pow).then_inc(s["root"], 1)

        @block.scalar
        def _(act):
            with act.If(asked(act)):
                with act.Fori(0, nb) as i:
                    for h in range(H):
                        wait(act, i, "z", H, h + 1)
                        for t in range(IT):
                            ins = act.activation(PR[:, t, :], Z[:, t, :], ACT.Exp, bias=nmax[:, t:t + 1],
                                                 accum_out=rsum[:, t:t + 1])
                        ins.then_inc(s["p"], 1)

        @block.vector
        def _(v):
            v.memset(ones[:, :], 1.0).then_inc(s["v"], 1)
            v.memset(half[:, :], -0.5).then_inc(s["v"], 1)
            v.tensor_reduce(odd[:, 0:1], kept["odd"][:, :], AX, ALU.add).then_inc(s["v"], 1)
            v.wait_ge(s["v"], 3)
            v.tensor_scalar(odd[:, 1:2], odd[:, 0:1], 0.25 * IT * N * nb, None, ALU.is_gt).then_inc(s["odd"], 1)
            v.wait_ge(s["odd_pe"], 1)
            v.tensor_copy(any_odd[:, :], Eb[:, 0:1]).then_inc(s["odd"], 1)
            with v.If(asked(v)):
                v.wait_ge(s["const"], 7 * 16)
                with v.Fori(0, nb) as i:
                    done = [0]
                    V = 6 + H * (2 * T - 1 + 4) + 10

                    def step(ins):
                        ins.then_inc(s["v"], 1)
                        done[0] += 1

                    def steps_done():
                        v.wait_ge(s["v"], i * V + (3 + done[0]))
                        v.sem_inc(s["passed"], 1)

                    wait(v, i, "loaded", 32, 32)
                    for t in range(IT):
                        ins = v.bn_stats(stats[:, t, :], X[:, t, :])
                    step(ins)
                    steps_done()
                    for t in range(IT):
                        ins = v.bn_aggr(mv[:, t, :], stats[:, t, :])
                    step(ins)
                    steps_done()
                    v.tensor_scalar(rstd[:, :], mv[:, :, 1], EPS_LN, None, ALU.add).then_inc(s["var"], 1)
                    wait(v, i, "root", 2, 1)
                    for t in range(IT):
                        ins = v.tensor_scalar(XN[:, t, :], X[:, t, :], mv[:, t, 0:1], rstd[:, t:t + 1],
                                              ALU.subtract, ALU.mult)
                    ins.then_inc(s["xn"], 1)
                    wait(v, i, "xt_pe", 1, 1)
                    v.tensor_copy(XT[:, 0, :], Ab[0][:, :])
                    v.tensor_copy(XT[:, 1, :], Ab[1][:, :]).then_inc(s["xt"], 1)
                    wait(v, i, "h_pe", 1, 1)
                    for g in range(2):
                        step(v.tensor_copy(HS[:, 2 * g:2 * g + 2, :].rearrange(flat), Ab[g][:, :]))
                    step(v.tensor_copy(rows[0:ROWS, :], Eb[0:ROWS, :]))
                    steps_done()
                    step(v.tensor_scalar(left[0:ROWS, :], rows[0:ROWS, :], sel[0:ROWS, 0:1], sel[0:ROWS, 1:2],
                                         ALU.mult, ALU.add))
                    for h in range(H):
                        for ty in range(T):
                            steps_done()
                            c = 2 + 2 * (H * ty + h)
                            v.tensor_scalar(right[0:ROWS, :], rows[0:ROWS, :], sel[0:ROWS, c:c + 1],
                                            sel[0:ROWS, c + 1:c + 2], ALU.mult, ALU.add).then_inc(s["right"], 1)
                            wait(v, i, "typed", H * T, T * h + ty + 1)
                            into = TM if ty else Z
                            for t in range(IT):
                                ins = v.scalar_tensor_tensor(out=into[:, t, :], in0=ADJ[:, t, :], scalar=ty + 1.0,
                                                             in1=Zb[t][:, :], op0=ALU.is_equal, op1=ALU.mult)
                            step(ins)
                            if ty:
                                steps_done()
                                step(v.tensor_tensor(Z[:, :, :].rearrange(flat), Z[:, :, :].rearrange(flat),
                                                     TM[:, :, :].rearrange(flat), ALU.add))
                        steps_done()
                        Zf, TMf, Af = (b[:, :, :].rearrange(flat) for b in (Z, TM, ADJ))
                        step(v.tensor_scalar(TMf, Af, 0.0, NEG, ALU.is_equal, ALU.mult))
                        step(v.scalar_tensor_tensor(out=Zf, in0=Zf, scalar=0.01, in1=Zf, op0=ALU.mult, op1=ALU.max))
                        steps_done()
                        step(v.tensor_tensor(Zf, Zf, TMf, ALU.add))
                        steps_done()
                        v.tensor_reduce(nmax[:, :], Z[:, :, :], AX, ALU.max, negate=True).then_inc(s["z"], 1)
                        wait(v, i, "p", H, h + 1)
                        step(v.reciprocal(rinv[:, :], rsum[:, :]))
                        wait(v, i, "t", H, h + 1)
                        for k in range(IT):
                            ins = v.tensor_copy(PT[:, k, :], Zb[k][:, :])
                        ins.then_inc(s["ev"], 1)
                        wait(v, i, "pv", H, h + 1)
                        steps_done()
                        v.tensor_tensor(G[:, :, h * E:(h + 1) * E], Ab[0][:, 0:IT * E].rearrange("p (t e) -> p t e", t=IT),
                                        bcast(rinv[:, :], E), ALU.mult).then_inc(s["g"], 1)
                    wait(v, i, "g", H, H)
                    over = lambda a: a[:, :].unsqueeze(1).to_broadcast([P, IT, D])
                    heads = "p t (h e) -> p (t h) e"
                    Gh, Sh = G[:, :, :].rearrange(heads, h=H), SQ[:, :, :].rearrange(heads, h=H)
                    step(v.tensor_tensor(G[:, :, :], G[:, :, :], over(bias), ALU.add))
                    steps_done()
                    step(v.scalar_tensor_tensor(out=G[:, :, :].rearrange(flat), in0=G[:, :, :].rearrange(flat), scalar=0.0,
                                                in1=HS[:, :, :].rearrange(flat), op0=ALU.max, op1=ALU.add))
                    steps_done()
                    for power in (1, 2):
                        if power == 2:
                            step(v.tensor_tensor(SQ[:, :, :], G[:, :, :], G[:, :, :], ALU.mult))
                            steps_done()
                        step(v.tensor_reduce(sums[:, :], Gh if power == 1 else Sh, AX, ALU.add))
                        steps_done()
                        ins = v.tensor_scalar(sums[:, :], sums[:, :], 1.0 / E, 0.0 if power == 1 else 1e-6,
                                              ALU.mult, ALU.add)
                        if power == 1:
                            step(ins)
                            steps_done()
                        else:
                            ins.then_inc(s["var"], 1)
                            wait(v, i, "root", 2, 2)
                        step(v.tensor_tensor(Gh, Gh, bcast(sums[:, :], E), ALU.subtract if power == 1 else ALU.mult))
                        steps_done()
                    step(v.tensor_tensor(G[:, :, :], G[:, :, :], over(gamma), ALU.mult))
                    steps_done()
                    step(v.tensor_tensor(G[:, :, :], G[:, :, :], over(beta), ALU.add))
                    steps_done()
                    v.tensor_tensor(G[:, :, :], G[:, :, :], X[:, :, :], ALU.add).then_inc(s["out"], 1)
                    V_MADE = done[0]
                    assert V_MADE == V, (V_MADE, V)


def state_space_phase(nc, nb, x_in, w, consts, x_out):
    N, T = 512, 4
    DI, DS, NH, HD = 512, 64, 8, 64
    CT = DI // P
    EPS = 1e-5
    PAIRS = NH // 2
    PACK = [[(0, 0, 0, 512)], [(0, 1, 0, 384), (0, 3, 384, 128)], [(1, 0, 0, 512)],
            [(1, 1, 0, 384), (1, 3, 384, 128)], [(0, 2, 0, 256), (1, 2, 256, 256)]]
    GKIND = [0, 1, 0, 1, 2]
    NZ = len(PACK)
    ITEMS = PAIRS * NZ
    NM = 2 * NZ
    NE = 4
    PROJ = ["dt", "bc"] + [("x", c) for c in range(CT)] + [("z", c) for c in range(CT)]
    NP = len(PROJ)
    with ExitStack() as ctx:
        m = Memory(nc, ctx, "ssm")
        ident = m.sb("ident", [P, P])
        ident_bf = m.sb("ident_bf", [P, P], BF16)
        causal = m.sb("causal", [P, P])
        causal_bf = m.sb("causal_bf", [P, P], BF16)
        sel = m.sb("sel", [P, 2 + 2 * NH])
        ones = m.sb("ones", [P, N])
        half = m.sb("half", [P, 16])
        W_in = m.sb("W_in", [P, KC, 2 * DI + 2 * DS])
        Wdt = m.sb("Wdt", [P, KC, P])
        Wc = m.sb("Wc", [P, CT, D])
        cw = m.sb("cw", [P, CT + 1, 4])
        cb = m.sb("cb", [P, CT + 1])
        skip = m.sb("skip", [P, CT])
        normw = m.sb("normw", [P, CT])
        dtb = m.sb("dtb", [P, 1])
        alog = m.sb("alog", [P, 1])
        aexp = m.sb("aexp", [P, 1])
        sign = m.sb("sign", [P, 1])
        blin = m.sb("blin", [P, D])
        X = [m.sb(f"X{k}", [P, T, D]) for k in range(2)]
        stats = m.sb("stats", [P, T, 6])
        mv = m.sb("mv", [P, T, 2])
        rstd = m.sb("rstd", [P, T])
        XN = m.sb("XN", [P, T, D])
        XT = m.sb("XT", [P, KC, N])
        sp_abs = m.sb("sp_abs", [P, N])
        sp_pos = m.sb("sp_pos", [P, N])
        dA = rest = sp_pos
        DT = m.sb("DT", [P, N])
        AC = m.sb("AC", [P, N])
        parts = m.sb("parts", [P, N], BF16)
        dtt = m.sb("dtt", [P, T, NH])
        L = [m.sb(f"L{k}", [P, N], BF16) for k in range(2)]
        R = [m.sb(f"R{k}", [P, NH, N], BF16) for k in range(2)]
        CV = [m.sb(f"CV{k}", [P, N]) for k in range(3)]
        TH = [m.sb(f"TH{k}", [P, N]) for k in range(2)]
        THZ = [m.sb(f"THZ{k}", [P, N]) for k in range(2)]
        BP = m.sb("BP", [P, N])
        CP = m.sb("CP", [P, N])
        XC = [m.sb(f"XC{k}", [P, CT, N]) for k in range(2)]
        ZS = [m.sb(f"ZS{k}", [P, CT, N]) for k in range(2)]
        XD = [m.sb(f"XD{k}", [P, T, DI]) for k in range(2)]
        G = [m.sb(f"G{k}", [P, 3, N]) for k in range(2)]
        EX = [m.sb(f"EX{k}", [P, N]) for k in range(NE)]
        M = [m.sb(f"M{k}", [P, N]) for k in range(NM)]
        Y = m.sb("Y", [P, CT, N])
        SQ = [m.sb(f"SQ{k}", [P, N]) for k in range(2)]
        SS = m.sb("SS", [P, N])
        rms = m.sb("rms", [P, T])
        OUT = m.sb("OUT", [P, T, D])
        RES = [m.sb(f"RES{k}", [P, T, D]) for k in range(2)]
        W_out, WoT = OUT, Y[:, 0:KC, :]
        W_lin = Y[:, KC, :].rearrange("p (c d) -> p c d", c=KC)
        Zb = [m.ps(f"Z{k}") for k in range(2)]
        Yb = [m.ps(f"Y{k}") for k in range(2)]
        Jb = [m.ps(f"J{k}") for k in range(2)]
        Ab = [m.ps(f"A{k}") for k in range(2)]
        names = ("zero w setup_pe setup_v setup_a st mv rstd xn xt_pe xt pj conv tap th thz silu zs sp_a sp_b sp_c "
                 "spr dt dA ac s1 s2 s3 s4 parts dtt_pe dtt lr g_pe gr xd_pe xd z ex m y y1 y2 sq ss ss_pe ssr "
                 "rms1 rms o_pe o xb out stored").split()
        s = {n: m.sem(n) for n in names}
        x_loaded = [m.sem(f"x_loaded{k}") for k in range(2)]
        xv = x_in.rearrange("b (t p) d -> b p t d", p=P)
        ov = x_out.rearrange("b (t p) d -> b p t d", p=P)
        flat = "p t d -> p (t d)"
        TAPS = 3 * (CT + 1)

        def bank_read(b, eng, k):
            if k < 0:
                b.wait(eng, s["zs"], CT, k + 1)
            elif k == 0:
                b.wait(eng, s["spr"], 1, 1)
            elif k <= CT + 1:
                b.wait(eng, s["tap"], TAPS, 3 * k)
            else:
                b.wait(eng, s["zs"], CT, k - CT - 1)

        passed_v, passed_g, passed_pe, passed_a = (m.sem(f"passed_{n}") for n in ("v", "g", "pe", "act"))
        ctx.push(m.clear)
        block = ctx.enter_context(nc.Block())

        @block.sync
        def _(sp):
            n = 0

            def put(dst, src, **kw):
                nonlocal n
                n += 1
                sp.dma_start(dst, src, **kw).then_inc(s["w"], 16)

            sp.dma_start(X[0][:, :, :], xv[0]).then_inc(x_loaded[0], 16)
            put(ident[:, :], consts["identity"])
            put(causal[:, :], consts["causal"])
            put(sel[:, :], consts["decay_selectors"])
            put(W_in[:, :, :], w["W_in"].rearrange("(c k) e -> k c e", k=P)[:, :, 0:2 * DI + 2 * DS])
            put(W_out[:, :, :], w["W_out"].rearrange("(c k) e -> k c e", k=P))
            put(W_lin[:, :, :], w["W_lin"].rearrange("(c k) e -> k c e", k=P))
            put(cw[:, :, :], w["conv_w"].rearrange("(c k) e -> k c e", k=P))
            put(cb[:, :], w["conv_b"].rearrange("(c k) -> k c", k=P), allow_slow_non_contiguous=True)
            put(normw[:, :], w["norm_w"].rearrange("(c k) -> k c", k=P), allow_slow_non_contiguous=True)
            put(blin[:, :], w["b_lin"].rearrange("(o d) -> o d", o=1).to_broadcast([P, D]))
            for h in range(2):
                put(skip[HD * h:HD * (h + 1), :],
                    w["D"].rearrange("(o c h) -> o c h", o=1, h=2)[:, :, h].to_broadcast([HD, CT]),
                    allow_slow_non_contiguous=True)
            assert n + 3 * 2 * 3 == N_W

            def load(b):
                b.wait(sp, s["xn"], T, -T)
                b.wait(sp, s["xb"], 1, -1)
                sp.dma_start(X[b.slot][:, :, :], xv[b.index()]).then_inc(x_loaded[b.slot], 16)

            def before(b):
                load(b + 1)

            def body(b):
                if b.reg is not None or b.off < nb - 2:
                    load(b + 2)
                if b.reg is not None or b.off > 0:
                    store(b + -1)

            def store(b):
                b.wait(sp, s["out"], 1, 1)
                sp.dma_start(ov[b.index()], OUT[:, :, :]).then_inc(s["stored"], 16)

            pipeline(sp, nb, before, body, store, 2, 2)
            sp.wait_ge(s["stored"], 16 * nb)

        @block.tensor
        def _(pe):
            pe.wait_ge(s["w"], 16 * N_W)
            for kc in range(KC):
                for c in range(CT):
                    ins = pe.transpose(Zb[kc][:, c * P:(c + 1) * P], W_out[:, c, kc * P:(kc + 1) * P], ident[:, :])
            ins.then_inc(s["setup_pe"], 1)
            pe.wait_ge(s["setup_v"], 2)
            for c in range(CT):
                for kc in range(KC):
                    ins = pe.matmul(Jb[c // 2][:, (c % 2) * D:(c % 2 + 1) * D], WoT[:, kc, c * P:(c + 1) * P],
                                    W_lin[:, kc, :], start=(kc == 0), stop=(kc == KC - 1))
            ins.then_inc(s["setup_pe"], 1)
            pe.wait_ge(s["setup_v"], 8)

            def xn_turned(b):
                b.wait(pe, s["xn"], T, T)
                b.wait(pe, s["xd"], T, 0)
                for kc in range(KC):
                    for t in range(T):
                        ins = pe.transpose(Ab[1 - kc][:, t * P:(t + 1) * P], XN[:, t, kc * P:(kc + 1) * P],
                                           ident[:, :])
                    ins.then_inc(s["xt_pe"], 1)

            def project(b, k):
                if k == 0:
                    b.wait(pe, s["xt"], 2, 2)
                bank_read(b, pe, k - 2)
                what = PROJ[k]
                for kc in range(KC):
                    if what == "dt":
                        lhs = Wdt[:, kc, :]
                    else:
                        c = 2 * DI if what == "bc" else (DI if what[0] == "x" else 0) + what[1] * P
                        lhs = W_in[:, kc, c:c + P]
                    ins = pe.matmul(Jb[k % 2][:, :], lhs, XT[:, kc, :], start=(kc == 0), stop=(kc == KC - 1))
                ins.then_inc(s["pj"], 1)

            def dt_turned(b):
                b.wait(pe, s["dt"], 1, 1)
                b.wait_apart(pe, passed_pe, s["xt"], 2, 2)
                b.wait_apart(pe, passed_pe, s["o"], 2, -3)
                for t in range(T):
                    ins = pe.transpose(Ab[1][:, NH * t:NH * (t + 1)], DT[0:NH, t * P:(t + 1) * P],
                                       ident[0:NH, 0:NH])
                ins.then_inc(s["dtt_pe"], 1)

            def products(b, gs):
                b.wait(pe, s["silu"], 6, 2)
                b.wait(pe, s["o"], 2, -2)
                for g in gs:
                    if g == 1:
                        b.wait(pe, s["dtt"], 1, 1)
                    if g == 2:
                        b.wait(pe, s["gr"], 4, 1)
                    for (_, t, c, n) in (PACK[0], PACK[1], PACK[4][0:1])[g]:
                        ins = pe.matmul(Ab[g % 2][:, c:c + n], BP[:, t * P:(t + 1) * P], CP[:, t * P:],
                                        start=True, stop=True, skip_group_check=True)
                    ins.then_inc(s["g_pe"], 1)

            def x_turned(b, t):
                b.wait(pe, s["silu"], 6, 6)
                if t < 2:
                    b.wait(pe, s["gr"], 4, 2 if t == 0 else 4)
                else:
                    b.wait(pe, s["xd"], T, t - 1)
                for c in range(CT):
                    ins = pe.transpose(Ab[1 - t % 2][:, c * P:(c + 1) * P], XC[b.slot][:, c, t * P:(t + 1) * P],
                                       ident[:, :])
                ins.then_inc(s["xd_pe"], 1)

            def exponents(b, n):
                q, i = n // NZ, n % NZ
                if n == 0:
                    b.wait(pe, s["lr"], NH + 1, NH + 1)
                b.wait(pe, s["ex"], ITEMS, n - 1)
                for (hh, t, c, cols) in PACK[i]:
                    pe.matmul(Zb[n % 2][:, c:c + cols], L[b.slot][:, t * P:(t + 1) * P],
                              R[b.slot][:, 2 * q + hh, t * P:], start=True, stop=False, skip_group_check=True)
                    ins = pe.matmul(Zb[n % 2][:, c:c + P], ident_bf[:, :], causal_bf[:, :],
                                    start=False, stop=True, skip_group_check=True)
                ins.then_inc(s["z"], 1)

            def outputs(b, q):
                b.wait(pe, s["m"], ITEMS, NZ * (q + 1))
                b.wait(pe, s["y1"], PAIRS, q - 1)
                if q == 0:
                    b.wait(pe, s["xd"], T, T)
                where = {(hh, t): (i, c, cols) for i, p in enumerate(PACK) for (hh, t, c, cols) in p}
                for t in range(T):
                    for hh in range(2):
                        i, c, cols = where[hh, t]
                        h = 2 * q + hh
                        ins = pe.matmul(Yb[q % 2][HD * hh:HD * (hh + 1), t * P:], XD[b.slot][:, t, HD * h:HD * (h + 1)],
                                        M[(NZ * q + i) % NM][:, c:c + cols], start=(t == 0), stop=(t == T - 1),
                                        skip_group_check=True)
                ins.then_inc(s["y"], 1)

            def sums(b):
                b.wait(pe, s["ss"], PAIRS - 1, PAIRS - 1)
                for t in range(T):
                    ins = pe.matmul(Ab[0][:, t:t + 1], SS[:, t * P:(t + 1) * P], ones[:, 0:1], start=True, stop=True)
                ins.then_inc(s["ss_pe"], 1)

            def result(b, g):
                if g == 1:
                    b.wait(pe, s["ssr"], 1, 1)
                for t in (2 * g, 2 * g + 1):
                    for c in range(CT):
                        ins = pe.matmul(Ab[1 - g][:, (t % 2) * D:(t % 2 + 1) * D], Y[:, c, t * P:(t + 1) * P],
                                        Wc[:, c, :], start=(c == 0), stop=(c == CT - 1))
                ins.then_inc(s["o_pe"], 1)

            def pre(b):
                xn_turned(b)
                for k in range(NP):
                    project(b, k)
                    if k == 1:
                        dt_turned(b)
                products(b, (0, 1, 2))
                for t in range(T):
                    x_turned(b, t)

            def body(b):
                some = b.reg is not None
                nxt, prev = some or b.off < nb - 1, some or b.off > 0
                for n in range(ITEMS):
                    exponents(b, n)
                    if prev:
                        if n == 1:
                            outputs(b + -1, PAIRS - 1)
                        if n == 5:
                            (b + 1).wait(pe, s["xt"], 2, 2) if nxt else None
                            sums(b + -1)
                    if nxt:
                        if n == 0:
                            xn_turned(b + 1)
                        if n == 9:
                            dt_turned(b + 1)
                        if 0 <= n - 2 < NP:
                            project(b + 1, n - 2)
                    if prev and n == 6:
                        result(b + -1, 0)
                    if prev and n == 7:
                        result(b + -1, 1)
                    if nxt:
                        if n == 10:
                            b.wait(pe, s["o"], 2, 0)
                            products(b + 1, (0, 1))
                        if n == 12:
                            products(b + 1, (2,))
                        if 13 <= n < 13 + T:
                            x_turned(b + 1, n - 13)
                    if n >= 6 and (n - 6) % NZ == 0:
                        outputs(b, (n - 6) // NZ)

            def after(b):
                outputs(b, PAIRS - 1)
                sums(b)
                result(b, 0)
                result(b, 1)

            pipeline(pe, nb, pre, body, after, 2, 2)

        @block.scalar
        def _(act):
            act.wait_ge(s["zero"], 4)
            wdt = w["W_in"].rearrange("(c k) e -> k c e", k=P)[:, :, 2 * DI + 2 * DS:]
            for q in (0, 64, 96):
                for r in (q, q + NH):
                    act.dma_start(Wdt[:, :, r:r + NH], wdt).then_inc(s["w"], 16)
                    act.dma_start(dtb[r:r + NH, :], w["dt_bias"].rearrange("(h o) -> h o", o=1)).then_inc(s["w"], 16)
                    act.dma_start(alog[r:r + NH, :], w["A_log"].rearrange("(h o) -> h o", o=1)).then_inc(s["w"], 16)
            act.wait_ge(s["w"], 16 * N_W)
            act.activation(aexp[:, :], alog[:, :], ACT.Exp).then_inc(s["setup_a"], 1)
            act.wait_ge(s["setup_v"], 8)

            def xt_out(b):
                b.wait(act, s["pj"], NP, 0)
                for kc in range(KC):
                    b.wait(act, s["xt_pe"], 2, kc + 1)
                    act.activation(XT[:, kc, :], Ab[1 - kc][:, :], ACT.Copy).then_inc(s["xt"], 1)

            def softplus_abs(b):
                b.wait(act, s["pj"], NP, 1)
                b.wait(act, s["dt"], 1, 0)
                act.activation(sp_abs[:, :], Jb[0][:, :], ACT.Abs, bias=dtb[:, :]).then_inc(s["sp_a"], 1)

            def softplus_log(b):
                b.wait(act, s["sp_a"], 1, 1)
                act.activation(sp_abs[:, :], sp_abs[:, :], ACT.Exp, scale=-1.0).then_inc(s["sp_b"], 1)
                b.wait(act, s["sp_b"], 1, 1)
                act.activation(sp_abs[:, :], sp_abs[:, :], ACT.Ln, bias=1.0).then_inc(s["sp_c"], 1)

            def conv_first(b, k):
                c = CT if k == 1 else k - 2
                b.wait(act, s["pj"], NP, k + 1)
                b.wait(act, s["silu"], CT + 2, k - 2 if k > 3 else 0)
                act.activation(CV[k % 3][:, :], Jb[k % 2][:, :], ACT.Identity, scale=cw[:, c, 3:4],
                               bias=cb[:, c:c + 1]).then_inc(s["conv"], 1)

            def tanh_conv(b, k):
                b.wait(act, s["tap"], TAPS, 3 * k)
                b.wait(act, s["silu"], CT + 2, k - 1 if k > 2 else 0)
                act.activation(TH[k % 2][:, :], CV[k % 3][:, :], ACT.Tanh, scale=0.5).then_inc(s["th"], 1)

            def tanh_z(b, k):
                b.wait(act, s["pj"], NP, k + 1)
                b.wait(act, s["zs"], CT, k - CT - 3)
                act.activation(THZ[k % 2][:, :], Jb[k % 2][:, :], ACT.Tanh, scale=0.5).then_inc(s["thz"], 1)

            def products_out(b, gs):
                for g in gs:
                    b.wait(act, s["g_pe"], 3, g + 1)
                    for c in ((0, N),) if g < 2 else ((0, N // 2), (N // 2, N)):
                        n = c[1] - c[0]
                        act.activation(G[b.slot][:, g, c[0]:c[1]], Ab[g % 2][:, 0:n], ACT.Copy,
                                       scale=0.125).then_inc(s["gr"], 1)

            def decay(b, n):
                b.wait(act, s["z"], ITEMS, n + 1)
                b.wait(act, s["m"], ITEMS, n + 1 - NE)
                act.activation(EX[n % NE][:, :], Zb[n % 2][:, :], ACT.Exp).then_inc(s["ex"], 1)

            def square(b, q):
                b.wait(act, s["y2"], PAIRS, q + 1)
                b.wait(act, s["ss"], PAIRS - 1, max(q - 2, 0) if q else -1)
                act.activation((SS if q == 0 else SQ[q % 2])[:, :], Y[:, q, :], ACT.Square).then_inc(s["sq"], 1)

            def result_out(b):
                b.wait(act, s["rms"], 1, 1)
                b.wait(act, s["stored"], 16, 0)
                for t in range(T):
                    g = t // 2
                    b.wait(act, s["o_pe"], 2, g + 1)
                    ins = act.activation(OUT[:, t, :], Ab[1 - g][:, (t % 2) * D:(t % 2 + 1) * D], ACT.Copy,
                                         scale=rms[:, t:t + 1])
                    if t % 2:
                        ins.then_inc(s["o"], 1)

            def pre(b):
                xt_out(b)
                softplus_abs(b)
                softplus_log(b)
                for k in range(1, NP):
                    if k <= CT + 1:
                        conv_first(b, k)
                        tanh_conv(b, k)
                    else:
                        tanh_z(b, k)
                products_out(b, (0, 1, 2))

            def body(b):
                some = b.reg is not None
                nxt, prev = some or b.off < nb - 1, some or b.off > 0
                for n in range(ITEMS):
                    decay(b, n)
                    if prev and n == 3:
                        square(b + -1, PAIRS - 1)
                    if nxt:
                        if n == 1:
                            xt_out(b + 1)
                        if n == 3:
                            softplus_abs(b + 1)
                        if 1 <= n - 3 <= CT + 1:
                            conv_first(b + 1, n - 3)
                        if 1 <= n - 4 <= CT + 1:
                            tanh_conv(b + 1, n - 4)
                        if CT + 1 < n - 3 < NP:
                            tanh_z(b + 1, n - 3)
                        if n == 5:
                            softplus_log(b + 1)
                        if n == 10:
                            products_out(b + 1, (0, 1))
                        if n == 12:
                            products_out(b + 1, (2,))
                    if prev and n == 8:
                        result_out(b + -1)
                    if n == 10:
                        square(b, 0)
                    if n > 8 and (n - 8) % NZ == 0:
                        square(b, (n - 8) // NZ)

            def after(b):
                square(b, PAIRS - 1)
                result_out(b)

            pipeline(act, nb, pre, body, after, 2, 2)

        @block.vector
        def _(v):
            v.memset(Wdt[:, :, :], 0.0).then_inc(s["zero"], 1)
            v.memset(dtb[:, :], 0.0).then_inc(s["zero"], 1)
            v.memset(alog[:, :], 0.0).then_inc(s["zero"], 1)
            v.memset(BP[:, :], 0.0).then_inc(s["zero"], 1)
            v.memset(CP[:, :], 0.0)
            v.memset(ones[:, :], 1.0)
            v.memset(half[:, :], -0.5)
            v.wait_ge(s["setup_pe"], 1)
            for kc in range(KC):
                v.tensor_copy(WoT[:, kc, :], Zb[kc][:, :]).then_inc(s["setup_v"], 1)
            v.wait_ge(s["w"], 16 * N_W)
            v.tensor_copy(ident_bf[:, :], ident[:, :]).then_inc(s["setup_v"], 1)
            v.tensor_copy(causal_bf[:, :], causal[:, :]).then_inc(s["setup_v"], 1)
            v.tensor_scalar(skip[:, :], skip[:, :], 0.5, None, ALU.mult).then_inc(s["setup_v"], 1)
            v.wait_ge(s["setup_a"], 1)
            v.tensor_scalar(sign[:, :], sel[:, 0:1], 1.0, sel[:, 1:2], ALU.mult, ALU.subtract
                            ).then_inc(s["setup_v"], 1)
            v.wait_ge(s["setup_v"], 6)
            v.tensor_tensor(aexp[:, :], aexp[:, :], sign[:, :], ALU.mult).then_inc(s["setup_v"], 1)
            v.wait_ge(s["setup_pe"], 2)
            for c in range(CT):
                ins = v.tensor_scalar(Wc[:, c, :], Jb[c // 2][:, (c % 2) * D:(c % 2 + 1) * D], normw[:, c:c + 1],
                                      None, ALU.mult)
            ins.then_inc(s["setup_v"], 1)
            v.wait_ge(s["setup_v"], 8)

            def norm_stats(b):
                b.dma_wait(v, x_loaded)
                b.wait(v, s["xn"], T, 0)
                for t in range(T):
                    ins = v.bn_stats(stats[:, t, :], X[b.slot][:, t, :])
                ins.then_inc(s["st"], 1)
                b.wait_apart(v, passed_v, s["st"], 1, 1)
                for t in range(T):
                    ins = v.bn_aggr(mv[:, t, :], stats[:, t, :])
                ins.then_inc(s["mv"], 1)

            def relu_steps(b):
                b.wait(v, s["sp_a"], 1, 1)
                b.wait(v, s["parts"], 1, 0)
                v.tensor_scalar(sp_pos[:, :], Jb[0][:, :], dtb[:, 0:1], 0.0, ALU.add, ALU.max).then_inc(s["spr"], 1)

            def steps(b, stages=(0, 1, 2)):
                if 0 in stages:
                    b.wait(v, s["sp_c"], 1, 1)
                    b.wait(v, s["dtt_pe"], 1, 0)
                    b.wait(v, s["spr"], 1, 1)
                    v.tensor_tensor(DT[:, :], sp_pos[:, :], sp_abs[:, :], ALU.add).then_inc(s["dt"], 1)
                    b.wait(v, s["dt"], 1, 1)
                    v.tensor_scalar(dA[:, :], DT[:, :], aexp[:, 0:1], None, ALU.mult).then_inc(s["dA"], 1)
                if 1 in stages:
                    b.wait(v, s["dA"], 1, 1)
                    v.tensor_tensor_scan(AC[:, :], ones[:, :], dA[:, :], 0.0, ALU.mult, ALU.add).then_inc(s["ac"], 1)
                    b.wait(v, s["ac"], 1, 1)
                    b.wait(v, s["lr"], NH + 1, 0)
                    v.tensor_copy(parts[:, :], AC[:, :]).then_inc(s["s1"], 1)
                    b.wait(v, s["s1"], 1, 1)
                    v.tensor_tensor(rest[64:P, :], AC[64:P, :], parts[64:P, :], ALU.subtract).then_inc(s["s2"], 1)
                if 2 in stages:
                    b.wait(v, s["s2"], 1, 1)
                    v.tensor_copy(parts[64:P, :], rest[64:P, :]).then_inc(s["s3"], 1)
                    b.wait(v, s["s3"], 1, 1)
                    v.tensor_tensor(rest[96:P, :], rest[96:P, :], parts[96:P, :], ALU.subtract).then_inc(s["s4"], 1)
                    b.wait(v, s["s4"], 1, 1)
                    v.tensor_copy(parts[96:P, :], rest[96:P, :]).then_inc(s["parts"], 1)

            def dt_out(b):
                b.wait(v, s["dtt_pe"], 1, 1)
                b.wait(v, s["xd"], T, 0)
                v.tensor_copy(dtt[:, :, :].rearrange("p t h -> p (t h)"), Ab[1][:, 0:T * NH]).then_inc(s["dtt"], 1)

            def taps(b, k):
                c = CT if k == 1 else k - 2
                b.wait(v, s["conv"], CT + 1, k)
                for j in range(1, 4):
                    b.wait(v, s["tap"], TAPS, 3 * (k - 1) + j - 1)
                    v.scalar_tensor_tensor(out=CV[k % 3][:, j:], in0=Jb[k % 2][:, 0:N - j], scalar=cw[:, c, 3 - j:4 - j],
                                           in1=CV[k % 3][:, j:], op0=ALU.mult, op1=ALU.add).then_inc(s["tap"], 1)

            def silu_conv(b, k):
                b.wait(v, s["th"], CT + 1, k)
                if k == 1:
                    b.wait(v, s["g_pe"], 3, 0)
                    for r, dst in ((0, BP), (64, CP)):
                        ins = v.scalar_tensor_tensor(out=dst[0:64, :], in0=TH[1][r:r + 64, :], scalar=1.0,
                                                     in1=CV[1][r:r + 64, :], op0=ALU.add, op1=ALU.mult)
                        ins.then_inc(s["silu"], 1)
                    v.wait_ge(s["zero"], 4)
                else:
                    b.wait(v, s["y1"], PAIRS, -PAIRS)
                    ins = v.scalar_tensor_tensor(out=XC[b.slot][:, k - 2, :], in0=TH[k % 2][:, :], scalar=1.0,
                                                 in1=CV[k % 3][:, :], op0=ALU.add, op1=ALU.mult)
                    ins.then_inc(s["silu"], 1)

            def silu_z(b, k):
                b.wait(v, s["thz"], CT, k - CT - 1)
                b.wait(v, s["y2"], PAIRS, -PAIRS)
                v.scalar_tensor_tensor(out=ZS[b.slot][:, k - CT - 2, :], in0=THZ[k % 2][:, :], scalar=1.0,
                                       in1=Jb[k % 2][:, :], op0=ALU.add, op1=ALU.mult).then_inc(s["zs"], 1)

            def x_dt(b, t):
                b.wait(v, s["xd_pe"], T, t + 1)
                b.wait(v, s["dtt"], 1, 1)
                b.wait(v, s["y"], PAIRS, -PAIRS)
                v.tensor_tensor(XD[b.slot][:, t, :].rearrange("p (h e) -> p h e", h=NH),
                                Ab[1 - t % 2][:, :].rearrange("p (h e) -> p h e", h=NH), bcast(dtt[:, t, :], HD),
                                ALU.mult).then_inc(s["xd"], 1)

            def decayed(b, n):
                q, i = n // NZ, n % NZ
                b.wait(v, s["ex"], ITEMS, n + 1)
                if n == 0:
                    b.wait(v, s["gr"], 4, 4)
                b.wait(v, s["y"], PAIRS, q - 1)
                v.tensor_tensor(M[n % NM][:, :], EX[n % NE][:, :], G[b.slot][:, GKIND[i], :], ALU.mult
                                ).then_inc(s["m"], 1)

            def gated(b, q):
                b.wait(v, s["y"], PAIRS, q + 1)
                if q == 0:
                    b.wait(v, s["o_pe"], 2, 0)
                v.scalar_tensor_tensor(out=Y[:, q, :], in0=XC[b.slot][:, q, :], scalar=skip[:, q:q + 1],
                                       in1=Yb[q % 2][:, :], op0=ALU.mult, op1=ALU.add).then_inc(s["y1"], 1)
                b.wait(v, s["y1"], PAIRS, q + 1)
                v.tensor_tensor(Y[:, q, :], Y[:, q, :], ZS[b.slot][:, q, :], ALU.mult).then_inc(s["y2"], 1)

            def mean_square(b):
                b.wait(v, s["ss_pe"], 1, 1)
                b.wait(v, s["o"], 2, 0)
                v.tensor_scalar(rms[:, :], Ab[0][:, 0:T], 0.25 / DI, EPS, ALU.mult, ALU.add).then_inc(s["ssr"], 1)

            def pre(b):
                norm_stats(b)
                for k in range(NP):
                    if k == 0:
                        relu_steps(b)
                        steps(b)
                    elif k <= CT + 1:
                        taps(b, k)
                        silu_conv(b, k)
                    else:
                        silu_z(b, k)
                    if k == 1:
                        dt_out(b)
                for t in range(T):
                    x_dt(b, t)
                norm_stats(b + 1)

            def body(b):
                some = b.reg is not None
                nxt, prev = some or b.off < nb - 1, some or b.off > 0
                nxt2 = some or b.off < nb - 2
                for n in range(ITEMS):
                    if nxt:
                        if 14 <= n < 14 + T:
                            x_dt(b + 1, n - 14)
                        if n == 3:
                            relu_steps(b + 1)
                        if CT + 1 < n - 3 < NP:
                            silu_z(b + 1, n - 3)
                        if 1 <= n - 3 <= CT + 1:
                            taps(b + 1, n - 3)
                        if n == 9:
                            dt_out(b + 1)
                    if n == 0:
                        if prev:
                            decayed(b + -1, ITEMS - 1)
                    else:
                        decayed(b, n - 1)
                    if nxt:
                        if n in (5, 6, 7):
                            steps(b + 1, (n - 5,))
                        if 1 <= n - 4 <= CT + 1:
                            silu_conv(b + 1, n - 4)
                    if prev:
                        if n == 2:
                            gated(b + -1, PAIRS - 1)
                        if n == 6:
                            mean_square(b + -1)
                    if nxt2 and n == 11:
                        norm_stats(b + 2)
                    if n == 9:
                        gated(b, 0)
                    if n > 7 and (n - 7) % NZ == 0:
                        gated(b, (n - 7) // NZ)

            def after(b):
                decayed(b, ITEMS - 1)
                gated(b, PAIRS - 1)
                mean_square(b)

            pipeline(v, nb, pre, body, after, 2, 2)

        @block.gpsimd
        def _(g):
            g.wait_ge(s["setup_v"], 8)

            def normalised(b):
                b.wait_apart(g, passed_g, s["mv"], 1, 1)
                b.wait_apart(g, passed_g, s["xt_pe"], 2, 0)
                g.tensor_scalar(rstd[:, :], mv[:, :, 1], EPS_LN, None, ALU.add).then_inc(s["rstd"], 1)
                b.wait_apart(g, passed_g, s["rstd"], 2, 1)
                g.tensor_tensor(rstd[:, :], rstd[:, :], half[:, 0:T], ALU.pow).then_inc(s["rstd"], 1)
                b.wait_apart(g, passed_g, s["rstd"], 2, 2)
                for t in range(T):
                    g.tensor_scalar(XN[:, t, :], X[b.slot][:, t, :], mv[:, t, 0:1], rstd[:, t:t + 1],
                                    ALU.subtract, ALU.mult).then_inc(s["xn"], 1)

            def rows(b):
                b.wait_apart(g, passed_g, s["parts"], 1, 1)
                b.wait_apart(g, passed_g, s["z"], ITEMS, -ITEMS)
                g.tensor_scalar(L[b.slot][:, :], parts[:, :], sel[:, 0:1], sel[:, 1:2], ALU.mult, ALU.add
                                ).then_inc(s["lr"], 1)
                for h in range(NH):
                    g.tensor_scalar(R[b.slot][:, h, :], parts[:, :], sel[:, 2 + 2 * h:3 + 2 * h],
                                    sel[:, 3 + 2 * h:4 + 2 * h], ALU.mult, ALU.add).then_inc(s["lr"], 1)

            def squares(b, q):
                b.wait_apart(g, passed_g, s["sq"], PAIRS, q + 1)
                b.wait_apart(g, passed_g, s["ss"], PAIRS - 1, q - 1)
                g.tensor_tensor(SS[:, :], SS[:, :], SQ[q % 2][:, :], ALU.add).then_inc(s["ss"], 1)

            def scale(b):
                b.wait_apart(g, passed_g, s["ssr"], 1, 1)
                g.tensor_tensor(rms[:, :], rms[:, :], half[:, 0:T], ALU.pow).then_inc(s["rms1"], 1)
                b.wait_apart(g, passed_g, s["rms1"], 1, 1)
                g.tensor_scalar(rms[:, :], rms[:, :], 0.5, None, ALU.mult).then_inc(s["rms"], 1)

            def finish(b):
                b.wait_apart(g, passed_g, s["xb"], 1, 1)
                b.wait_apart(g, passed_g, s["o"], 2, 2)
                g.tensor_tensor(OUT[:, :, :], OUT[:, :, :], RES[b.slot][:, :, :], ALU.add).then_inc(s["out"], 1)

            def residual(b):
                b.wait_apart(g, passed_g, s["out"], 1, -1)
                b.dma_wait(g, x_loaded)
                g.tensor_tensor(RES[b.slot][:, :, :], X[b.slot][:, :, :], blin[:, :].unsqueeze(1).to_broadcast([P, T, D]),
                                ALU.add).then_inc(s["xb"], 1)

            def pre(b):
                normalised(b)
                rows(b)
                normalised(b + 1)

            def body(b):
                some = b.reg is not None
                nxt, prev = some or b.off < nb - 1, some or b.off > 0
                nxt2 = some or b.off < nb - 2
                residual(b)
                if prev:
                    squares(b + -1, PAIRS - 1)
                if prev:
                    scale(b + -1)
                    finish(b + -1)
                if nxt:
                    rows(b + 1)
                if nxt2:
                    normalised(b + 2)
                squares(b, 1)
                squares(b, 2)

            def after(b):
                squares(b, PAIRS - 1)
                scale(b)
                finish(b)

            pipeline(g, nb, pre, body, after, 2, 2)


N_W = 12 + 3 * 2 * 3


def lstm_phase(nc, x_in, w, consts, x_out):
    B, NT, S, J, HB = 32, 512, 16, 4, 64
    CH = NT // S
    TILES = B * S // P
    BT = P // S
    GATES = (0, 1, 3, 2)
    with ExitStack() as ctx:
        m = Memory(nc, ctx, "lstm")
        ident = m.sb("ident", [P, P])
        rep = m.sb("rep", [P, P])
        rep_bf = m.sb("rep_bf", [P, P], BF16)
        ones_bf = m.sb("ones_bf", [P, B], BF16)
        half = m.sb("half", [P, 16])
        Wih = m.sb("Wih", [P, KC, J, 4 * HB])
        Whh = m.sb("Whh", [P, KC, J, 4 * HB])
        bias = m.sb("bias", [P, J * 4 * HB], BF16)
        wl = m.sb("wl", [P, KC, 2])
        bl = m.sb("bl", [B, 2])
        fw = m.sb("fw", [P, HB])
        bw = m.sb("bw", [P, HB])
        cinc = m.sb("cinc", [P, HB])
        cown = m.sb("cown", [P, HB])
        U = m.sb("U", [P, NT, HB])
        raw = m.sb("raw", [P, TILES, D])
        XN = m.sb("XN", [P, TILES, D])
        stats = m.sb("stats", [P, TILES, 6])
        mv = m.sb("mv", [P, TILES, 2])
        rstd = m.sb("rstd", [P, TILES])
        XT = [m.sb(f"XT{k}", [P, KC, B, S]) for k in range(2)]
        H = [m.sb(f"H{k}", [P, S, HB]) for k in range(2)]
        TC = [m.sb(f"TC{k}", [P, 5, HB]) for k in range(2)]
        AB = m.sb("AB", [P, 2, HB])
        tc = m.sb("tc", [P, HB])
        HT = [m.sb(f"HT{k}", [P, HB]) for k in range(2)]
        lg = m.sb("lg", [B, S, 2])
        gate = m.sb("gate", [P, S], BF16)
        gS = m.sb("gS", [P, S])
        own = m.sb("own", [P, S, HB])
        inc = m.sb("inc", [P, S + 1, HB])
        Gb = [m.ps(f"G{k}") for k in range(2)]
        XTb = [m.ps(f"XT{k}") for k in range(2)]
        LGb = [m.ps(f"LG{k}") for k in range(2)]
        REPb = m.ps("REP")
        names = ("w setup_v setup_pe wready zero raw_in st mv rstd xn xt_pe xt g tg ab c2 tc h ht lgp lg gate repp gs "
                 "own inc a u done tot bias1 bias2 fin outs").split()
        s = {n: m.sem(n) for n in names}
        resid = [m.sem(f"resid{k}") for k in range(2)]
        xv = x_in.rearrange("b (c t) d -> c b t d", t=S)
        passed_v, passed_g, passed_pe, passed_a = (m.sem(f"passed_{n}") for n in ("v", "g", "pe", "act"))
        ctx.push(m.clear)
        block = ctx.enter_context(nc.Block())

        def store(eng, c, blocks):
            eng.wait_ge(s["fin"], c.index() + 1)
            for j in blocks:
                eng.dma_start(x_out.rearrange("b (c t) d -> c b t d", t=S)[c.index()][:, :, HB * j:HB * (j + 1)],
                              U[32 * j:32 * (j + 1), bass.ds(c.index() * S, S), :]).then_inc(s["outs"], 16)

        flatU = U[:, :, :].rearrange("p t e -> p (t e)")
        nat_ih = flatU[:, 0:8 * D].rearrange("p (r k) -> p r k", k=D)
        nat_hh = flatU[:, 8 * D:16 * D].rearrange("p (r k) -> p r k", k=D)
        b1 = flatU[:, 16 * D:20 * D]
        b2 = flatU[:, 20 * D:24 * D]
        b3 = flatU[:, 24 * D:28 * D]
        b4 = flatU[:, 28 * D:30 * D].bitcast(BF16)

        @block.sync
        def _(sp):
            n = 0

            def put(dst, src, **kw):
                nonlocal n
                n += 1
                sp.dma_start(dst, src, **kw).then_inc(s["w"], 16)

            put(ident[:, :], consts["identity"])
            put(rep[:, :], consts["repeat"])
            put(nat_ih, w["W_ih"].rearrange("(r p) k -> p r k", p=P))
            for c in range(KC):
                for j in range(J):
                    k = HB * j + 32 * c
                    put(nat_hh[:, :, P * c + 32 * j:P * c + 32 * (j + 1)],
                        w["W_hh"].rearrange("(r p) k -> p r k", p=P)[:, :, k:k + 32])
            put(b1, w["b_ih"].rearrange("(o g) -> o g", o=1).to_broadcast([P, 4 * D]))
            put(b2, w["b_hh"].rearrange("(o g) -> o g", o=1).to_broadcast([P, 4 * D]))
            put(bl[:, :], w["b_lin"].rearrange("(o l) -> o l", o=1).to_broadcast([B, 2]))
            for c in range(KC):
                for l in range(2):
                    src = w["W_lin"][l, :].rearrange("(j c p o) -> c j p o", j=J, c=KC, o=1)[c]
                    for j in range(J):
                        sp.dma_start(wl[32 * j:32 * (j + 1), c, l:l + 1], src[j]).then_inc(s["zero"], 16)
            for j in range(J):
                put(fw[32 * j:32 * (j + 1), :], w["fw_att"][:, HB * j:HB * (j + 1)].to_broadcast([B, HB]))
                put(bw[32 * j:32 * (j + 1), :], w["bw_att"][:, HB * j:HB * (j + 1)].to_broadcast([B, HB]))
            assert n == N_PUT
            sp.wait_ge(s["setup_v"], 1)

            def load(c):
                c.wait(sp, s["xn"], TILES, 0)
                for k in range(TILES):
                    for b in range(BT):
                        sp.dma_start(raw[S * b:S * (b + 1), k, :], xv[c.index()][BT * k + b]
                                     ).then_inc(s["raw_in"], 16)

            def residual(c):
                c.wait(sp, s["done"], 1, -1)
                for j in range(J):
                    sp.dma_start(U[32 * j:32 * (j + 1), bass.ds(c.index() * S, S), :],
                                 xv[c.index()][:, :, HB * j:HB * (j + 1)]).then_inc(resid[c.slot], 16)

            def body(c):
                if c.reg is not None or c.off < CH - 1:
                    load(c + 1)
                residual(c)

            pipeline(sp, CH, load, body, lambda c: None, 2)

            with sp.Fori(0, CH) as i:
                store(sp, Batch(i, 0, 1), range(J // 2))
            sp.wait_ge(s["outs"], 16 * J * CH)

        @block.tensor
        def _(pe):
            pe.wait_ge(s["w"], 16 * N_PUT)
            n = 0
            for nat in (nat_ih, nat_hh):
                for c in range(KC):
                    for r0 in range(0, 8, 4):
                        pe.wait_ge(s["wready"], 4 * max(n - 1, 0))
                        for r in range(r0, r0 + 4):
                            ins = pe.transpose(XTb[n % 2][:, (r % 4) * P:(r % 4 + 1) * P],
                                               nat[:, r, c * P:(c + 1) * P], ident[:, :])
                        ins.then_inc(s["setup_pe"], 1)
                        n += 1
            pe.wait_ge(s["setup_v"], 1)
            pe.wait_ge(s["wready"], 4 * n)

            def turned(c):
                c.wait(pe, s["xn"], TILES, TILES)
                for kc in range(KC):
                    c.wait(pe, s["xt"], KC, kc - 1)
                    for k in range(TILES):
                        ins = pe.transpose(XTb[kc][:, k * P:(k + 1) * P], XN[:, k, kc * P:(kc + 1) * P], ident[:, :])
                    ins.then_inc(s["xt_pe"], 1)

            def inputs(c, t):
                if t == 0:
                    c.wait(pe, s["xt"], KC, KC)
                c.wait(pe, s["tg"], S, t - 1)
                bank = Gb[t % 2]
                for j in range(J):
                    pe.matmul(bank[32 * j:32 * (j + 1), 0:4 * HB], ones_bf[:, :], bias[:, 4 * HB * j:4 * HB * (j + 1)],
                              start=True, stop=False, skip_group_check=True)
                for kc in range(KC):
                    for j in range(J):
                        pe.matmul(bank[32 * j:32 * (j + 1), 0:4 * HB], XT[c.slot][:, kc, :, t], Wih[:, kc, j, :],
                                  start=False, stop=False, skip_group_check=True)

            def hidden(c, t):
                c.wait(pe, s["ht"], S, t + 1)
                for kc in range(KC):
                    for j in range(J):
                        ins = pe.matmul(Gb[t % 2][32 * j:32 * (j + 1), 0:4 * HB], HT[t % 2][:, 32 * kc:32 * (kc + 1)],
                                        Whh[:, kc, j, :], start=False, stop=(kc == KC - 1), skip_group_check=True)
                ins.then_inc(s["g"], 1)

            def logit(c, t, turned_h):
                for kc in range(KC):
                    ins = pe.matmul(LGb[c.slot][0:B, 2 * t:2 * t + 2], turned_h[:, 32 * kc:32 * (kc + 1)], wl[:, kc, :],
                                    start=(kc == 0), stop=(kc == KC - 1), skip_group_check=True)
                ins.then_inc(s["lgp"], 1)

            def repeat_gate(c):
                c.wait(pe, s["gate"], 1, 1)
                c.wait(pe, s["gs"], 1, 0)
                pe.matmul(REPb[:, 0:S], rep_bf[:, :], gate[:, :], start=True, stop=True).then_inc(s["repp"], 1)

            def before(c):
                turned(c)
                inputs(c, 0)

            def body(c):
                some = c.reg is not None
                nxt, prev = some or c.off < CH - 1, some or c.off > 0
                for t in range(S):
                    hidden(c, t)
                    if t < S - 1:
                        inputs(c, t + 1)
                    elif nxt:
                        inputs(c + 1, 0)
                    if t > 0:
                        logit(c, t - 1, HT[t % 2])
                    elif prev:
                        logit(c + -1, S - 1, HT[0])
                    if prev and t == 2:
                        repeat_gate(c + -1)
                    if nxt and t == 11:
                        turned(c + 1)

            def after(c):
                c.wait(pe, s["ht"], S, S + 1)
                logit(c, S - 1, HT[0])
                repeat_gate(c)

            pipeline(pe, CH, before, body, after, 2)

        @block.scalar
        def _(act):
            def evacuate(c, kc):
                c.wait(act, s["xt_pe"], KC, kc + 1)
                c.wait(act, s["g"], S, -S)
                act.activation(XT[c.slot][:, kc, :, :].rearrange("p b t -> p (b t)"), XTb[kc][:, :], ACT.Copy
                               ).then_inc(s["xt"], 1)

            def gates(c, t):
                c.wait(act, s["g"], S, t + 1)
                c.wait(act, s["h"], S, t - 1)
                act.activation(TC[t % 2][:, 0:4, :].rearrange("p g e -> p (g e)"), Gb[t % 2][:, 0:4 * HB], ACT.Tanh
                               ).then_inc(s["tg"], 1)

            def cell(c, t):
                c.wait(act, s["c2"], S, t + 1)
                act.activation(tc[:, :], TC[(t + 1) % 2][:, 4, :], ACT.Tanh, scale=0.5).then_inc(s["tc"], 1)

            def before(c):
                act.wait_ge(s["wready"], 32)
                evacuate(c, 0)
                evacuate(c, 1)

            def body(c):
                nxt = c.reg is not None or c.off < CH - 1
                for t in range(S):
                    gates(c, t)
                    cell(c, t)
                    if nxt and t in (12, 13):
                        evacuate(c + 1, t - 12)

            pipeline(act, CH, before, body, lambda c: None, 2)
            with act.Fori(0, CH) as i:
                store(act, Batch(i, 0, 1), range(J // 2, J))

        @block.vector
        def _(v):
            v.memset(ones_bf[:, :], 1.0)
            v.memset(half[:, :], -0.5)
            v.memset(bias[:, :], 0.0)
            v.memset(gate[:, :], 0.0)
            v.memset(TC[0][:, 4, :], 0.0)
            v.memset(inc[:, S, :], 0.0).then_inc(s["tot"], 1)
            n = 0
            for which in range(2):
                W = (Wih, Whh)[which]
                for c in range(KC):
                    for r0 in range(0, 8, 4):
                        v.wait_ge(s["setup_pe"], n + 1)
                        for r in range(r0, r0 + 4):
                            g = GATES[r // 2]
                            scale = (1.0 if g == 3 else 0.5) * (0.5 if which else 1.0)
                            v.tensor_scalar(W[:, c, 2 * (r % 2):2 * (r % 2) + 2, g * HB:(g + 1) * HB],
                                            XTb[n % 2][:, (r % 4) * P:(r % 4 + 1) * P].rearrange("p (j e) -> p j e", j=2),
                                            scale, None, ALU.mult).then_inc(s["wready"], 1)
                        n += 1
            v.wait_ge(s["w"], 16 * N_PUT)
            v.tensor_copy(rep_bf[:, :], rep[:, :])
            v.tensor_tensor(b3, b1, b2, ALU.add).then_inc(s["bias1"], 1)
            v.wait_ge(s["bias1"], 1)
            for r in range(4):
                g = GATES[r]
                v.tensor_scalar(b1.rearrange("p (j g e) -> p j g e", j=J, g=4)[:, :, g],
                                b3[:, r * D:(r + 1) * D].rearrange("p (j e) -> p j e", j=J),
                                1.0 if g == 3 else 0.5, None, ALU.mult).then_inc(s["bias1"], 1)
            v.wait_ge(s["bias1"], 5)
            for k, q in enumerate((0, 64, 96)):
                v.tensor_copy(b4, b1).then_inc(s["bias2"], 1)
                v.wait_ge(s["bias2"], 3 * k + 1)
                v.tensor_copy(bias[q:q + 1, :], b4[q:q + 1, :]).then_inc(s["bias2"], 1)
                v.tensor_tensor(b1, b1, b4, ALU.subtract).then_inc(s["bias2"], 1)
                v.wait_ge(s["bias2"], 3 * k + 3)
            v.tensor_tensor(cinc[:, :], fw[:, :], bw[:, :], ALU.subtract).then_inc(s["bias1"], 1)
            v.tensor_scalar(cown[:, :], fw[:, :], -0.5, None, ALU.mult)
            v.tensor_scalar(bw[:, :], bw[:, :], 0.5, None, ALU.mult)
            v.wait_ge(s["zero"], 16 * 2 * KC * J)
            v.tensor_scalar(wl[:, :, :], wl[:, :, :], 0.5, None, ALU.mult)
            v.wait_ge(s["bias1"], 6)
            v.tensor_scalar(cinc[:, :], cinc[:, :], 0.5, None, ALU.mult).then_inc(s["setup_v"], 1)
            v.memset(HT[0][:, :], 0.0).then_inc(s["ht"], 1)
            v.wait_ge(s["tot"], 1)

            def norm(c, k):
                if k == 0:
                    c.wait(v, s["raw_in"], 16 * P // S * TILES, 16 * P // S * TILES)
                    c.wait(v, s["xn"], TILES, 0)
                if k < TILES:
                    v.bn_stats(stats[:, k, :], raw[:, k, :]).then_inc(s["st"], 1)
                else:
                    c.wait_apart(v, passed_v, s["st"], TILES, TILES)
                    for i in range(TILES):
                        ins = v.bn_aggr(mv[:, i, :], stats[:, i, :])
                    ins.then_inc(s["mv"], 1)

            def step(c, t):
                c.wait(v, s["tg"], S, t + 1)
                c.wait(v, s["c2"], S, t)
                v.scalar_tensor_tensor(out=AB[:, :, :], in0=TC[t % 2][:, 0:2, :], scalar=1.0, in1=TC[t % 2][:, 3:5, :],
                                       op0=ALU.add, op1=ALU.mult).then_inc(s["ab"], 1)
                c.wait(v, s["ab"], S, t + 1)
                v.scalar_tensor_tensor(out=TC[(t + 1) % 2][:, 4, :], in0=AB[:, 1, :], scalar=0.5, in1=AB[:, 0, :],
                                       op0=ALU.mult, op1=ALU.add).then_inc(s["c2"], 1)
                if t == 0:
                    c.wait(v, s["done"], 1, -1)
                c.wait(v, s["tc"], S, t + 1)
                v.scalar_tensor_tensor(out=H[c.slot][:, t, :], in0=TC[t % 2][:, 2, :], scalar=1.0, in1=tc[:, :],
                                       op0=ALU.add, op1=ALU.mult).then_inc(s["h"], 1)
                c.wait(v, s["h"], S, t + 1)
                c.wait(v, s["lgp"], S, t - 1)
                v.transpose(HT[(t + 1) % 2][:, :], H[c.slot][:, t, :]).then_inc(s["ht"], 1)

            def choose(c):
                c.wait(v, s["lgp"], S, S)
                v.tensor_tensor(lg[:, :, :], LGb[c.slot][0:B, 0:2 * S].rearrange("b (t l) -> b t l", l=2),
                                bl[:, :].unsqueeze(1).to_broadcast([B, S, 2]), ALU.add).then_inc(s["lg"], 1)
                c.wait(v, s["lg"], 1, 1)
                c.wait(v, s["repp"], 1, 0)
                v.tensor_tensor(gate[0:B, :], lg[:, :, 1], lg[:, :, 0], ALU.is_gt).then_inc(s["gate"], 1)

            def gate_out(c):
                c.wait(v, s["repp"], 1, 1)
                c.wait(v, s["own"], 1, 0)
                v.tensor_copy(gS[:, :], REPb[:, 0:S]).then_inc(s["gs"], 1)

            def before(c):
                for k in range(TILES + 1):
                    norm(c, k)

            def body(c):
                some = c.reg is not None
                nxt, prev = some or c.off < CH - 1, some or c.off > 0
                for t in range(S):
                    step(c, t)
                    if prev and t == 1:
                        choose(c + -1)
                    if prev and t == 2:
                        gate_out(c + -1)
                    if nxt and 3 <= t < 3 + TILES + 1:
                        norm(c + 1, t - 3)

            def after(c):
                choose(c)
                gate_out(c)

            pipeline(v, CH, before, body, after, 2)
            v.wait_ge(s["done"], CH)
            v.wait_ge(s["tot"], 2)
            with v.Fori(0, CH) as i:
                Uc = U[:, bass.ds(i * S, S), :]
                v.tensor_tensor(Uc, Uc, bw[:, :].unsqueeze(1).to_broadcast([P, S, HB]), ALU.add).then_inc(s["fin"], 1)

        @block.gpsimd
        def _(g):
            g.wait_ge(s["setup_v"], 1)

            def normalised(c):
                c.wait_apart(g, passed_g, s["mv"], 1, 1)
                c.wait_apart(g, passed_g, s["xt_pe"], KC, 0)
                g.tensor_scalar(rstd[:, :], mv[:, :, 1], EPS_LN, None, ALU.add).then_inc(s["rstd"], 1)
                c.wait_apart(g, passed_g, s["rstd"], 2, 1)
                g.tensor_tensor(rstd[:, :], rstd[:, :], half[:, 0:TILES], ALU.pow).then_inc(s["rstd"], 1)
                c.wait_apart(g, passed_g, s["rstd"], 2, 2)
                for k in range(TILES):
                    g.tensor_scalar(XN[:, k, :], raw[:, k, :], mv[:, k, 0:1], rstd[:, k:k + 1],
                                    ALU.subtract, ALU.mult).then_inc(s["xn"], 1)

            def sums(c):
                c.wait_apart(g, passed_g, s["gs"], 1, 1)
                Hc = H[c.slot][:, :, :]
                g.tensor_tensor(own[:, :, :], Hc, bcast(gS[:, :], HB), ALU.mult).then_inc(s["own"], 1)
                g.tensor_copy(inc[:, 0, :], inc[:, S, :]).then_inc(s["inc"], 1)
                c.wait_apart(g, passed_g, s["own"], 1, 1)
                for t in range(S):
                    c.wait_apart(g, passed_g, s["inc"], S + 1, t + 1)
                    g.tensor_tensor(inc[:, t + 1, :], inc[:, t, :], own[:, t, :], ALU.add).then_inc(s["inc"], 1)
                c.wait_apart(g, passed_g, s["inc"], S + 1, S + 1)
                g.tensor_tensor(own[:, :, :], own[:, :, :], cown[:, :].unsqueeze(1).to_broadcast([P, S, HB]),
                                ALU.mult).then_inc(s["a"], 1)
                c.dma_wait4(g, resid)
                Uc = U[:, bass.ds(c.index() * S, S), :]
                g.tensor_tensor(Uc, Uc, Hc, ALU.add).then_inc(s["u"], 1)
                c.wait_apart(g, passed_g, s["u"], 3, 1)
                c.wait_apart(g, passed_g, s["a"], 2, 1)
                g.tensor_tensor(Uc, Uc, own[:, :, :], ALU.add).then_inc(s["u"], 1)
                c.wait_apart(g, passed_g, s["u"], 3, 2)
                g.tensor_tensor(own[:, :, :], inc[:, 1:, :], cinc[:, :].unsqueeze(1).to_broadcast([P, S, HB]),
                                ALU.mult).then_inc(s["a"], 1)
                c.wait_apart(g, passed_g, s["a"], 2, 2)
                g.tensor_tensor(Uc, Uc, own[:, :, :], ALU.add).then_inc(s["u"], 1)
                c.wait_apart(g, passed_g, s["u"], 3, 3)
                g.nop().then_inc(s["done"], 1)

            def body(c):
                some = c.reg is not None
                if some or c.off > 0:
                    sums(c + -1)
                if some or c.off < CH - 1:
                    normalised(c + 1)

            def after(c):
                sums(c)
                g.tensor_tensor(bw[:, :], bw[:, :], inc[:, S, :], ALU.mult).then_inc(s["tot"], 1)

            pipeline(g, CH, normalised, body, after, 2)


N_PUT = 6 + 2 * 4 + 2 * 4


GNN0 = {"W": "L0_gnn_W", "a_src": "L0_gnn_a_src", "a_dst": "L0_gnn_a_dst", "bias": "L0_gnn_bias",
        "gamma": "L0_gnn_ln_gamma", "beta": "L0_gnn_ln_beta"}
SSM = {n: f"L0_ffn_{n}" for n in "W_in conv_w conv_b dt_bias A_log D norm_w W_out W_lin b_lin".split()}
GNN1 = {"W": "L1_gnn_W", "a": "L1_gnn_a"}
LSTM = {n: f"L1_ffn_{n}" for n in "W_ih W_hh b_ih b_hh W_lin b_lin fw_att bw_att".split()}


def build(nc, a, consts, out):
    nb = a["x"].shape[0]
    x1, x2, x3 = (nc.dram_tensor(f"x{k}", list(a["x"].shape), F32).ap() for k in (1, 2, 3))
    pick = lambda names: {n: a[full] for n, full in names.items()}
    with ExitStack() as ctx:
        m = Memory(nc, ctx, "kept")
        kept = {"odd": m.sb("odd", [P, nb]), "WG": m.sb("WG", [P, KC, 40])}
        attention_phase(nc, 0, nb, a["x"], a["adj"], pick(GNN0), consts, x1, kept)
        typed_attention_phase(nc, nb, a["x"], a["adj"], pick(GNN0), consts, kept, x1)
    state_space_phase(nc, nb, x1, pick(SSM), consts, x2)
    attention_phase(nc, 1, nb, x2, a["adj"], pick(GNN1), consts, x3)
    lstm_phase(nc, x3, pick(LSTM), consts, out)


def kernel(**inputs):
    import concourse.bacc as bacc
    from concourse.bass_utils import run_bass_kernel_spmd

    nc = bacc.Bacc("TRN2", target_bir_lowering=False, num_devices=1)
    arrays, aps = {}, {}
    for name, value in {**inputs, **constants()}.items():
        value = np.ascontiguousarray(value)
        arrays[f"in_{name}"] = value
        aps[name] = nc.dram_tensor(f"in_{name}", value.shape, mybir.dt.from_np(value.dtype), kind="ExternalInput").ap()
    out = nc.dram_tensor("out", inputs["x"].shape, F32, kind="ExternalOutput").ap()
    build(nc, aps, aps, out)
    result = run_bass_kernel_spmd(nc, [arrays], core_ids=[0])
    return result.results[0]["out"]
```
